# Optimizing a Trainium2 kernel written in Bass

```python
import numpy as np
import jax
import jax.numpy as jnp

def _softmax(x, axis=-1):
    return jax.nn.softmax(x, axis=axis)

def _gelu(x):
    return jax.nn.gelu(x, approximate=True)

def _silu(x):
    return jax.nn.silu(x)

def _sigmoid(x):
    return jax.nn.sigmoid(x)

def _layernorm(x, axis=-1, eps=1e-05):
    m = jnp.mean(x, axis=axis, keepdims=True)
    v = jnp.var(x, axis=axis, keepdims=True)
    return (x - m) / jnp.sqrt(v + eps)

def _scatter_add(tgt, idx, src, axis=0):
    return tgt.at[idx].add(src)

def _segment_sum(src, seg, n):
    return jax.ops.segment_sum(src, seg, n)
kernel_name = 'mk_conv_attn_hybrid_d2_conv_nhwc768_r4_b21587'

def setup_inputs(seed: int=0):
    np.random.seed(seed)
    _w = jnp.asarray

    def _rec_inputs():
        import jax
        import jax.numpy as jnp
        _gk = jax.random.key(seed)
        x = -4.65e-05 + 0.9999 * jax.random.normal(jax.random.fold_in(_gk, 1), (16, 16, 16, 192), jnp.float32)
        return x
    x = _rec_inputs()

    def _L0_conv_setup():
        import jax, jax.numpy as jnp
        import numpy as np
        RATE = 0.25

        def _low_mask(w, h):
            line = int((w * h * RATE) ** 0.5 // 2)
            m = np.zeros((w, h), dtype=np.float32)
            m[w // 2 - line:w // 2 + line, h // 2 - line:h // 2 + line] = 1.0
            return jnp.asarray(m)

        def fft_low(x):
            xb = jnp.transpose(x, (0, 3, 2, 1))
            w, h = (xb.shape[-2], xb.shape[-1])
            mask = _low_mask(w, h)
            fft = jnp.fft.fftshift(jnp.fft.fft2(xb, norm='forward'), axes=(-2, -1))
            fft = fft * mask
            inv = jnp.fft.ifft2(jnp.fft.ifftshift(fft, axes=(-2, -1)), norm='forward').real
            inv = jnp.abs(inv)
            return jnp.transpose(inv, (0, 3, 2, 1))
        key = jax.random.key(seed)
        k_x, k_w1, k_b1, k_w2, k_b2 = jax.random.split(key, 5)
        B, H, W, C = (16, 16, 16, 192)
        Dh = int(C * 0.25)
        s1 = 1.0 / np.sqrt(C)
        s2 = 1.0 / np.sqrt(Dh)
        return {'x': jax.random.normal(k_x, (B, H, W, C), dtype=jnp.float32), 'W1': jax.random.uniform(k_w1, (Dh, C), jnp.float32, -s1, s1), 'b1': jax.random.uniform(k_b1, (Dh,), jnp.float32, -s1, s1), 'W2': jax.random.uniform(k_w2, (C, Dh), jnp.float32, -s2, s2), 'b2': jax.random.uniform(k_b2, (C,), jnp.float32, -s2, s2)}
    _L0_conv_all = _L0_conv_setup()
    _L0_conv_in = {k: v for k, v in _L0_conv_all.items() if k in ('W1', 'b1', 'W2', 'b2')}
    del _L0_conv_all

    def _L1_attn_setup():
        import jax, jax.numpy as jnp
        import numpy as np
        B, S, H_DIM = (8, 2048, 192)
        N_HEADS = 12
        HEAD_DIM = H_DIM // N_HEADS

        def rotate_half(x):
            x1, x2 = jnp.split(x, 2, axis=-1)
            return jnp.concatenate((-x2, x1), axis=-1)

        def rotary_emb(seq_len, dim, dtype):
            inv_freq = 1.0 / 10000.0 ** (jnp.arange(0, dim, 2, dtype=jnp.float32) / dim)
            seq = jnp.arange(seq_len, dtype=jnp.float32)
            freqs = jnp.einsum('i,j->ij', seq, inv_freq)
            emb = jnp.concatenate((freqs, freqs), axis=-1)
            return emb[None, :, None, :].astype(dtype)
        key = jax.random.key(seed)
        ks = jax.random.split(key, 7)
        sq = 1.0 / np.sqrt(H_DIM)
        return {'x': jax.random.normal(ks[0], (B, S, H_DIM), dtype=jnp.float32), 'Wq': jax.random.normal(ks[1], (H_DIM, H_DIM), dtype=jnp.float32) * sq, 'bq': jax.random.normal(ks[2], (H_DIM,), dtype=jnp.float32) * 0.02, 'Wk': jax.random.normal(ks[3], (H_DIM, HEAD_DIM), dtype=jnp.float32) * sq, 'bk': jax.random.normal(ks[4], (HEAD_DIM,), dtype=jnp.float32) * 0.02, 'Wv': jax.random.normal(ks[5], (H_DIM, HEAD_DIM), dtype=jnp.float32) * sq, 'bv': jax.random.normal(ks[6], (HEAD_DIM,), dtype=jnp.float32) * 0.02}
    _L1_attn_all = _L1_attn_setup()
    _L1_attn_in = {k: v for k, v in _L1_attn_all.items() if k in ('Wq', 'bq', 'Wk', 'bk', 'Wv', 'bv')}
    del _L1_attn_all

    def _L1_ffn_setup():
        import jax, jax.numpy as jnp
        import numpy as np
        K = 2
        key = jax.random.key(seed)
        ks = jax.random.split(key, 5)
        B, T, D, E, H = (2, 512, 192, 8, 384)
        x = jax.random.normal(ks[0], (B, T, D), dtype=jnp.float32)
        gate_w = jax.random.normal(ks[1], (E, D), dtype=jnp.float32) * (1.0 / np.sqrt(D))
        gate_bank = jax.random.normal(ks[2], (E, D, H), dtype=jnp.float32) * (1.0 / np.sqrt(D))
        up_bank = jax.random.normal(ks[3], (E, D, H), dtype=jnp.float32) * (1.0 / np.sqrt(D))
        down_bank = jax.random.normal(ks[4], (E, H, D), dtype=jnp.float32) * (1.0 / np.sqrt(H))
        return {'x': x, 'gate_w': gate_w, 'gate_bank': gate_bank, 'up_bank': up_bank, 'down_bank': down_bank}
    _L1_ffn_all = _L1_ffn_setup()
    _L1_ffn_in = {k: v for k, v in _L1_ffn_all.items() if k in ('gate_w', 'gate_bank', 'up_bank', 'down_bank')}
    del _L1_ffn_all
    return {'x': x, 'L0_conv_W1': _L0_conv_in['W1'], 'L0_conv_b1': _L0_conv_in['b1'], 'L0_conv_W2': _L0_conv_in['W2'], 'L0_conv_b2': _L0_conv_in['b2'], 'L1_attn_Wq': _L1_attn_in['Wq'], 'L1_attn_bq': _L1_attn_in['bq'], 'L1_attn_Wk': _L1_attn_in['Wk'], 'L1_attn_bk': _L1_attn_in['bk'], 'L1_attn_Wv': _L1_attn_in['Wv'], 'L1_attn_bv': _L1_attn_in['bv'], 'L1_ffn_gate_w': _L1_ffn_in['gate_w'], 'L1_ffn_gate_bank': _L1_ffn_in['gate_bank'], 'L1_ffn_up_bank': _L1_ffn_in['up_bank'], 'L1_ffn_down_bank': _L1_ffn_in['down_bank']}

def reference(x, L0_conv_W1, L0_conv_b1, L0_conv_W2, L0_conv_b2, L1_attn_Wq, L1_attn_bq, L1_attn_Wk, L1_attn_bk, L1_attn_Wv, L1_attn_bv, L1_ffn_gate_w, L1_ffn_gate_bank, L1_ffn_up_bank, L1_ffn_down_bank):
    import jax
    import jax.numpy as jnp

    def _L0_conv_ref(x, W1, b1, W2, b2):
        import jax, jax.numpy as jnp
        import numpy as np
        RATE = 0.25

        def _low_mask(w, h):
            line = int((w * h * RATE) ** 0.5 // 2)
            m = np.zeros((w, h), dtype=np.float32)
            m[w // 2 - line:w // 2 + line, h // 2 - line:h // 2 + line] = 1.0
            return jnp.asarray(m)

        def fft_low(x):
            xb = jnp.transpose(x, (0, 3, 2, 1))
            w, h = (xb.shape[-2], xb.shape[-1])
            mask = _low_mask(w, h)
            fft = jnp.fft.fftshift(jnp.fft.fft2(xb, norm='forward'), axes=(-2, -1))
            fft = fft * mask
            inv = jnp.fft.ifft2(jnp.fft.ifftshift(fft, axes=(-2, -1)), norm='forward').real
            inv = jnp.abs(inv)
            return jnp.transpose(inv, (0, 3, 2, 1))
        xs = jnp.einsum('bhwc,dc->bhwd', x, W1) + b1
        xs = jax.nn.gelu(xs, approximate=False)
        xs = fft_low(xs)
        xs = jnp.einsum('bhwd,cd->bhwc', xs, W2) + b2
        return x + xs

    def _L1_attn_ref(x, Wq, bq, Wk, bk, Wv, bv):
        import jax, jax.numpy as jnp
        import numpy as np
        B, S, H_DIM = (8, 2048, 192)
        N_HEADS = 12
        HEAD_DIM = H_DIM // N_HEADS

        def rotate_half(x):
            x1, x2 = jnp.split(x, 2, axis=-1)
            return jnp.concatenate((-x2, x1), axis=-1)

        def rotary_emb(seq_len, dim, dtype):
            inv_freq = 1.0 / 10000.0 ** (jnp.arange(0, dim, 2, dtype=jnp.float32) / dim)
            seq = jnp.arange(seq_len, dtype=jnp.float32)
            freqs = jnp.einsum('i,j->ij', seq, inv_freq)
            emb = jnp.concatenate((freqs, freqs), axis=-1)
            return emb[None, :, None, :].astype(dtype)
        b, s, _ = x.shape
        q = (x @ Wq + bq).reshape(b, s, N_HEADS, HEAD_DIM)
        k = (x @ Wk + bk).reshape(b, s, 1, HEAD_DIM)
        v = (x @ Wv + bv).reshape(b, s, 1, HEAD_DIM)
        k = jnp.broadcast_to(k, (b, s, N_HEADS, HEAD_DIM))
        v = jnp.broadcast_to(v, (b, s, N_HEADS, HEAD_DIM))
        pos = rotary_emb(s, HEAD_DIM, x.dtype)
        cos, sin = (jnp.cos(pos), jnp.sin(pos))
        q = q * cos + rotate_half(q) * sin
        k = k * cos + rotate_half(k) * sin
        scale = HEAD_DIM ** (-0.5)
        attn = jnp.einsum('bsid,bsjd->bsij', q, k) * scale
        attn = jax.nn.softmax(attn, axis=-1)
        out = jnp.einsum('bsij,bsjd->bsid', attn, v)
        return out.reshape(b, s, N_HEADS * HEAD_DIM)

    def _L1_ffn_ref(x, gate_w, gate_bank, up_bank, down_bank):
        import jax, jax.numpy as jnp
        import numpy as np
        K = 2
        logits = jnp.einsum('btd,ed->bte', x, gate_w)
        probs = jax.nn.softmax(logits, axis=-1)
        selected_probs, selected_idx = jax.lax.top_k(probs, K)
        selected_probs = selected_probs / (jnp.sum(selected_probs, axis=-1, keepdims=True) + 1e-08)
        a = jnp.einsum('btd,edh->bteh', x, gate_bank)
        u = jnp.einsum('btd,edh->bteh', x, up_bank)
        h = jax.nn.silu(a) * u
        y_all = jnp.einsum('bteh,ehd->bted', h, down_bank)
        y_sel = jnp.take_along_axis(y_all, selected_idx[..., None], axis=2)
        y = jnp.sum(y_sel * selected_probs[..., None], axis=2)
        return y

    def _gn(v, G=32, eps=1e-05):
        B_, H_, W_, C_ = v.shape
        g = v.reshape(B_, H_, W_, G, C_ // G)
        m = jnp.mean(g, axis=(1, 2, 4), keepdims=True)
        s = jnp.var(g, axis=(1, 2, 4), keepdims=True)
        return ((g - m) / jnp.sqrt(s + eps)).reshape(v.shape)

    def _ln_c(v, eps=1e-06):
        m = jnp.mean(v, axis=-1, keepdims=True)
        s = jnp.var(v, axis=-1, keepdims=True)
        return (v - m) / jnp.sqrt(s + eps)

    def _ln_t(v, eps=1e-05):
        m = jnp.mean(v, axis=-1, keepdims=True)
        s = jnp.var(v, axis=-1, keepdims=True)
        return (v - m) / jnp.sqrt(s + eps)

    def _to_tokens(v):
        B_, H_, W_, C_ = v.shape
        return v.reshape(B_, H_ * W_, C_)

    def _from_tokens(t, like):
        return t.reshape(like.shape)
    x = _L0_conv_ref(x, L0_conv_W1, L0_conv_b1, L0_conv_W2, L0_conv_b2)
    t = _to_tokens(x)
    t = t + _L1_attn_ref(_ln_t(t), L1_attn_Wq, L1_attn_bq, L1_attn_Wk, L1_attn_bk, L1_attn_Wv, L1_attn_bv)
    t = t + _L1_ffn_ref(_ln_t(t), L1_ffn_gate_w, L1_ffn_gate_bank, L1_ffn_up_bank, L1_ffn_down_bank)
    x = _from_tokens(t, x)
    return x

_drawn_inputs = setup_inputs


def setup_inputs(seed=0):
    import zlib

    import numpy as np

    out = dict(_drawn_inputs(seed))
    spreads = {}
    factors = {}
    for name, (base, spread) in spreads.items():
        noise = np.random.default_rng([zlib.crc32(name.encode()), seed]).standard_normal(out[name].shape)
        drawn = base * np.exp(spread * noise) if base else spread * noise
        out[name] = jnp.asarray(drawn.astype(out[name].dtype))
    for name, factor in factors.items():
        out[name] = (out[name] * factor).astype(out[name].dtype)
    return out
```

```python
from contextlib import ExitStack

import concourse.bass as bass
from concourse import mybir

F32 = mybir.dt.float32
F32R = mybir.dt.float32r
I32 = mybir.dt.int32
U32 = mybir.dt.uint32
ALU = mybir.AluOpType
ACT = mybir.ActivationFunctionType
AX = mybir.AxisListType

P = 128
IMAGES, SIDE, C = 16, 16, 192
SEQ = SIDE * SIDE
TOKENS = IMAGES * SEQ
DH = 48
DP = 64
CB = C - P
HEADS, HD = 12, 16
QW = C + 3 * HD
KC, VC = C, C + 2 * HD
EXPERTS, HID = 8, 384
TILES = TOKENS // P
QT = 4
QUADS = TILES // QT
RING = 2
SLOTS = 32
MAPW = EXPERTS * SLOTS
YR = 3
XR = 6
TILES_MAX = -(-(2 * TOKENS // P + EXPERTS - 1) // XR) * XR
GC = C + CB
ROW = GC + 8
EPS = 1e-5
SCALE = HD ** -0.5


def quad(i, s):
    return RING * i + s


def made(n):
    return n + 1 + RING


def freed(n):
    return n + 1


def bcast(ap, axis, n):
    v = ap.unsqueeze(axis)
    shape = list(v.shape)
    shape[axis] = n
    return v.broadcast_to(shape)


def program(nc, x, xT, w1, w2, lowpass, wqkv, cos, sin, gate, wgu, down, tri, ident, iotas, ytab, out):
    chosen_rows = nc.dram_tensor("chosen_rows", [2 * TOKENS + (EXPERTS + 2) * P, C], F32)
    rows = nc.dram_tensor("rows", [TOKENS + P, ROW], F32)
    x_tiles = x.rearrange("(t p) c -> p t c", p=P)
    row_tiles = rows[0:TOKENS, :].rearrange("(t p) c -> p t c", p=P)

    with ExitStack() as whole:
        def keep(name, shape, dt=F32):
            return whole.enter_context(nc.sbuf_tensor(name, shape, dt))

        wa_hi = keep("wa_hi", [P, EXPERTS, 2 * HID], F32R)
        wa_lo = keep("wa_lo", [P, EXPERTS, 2 * HID], F32R)
        wb_hi = keep("wb_hi", [P, EXPERTS, 2 * HID], F32R)
        wb_lo = keep("wb_lo", [CB, EXPERTS, 2 * HID], F32R)
        wd_hi = keep("wd_hi", [P, EXPERTS, 3 * C], F32R)
        wd_lo = keep("wd_lo", [P, EXPERTS, 3 * C], F32R)
        eye = keep("eye", [P, P])
        idx_map = keep("idx_map", [P, MAPW + 2, 2], I32)
        tile_col = keep("tile_col", [P, TILES_MAX], I32)
        tile_exp = keep("tile_exp", [P, TILES_MAX], I32)

        xs = keep("xs", [P, TILES, C])
        mean, rstd = keep("mean", [P, TILES]), keep("rstd", [P, TILES])

        conv_phase(nc, xs, mean, rstd, x_tiles, xT, w1, w2, lowpass, wgu, wa_hi, wa_lo, ytab, eye, ident)
        attention_phase(nc, xs, mean, rstd, eye, wqkv, cos, sin, rows, wgu, wb_hi, wb_lo)
        routing_phase(nc, xs, mean, rstd, eye, gate, tri, iotas, row_tiles, down, wd_hi, wd_lo,
                      idx_map, tile_col, tile_exp)
        expert_phase(nc, xs, eye, rows, chosen_rows, out, wa_hi, wa_lo, wb_hi, wb_lo, wd_hi, wd_lo, idx_map, tile_col, tile_exp)


class Scope:

    def __init__(self, nc, stack, phase):
        self.nc, self.stack, self.phase = nc, stack, phase

    def sb(self, name, shape, dt=F32):
        return self.stack.enter_context(self.nc.sbuf_tensor(f"{self.phase}_{name}", shape, dt))

    def ps(self, name, shape):
        return self.stack.enter_context(self.nc.psum_tensor(f"{self.phase}_{name}", shape, F32))

    def sem(self, name):
        return self.stack.enter_context(self.nc.semaphore(f"{self.phase}_{name}"))


def conv_phase(nc, xs, mean, rstd, x_tiles, xT, w1, w2, lowpass, wgu, wa_hi, wa_lo, ytab, eye, ident):
    with ExitStack() as stack:
        a = Scope(nc, stack, "conv")
        w1a, w1b = a.sb("w1a", [P, DH]), a.sb("w1b", [CB + 1, DH])
        w2s = a.sb("w2s", [P, C])
        lp = a.sb("lp", [P, 2, SEQ])
        y_bias = a.sb("y_bias", [P, 1])
        xta, xtb = a.sb("xta", [P, RING, QT * P]), a.sb("xtb", [CB + 1, RING, QT * P])
        g = a.sb("g", [P, RING, 2, 2, DP])
        yt = a.sb("yt", [P, RING, SEQ])
        stage = a.sb("stage", [P, RING, 2 * HID])
        stats, mv = a.sb("stats", [P, RING, QT, 6]), a.sb("mv", [P, RING, QT, 2])
        vtmp, half = a.sb("vtmp", [P, RING, QT]), a.sb("half", [P, 1])
        ps_w1, ps_f = a.ps("ps_w1", [P, RING, 512]), a.ps("ps_f", [P, RING, 512])
        ps_c = a.ps("ps_c", [P, RING, 2, 512])

        consts_in = a.sem("consts_in")
        xt_in = [a.sem(f"xt_in{s}") for s in range(RING)]
        x_in = [a.sem(f"x_in{s}") for s in range(4)]
        stage_in = [a.sem(f"stage_in{s}") for s in range(RING)]
        filled = a.sem("filled")
        bias_row = a.sem("bias_row")
        w1_done, fft_done, w2_done = a.sem("w1_done"), a.sem("fft_done"), a.sem("w2_done")
        gelu_done, abs_done, hi_done = a.sem("gelu_done"), a.sem("abs_done"), a.sem("hi_done")
        added, stats_done, mv_done = a.sem("added"), a.sem("stats_done"), a.sem("mv_done")
        lo_done, eps_done, pow_done = a.sem("lo_done"), a.sem("eps_done"), a.sem("pow_done")
        mean_done = a.sem("mean_done")
        pool_turn, dve_turn = a.sem("pool_turn"), a.sem("dve_turn")

        with nc.Block() as block:
            @block.sync
            def _(sp):
                sp.dma_start(w1a[:], w1[0:P, :]).then_inc(consts_in, 16)
                sp.dma_start(w1b[:], w1[P:C + 1, :]).then_inc(consts_in, 16)

                def load(i, s):
                    q = quad(i, s)
                    sp.wait_ge(w1_done, freed(q))
                    sp.dma_start(xta[:, s, :], xT[0:P, bass.ts(q, QT * P)]).then_inc(xt_in[s], 16)
                    sp.dma_start(xtb[0:CB, s, :], xT[P:C, bass.ts(q, QT * P)]).then_inc(xt_in[s], 16)

                def load_weights(i, s):
                    q = quad(i, s)
                    sp.wait_ge(lo_done, freed(q))
                    sp.dma_start(stage[:, s], wgu[0:P, q, :]).then_inc(stage_in[s], 16)

                load(0, 0)
                sp.dma_start(lp[:], lowpass.rearrange("(h p) s -> p h s", p=P)).then_inc(consts_in, 16)
                sp.dma_start(w2s[0:DH + 1, :], w2).then_inc(consts_in, 16)
                sp.dma_start(w2s[DP:DP + DH + 1, :], w2).then_inc(consts_in, 16)
                sp.dma_start(y_bias[:], ytab).then_inc(consts_in, 16)
                sp.dma_start(eye[:], ident).then_inc(consts_in, 16)
                load(0, 1)
                for k, x_part in enumerate(x_in):
                    part = slice(k * TILES // 4, (k + 1) * TILES // 4)
                    sp.dma_start(xs[:, part, :], x_tiles[:, part, :]).then_inc(x_part, 16)
                load_weights(0, 0)
                load_weights(0, 1)
                with sp.Fori(1, QUADS // RING) as i:
                    for s in range(RING):
                        load(i, s)
                        load_weights(i, s)

            @block.tensor
            def _(pe):
                pe.sem_inc(w1_done, RING)
                pe.sem_inc(fft_done, RING)
                pe.sem_inc(w2_done, RING)
                pe.wait_ge(consts_in, 7 * 16)
                pe.wait_ge(filled, 2)
                pe.wait_ge(bias_row, 1)

                def in_product(i, s):
                    q = quad(i, s)
                    pe.wait_ge(xt_in[s], 32 * i + 32)
                    pe.wait_ge(gelu_done, freed(q))
                    for t in range(QT):
                        at = ps_w1[:, s, t * DH:(t + 1) * DH]
                        nc.tensor.matmul(at, xta[:, s, bass.ts(t, P)], w1a[:], start=True, stop=False)
                        last = nc.tensor.matmul(at, xtb[:, s, bass.ts(t, P)], w1b[:], start=False, stop=True)
                    last.then_inc(w1_done, 1)

                def lowpass_product(i, s):
                    q = quad(i, s)
                    pe.wait_ge(gelu_done, made(q))
                    pe.wait_ge(abs_done, freed(q))
                    for h in range(2):
                        last = nc.tensor.matmul(ps_f[:, s, 0:SEQ], g[:, s, h].rearrange("p m d -> p (m d)"),
                                                lp[:, h, :], start=(h == 0), stop=(h == 1))
                    last.then_inc(fft_done, 1)

                def out_product(i, s):
                    q = quad(i, s)
                    pe.wait_ge(abs_done, made(q))
                    pe.wait_ge(added, freed(q))
                    for m in range(2):
                        k = slice(DP * m, DP * m + DH + 1)
                        for h in range(2):
                            last = nc.tensor.matmul(ps_c[:, s, m, h * C:(h + 1) * C], yt[k, s, bass.ts(h, P)],
                                                    w2s[k, :], start=True, stop=True)
                    last.then_inc(w2_done, 1)

                in_product(0, 0)
                in_product(0, 1)
                lowpass_product(0, 0)
                with pe.Fori(1, QUADS // RING) as i:
                    in_product(i, 0)
                    lowpass_product(i - 1, 1)
                    out_product(i - 1, 0)
                    in_product(i, 1)
                    lowpass_product(i, 0)
                    out_product(i - 1, 1)
                last = QUADS // RING - 1
                lowpass_product(last, 1)
                out_product(last, 0)
                out_product(last, 1)

            @block.scalar
            def _(act):
                act.sem_inc(gelu_done, RING)
                act.sem_inc(abs_done, RING)
                act.sem_inc(hi_done, RING)
                act.wait_ge(consts_in, 7 * 16)
                act.wait_ge(filled, 2)

                def gelu(i, s):
                    q = quad(i, s)
                    act.wait_ge(w1_done, made(q))
                    act.wait_ge(fft_done, freed(q))
                    nc.scalar.activation(g[:, s].rearrange("p h m d -> p m h d")[:, :, :, 0:DH],
                                         ps_w1[:, s, 0:QT * DH].rearrange("p (m h d) -> p m h d", m=2, h=2),
                                         ACT.Gelu).then_inc(gelu_done, 1)

                def magnitude(i, s):
                    q = quad(i, s)
                    act.wait_ge(fft_done, made(q))
                    act.wait_ge(w2_done, freed(q))
                    nc.scalar.activation(yt[:, s, :], ps_f[:, s, 0:SEQ], ACT.Abs,
                                         bias=y_bias[:, 0:1]).then_inc(abs_done, 1)

                def split(i, s):
                    act.wait_ge(stage_in[s], 16 * i + 16)
                    nc.scalar.activation(wa_hi[:, quad(i, s), :], stage[:, s], ACT.Copy).then_inc(hi_done, 1)

                gelu(0, 0)
                gelu(0, 1)
                magnitude(0, 0)
                split(0, 0)
                with act.Fori(1, QUADS // RING) as i:
                    gelu(i, 0)
                    magnitude(i - 1, 1)
                    split(i - 1, 1)
                    gelu(i, 1)
                    magnitude(i, 0)
                    split(i, 0)
                last = QUADS // RING - 1
                magnitude(last, 1)
                split(last, 1)

            @block.gpsimd
            def _(pool):
                pool.sem_inc(lo_done, RING)
                pool.sem_inc(pow_done, RING)
                pool.sem_inc(eps_done, RING)
                pool.sem_inc(mean_done, RING)
                nc.gpsimd.memset(g[:], 0.0).then_inc(filled, 1)
                nc.gpsimd.memset(half[:], -0.5).then_inc(filled, 1)
                pool.wait_ge(filled, 2)

                def split(i, s):
                    q = quad(i, s)
                    pool.wait_ge(hi_done, made(q))
                    pool.sem_inc(pool_turn, 1)
                    nc.gpsimd.tensor_tensor(wa_lo[:, q, :], stage[:, s], wa_hi[:, q, :].bitcast(F32),
                                            ALU.subtract).then_inc(lo_done, 1)

                def deviation(i, s):
                    row_deviation(nc, pool, quad(i, s), s, mv, vtmp, half, mean, rstd, mv_done, eps_done,
                                  pow_done, mean_done, pool_turn)

                split(0, 0)
                with pool.Fori(1, QUADS // RING) as i:
                    split(i - 1, 1)
                    deviation(i - 1, 0)
                    split(i, 0)
                    deviation(i - 1, 1)
                last = QUADS // RING - 1
                split(last, 1)
                deviation(last, 0)
                deviation(last, 1)

            @block.vector
            def _(dve):
                nc.vector.memset(xtb[CB:CB + 1, :, :], 1.0).then_inc(bias_row, 1)
                dve.sem_inc(added, RING)
                dve.sem_inc(stats_done, RING)
                dve.sem_inc(mv_done, RING)

                def finish(i, s):
                    q = quad(i, s)
                    dve.wait_ge(w2_done, made(q))
                    for m in range(2):
                        at = xs[:, bass.ts(2 * q + m, 2), :]
                        ins = nc.vector.tensor_tensor(
                            at, ps_c[:, s, m, 0:2 * C].rearrange("p (h c) -> p h c", h=2), at, ALU.add)
                    ins.then_inc(added, 1)
                    row_statistics(nc, dve, q, s, xs, stats, mv, added, stats_done, mv_done, pow_done, mean_done, dve_turn)

                for x_part in x_in:
                    dve.wait_ge(x_part, 16)
                with dve.Fori(0, QUADS // RING) as i:
                    for s in range(RING):
                        finish(i, s)


def row_statistics(nc, dve, q, s, xs, stats, mv, written, stats_done, mv_done, pow_done, mean_done, dve_turn):
    dve.wait_ge(written, made(q))
    dve.sem_inc(dve_turn, 1)
    for t in range(QT):
        ins = nc.vector.bn_stats(stats[:, s, t, :], xs[:, QT * q + t, :])
    ins.then_inc(stats_done, 1)
    dve.wait_ge(stats_done, made(q))
    dve.wait_ge(pow_done, freed(q))
    dve.wait_ge(mean_done, freed(q))
    dve.sem_inc(dve_turn, 1)
    for t in range(QT):
        ins = nc.vector.bn_aggr(mv[:, s, t, :], stats[:, s, t, :])
    ins.then_inc(mv_done, 1)


def row_deviation(nc, pool, q, s, mv, vtmp, half, mean, rstd, mv_done, eps_done, pow_done, mean_done, pool_turn):
    pool.wait_ge(mv_done, made(q))
    pool.sem_inc(pool_turn, 1)
    nc.gpsimd.tensor_scalar(vtmp[:, s, :], mv[:, s, :, 1], EPS, None, ALU.add).then_inc(eps_done, 1)
    nc.gpsimd.tensor_copy(mean[:, bass.ts(q, QT)], mv[:, s, :, 0]).then_inc(mean_done, 1)
    pool.wait_ge(eps_done, made(q))
    pool.sem_inc(pool_turn, 1)
    nc.gpsimd.tensor_tensor(rstd[:, bass.ts(q, QT)], vtmp[:, s, :], half[:, 0:1].broadcast_to([P, QT]),
                            ALU.pow).then_inc(pow_done, 1)


def normalise(nc, dve, q, s, xs, mean, rstd, xn, tr_done, xn_done):
    dve.wait_ge(tr_done, freed(q))
    for t in range(QT):
        at = QT * q + t
        ins = nc.vector.tensor_scalar(xn[:, s, t, :], xs[:, at, :], mean[:, bass.ds(at, 1)],
                                      rstd[:, bass.ds(at, 1)], ALU.subtract, ALU.mult)
    ins.then_inc(xn_done, 1)


def transposes(nc, pe, q, s, xn, eye, ps_a, ps_b, xn_done, ev_done, tr_done):
    pe.wait_ge(xn_done, made(q))
    pe.wait_ge(ev_done, freed(q))
    for t in range(QT):
        nc.tensor.transpose(ps_a[:, s, bass.ts(t, P)], xn[:, s, t, 0:P], eye[:])
        ins = nc.tensor.transpose(ps_b[0:CB, s, bass.ts(t, P)], xn[:, s, t, P:C], eye[:])
    ins.then_inc(tr_done, 1)


def evacuate(nc, act, q, s, ps_a, ps_b, xa, xb, tr_done, used, ev_done):
    act.wait_ge(tr_done, made(q))
    act.wait_ge(used, freed(q))
    nc.scalar.activation(xa[:, s, :], ps_a[:, s, :], ACT.Copy)
    nc.scalar.activation(xb[0:CB, s, :], ps_b[0:CB, s, :], ACT.Copy).then_inc(ev_done, 1)


def attention_phase(nc, xs, mean, rstd, eye, wqkv, cos, sin, rows, wgu, wb_hi, wb_lo):
    with ExitStack() as stack:
        a = Scope(nc, stack, "attn")
        wqa, wqb = a.sb("wqa", [P, QW]), a.sb("wqb", [CB + 1, QW])
        cos_t, sin_t = a.sb("cos_t", [P, QT, 24]), a.sb("sin_t", [P, QT, 24])
        xn = a.sb("xn", [P, RING, QT, C])
        xa, xb = a.sb("xa", [P, RING, QT * P]), a.sb("xb", [CB + 1, RING, QT * P])
        qkv = a.sb("qkv", [P, RING, QT, QW])
        ka, kb, kr = a.sb("ka", [P, QT, 24]), a.sb("kb", [P, QT, 24]), a.sb("kr", [P, QT, 24])
        kc, kd, kk = a.sb("kc", [P, QT, HD]), a.sb("kd", [P, QT, HD]), a.sb("kk", [P, RING, QT, HD])
        prod = a.sb("prod", [P, QT, HEADS, HD])
        pv = a.sb("pv", [P, RING, QT, HEADS, HD])
        score, diff = a.sb("score", [P, RING, QT * HEADS]), a.sb("diff", [P, RING, QT * HEADS])
        ex, den = a.sb("ex", [P, RING, QT * HEADS]), a.sb("den", [P, RING, QT * HEADS])
        rec, wt = a.sb("rec", [P, RING, QT * HEADS]), a.sb("wt", [P, RING, QT * HEADS])
        stage = a.sb("stage", [P, RING, 2 * HID])
        stats, mv = a.sb("stats", [P, RING, QT, 6]), a.sb("mv", [P, RING, QT, 2])
        vtmp, half = a.sb("vtmp", [P, RING, QT]), a.sb("half", [P, 1])
        zero = a.sb("zero", [P, ROW])
        ps_a, ps_b = a.ps("ps_a", [P, RING, 512]), a.ps("ps_b", [P, RING, 512])
        ps_q = a.ps("ps_q", [P, RING, 2, 512])

        consts_in, stored, filled, bias_row = a.sem("consts_in"), a.sem("stored"), a.sem("filled"), a.sem("bias_row")
        stage_in = [a.sem(f"stage_in{s}") for s in range(RING)]
        xn_done, tr_done, ev_done = a.sem("xn_done"), a.sem("tr_done"), a.sem("ev_done")
        qkv_done, cp_done, kk_done = a.sem("qkv_done"), a.sem("cp_done"), a.sem("kk_done")
        rope_step = a.sem("rope_step")
        prod_done, score_done, diff_done = a.sem("prod_done"), a.sem("score_done"), a.sem("diff_done")
        ex_done, den_done, rec_done, wt_done = a.sem("ex_done"), a.sem("den_done"), a.sem("rec_done"), a.sem("wt_done")
        pv_done, res_done = a.sem("pv_done"), a.sem("res_done")
        stats_done, mv_done = a.sem("stats_done"), a.sem("mv_done")
        lo_done, eps_done, pow_done, mean_done = a.sem("lo_done"), a.sem("eps_done"), a.sem("pow_done"), a.sem("mean_done")
        hi_done, pool_turn, dve_turn = a.sem("hi_done"), a.sem("pool_turn"), a.sem("dve_turn")
        last = QUADS // RING - 1

        with nc.Block() as block:
            @block.sync
            def _(sp):
                sp.dma_start(wqa[:], wqkv[0:P, :]).then_inc(consts_in, 16)
                sp.dma_start(wqb[:], wqkv[P:C + 1, :]).then_inc(consts_in, 16)
                for h in range(2):
                    sp.dma_start(cos_t[:, 2 * h:2 * h + 2, :], cos.rearrange("(h p) d -> p h d", p=P)).then_inc(consts_in, 16)
                    sp.dma_start(sin_t[:, 2 * h:2 * h + 2, :], sin.rearrange("(h p) d -> p h d", p=P)).then_inc(consts_in, 16)
                sp.wait_ge(filled, 2)
                sp.dma_start(rows[TOKENS:TOKENS + P, :], zero[:]).then_inc(stored, 16)

                def load_weights(i, s):
                    q = quad(i, s)
                    sp.wait_ge(lo_done, freed(q))
                    sp.dma_start(stage[0:CB, s], wgu[P:C, q, :]).then_inc(stage_in[s], 16)
                    sp.dma_start(stage[CB:P, s], wgu[P:C, q, :]).then_inc(stage_in[s], 16)

                load_weights(0, 0)
                load_weights(0, 1)
                with sp.Fori(1, QUADS // RING) as i:
                    for s in range(RING):
                        load_weights(i, s)
                sp.wait_ge(stored, 16)

            @block.tensor
            def _(pe):
                pe.sem_inc(tr_done, RING)
                pe.sem_inc(qkv_done, RING)
                pe.wait_ge(consts_in, 6 * 16)
                pe.wait_ge(bias_row, 1)

                def turn(i, s):
                    transposes(nc, pe, quad(i, s), s, xn, eye, ps_a, ps_b, xn_done, ev_done, tr_done)

                def project(i, s):
                    q = quad(i, s)
                    pe.wait_ge(ev_done, made(q))
                    pe.wait_ge(cp_done, freed(q))
                    for t in range(QT):
                        at = ps_q[:, s, t // 2, (t % 2) * QW:(t % 2 + 1) * QW]
                        nc.tensor.matmul(at, xa[:, s, bass.ts(t, P)], wqa[:], start=True, stop=False)
                        ins = nc.tensor.matmul(at, xb[:, s, bass.ts(t, P)], wqb[:], start=False, stop=True)
                    ins.then_inc(qkv_done, 1)

                turn(0, 0)
                with pe.Fori(0, last) as i:
                    project(i, 0)
                    turn(i, 1)
                    project(i, 1)
                    turn(i + 1, 0)
                project(last, 0)
                turn(last, 1)
                project(last, 1)

            @block.scalar
            def _(act):
                act.sem_inc(ev_done, RING)
                act.sem_inc(cp_done, RING)
                act.sem_inc(ex_done, RING)
                act.sem_inc(hi_done, RING)

                def out_of_psum(i, s):
                    evacuate(nc, act, quad(i, s), s, ps_a, ps_b, xa, xb, tr_done, qkv_done, ev_done)

                def copy_qkv(i, s):
                    q = quad(i, s)
                    act.wait_ge(qkv_done, made(q))
                    act.wait_ge(prod_done, freed(q))
                    act.wait_ge(pv_done, freed(q))
                    for h in range(2):
                        ins = nc.scalar.activation(qkv[:, s, 2 * h:2 * h + 2, :],
                                                   ps_q[:, s, h, 0:2 * QW].rearrange("p (t c) -> p t c", t=2), ACT.Copy)
                    ins.then_inc(cp_done, 1)

                def exponential(i, s):
                    q = quad(i, s)
                    act.wait_ge(diff_done, made(q))
                    nc.scalar.activation(ex[:, s], diff[:, s], ACT.Exp, scale=SCALE).then_inc(ex_done, 1)

                def split(i, s):
                    act.wait_ge(stage_in[s], 32 * i + 32)
                    nc.scalar.activation(wb_hi[:, quad(i, s), :], stage[:, s], ACT.Copy).then_inc(hi_done, 1)

                def quad_work(i, s, more):
                    copy_qkv(i, s)
                    if more:
                        out_of_psum(i + (s + 1) // RING, (s + 1) % RING)
                    split(i, s)
                    exponential(i, s)

                out_of_psum(0, 0)
                with act.Fori(0, last) as i:
                    quad_work(i, 0, True)
                    quad_work(i, 1, True)
                quad_work(last, 0, True)
                quad_work(last, 1, False)

            @block.gpsimd
            def _(pool):
                for c in (lo_done, pow_done, eps_done, mean_done, kk_done, pv_done):
                    pool.sem_inc(c, RING)
                nc.gpsimd.memset(zero[:], 0.0).then_inc(filled, 1)
                nc.gpsimd.memset(half[:], -0.5).then_inc(filled, 1)
                pool.wait_ge(filled, 2)
                pool.wait_ge(consts_in, 6 * 16)

                def rotate_key(i, s):
                    q = quad(i, s)
                    pool.wait_ge(cp_done, made(q))
                    pool.wait_ge(prod_done, freed(q))
                    pool.sem_inc(pool_turn, 1)
                    nc.gpsimd.tensor_tensor(ka[:], qkv[:, s, :, KC:KC + 24], cos_t[:], ALU.mult)
                    nc.gpsimd.tensor_tensor(kb[:], qkv[:, s, :, KC + 8:KC + 32], sin_t[:], ALU.mult).then_inc(rope_step, 1)
                    pool.wait_ge(rope_step, 3 * q + 1)
                    nc.gpsimd.tensor_tensor(kr[:], ka[:], kb[:], ALU.add).then_inc(rope_step, 1)
                    pool.wait_ge(rope_step, 3 * q + 2)
                    nc.gpsimd.tensor_tensor(kc[:], kr[:, :, 0:HD], cos_t[:, :, 0:HD], ALU.mult)
                    nc.gpsimd.tensor_tensor(kd[:], kr[:, :, 8:8 + HD], sin_t[:, :, 0:HD], ALU.mult).then_inc(rope_step, 1)
                    pool.wait_ge(rope_step, 3 * q + 3)
                    nc.gpsimd.tensor_tensor(kk[:, s], kc[:], kd[:], ALU.subtract).then_inc(kk_done, 1)

                def split(i, s):
                    q = quad(i, s)
                    pool.wait_ge(hi_done, made(q))
                    pool.sem_inc(pool_turn, 1)
                    nc.gpsimd.tensor_tensor(wb_lo[:, q, :], stage[0:CB, s], wb_hi[0:CB, q, :].bitcast(F32),
                                            ALU.subtract).then_inc(lo_done, 1)

                def weigh_value(i, s):
                    q = quad(i, s)
                    pool.wait_ge(wt_done, made(q))
                    pool.wait_ge(res_done, freed(q))
                    pool.sem_inc(pool_turn, 1)
                    w = wt[:, s].rearrange("p (t h) -> p t h", t=QT)
                    for h in range(2):
                        t = slice(2 * h, 2 * h + 2)
                        ins = nc.gpsimd.tensor_tensor(pv[:, s, t], bcast(w[:, t, :], 3, HD),
                                                      bcast(qkv[:, s, t, VC:VC + HD], 2, HEADS), ALU.mult)
                    ins.then_inc(pv_done, 1)

                def deviation(i, s):
                    row_deviation(nc, pool, quad(i, s), s, mv, vtmp, half, mean, rstd, mv_done, eps_done,
                                  pow_done, mean_done, pool_turn)

                rotate_key(0, 0)
                split(0, 0)
                weigh_value(0, 0)
                rotate_key(0, 1)
                split(0, 1)
                deviation(0, 0)
                weigh_value(0, 1)
                with pool.Fori(1, QUADS // RING) as i:
                    for s in range(RING):
                        rotate_key(i, s)
                        split(i, s)
                        deviation(i - 1 + s, 1 - s)
                        weigh_value(i, s)
                deviation(last, 1)

            @block.vector
            def _(dve):
                nc.vector.memset(xb[CB:CB + 1, :, :], 1.0).then_inc(bias_row, 1)
                for c in (xn_done, prod_done, score_done, diff_done, den_done, rec_done, wt_done, res_done,
                          stats_done, mv_done):
                    dve.sem_inc(c, RING)

                def norm(i, s):
                    normalise(nc, dve, quad(i, s), s, xs, mean, rstd, xn, tr_done, xn_done)

                def scores(i, s):
                    q = quad(i, s)
                    dve.wait_ge(kk_done, made(q))
                    for h in range(2):
                        t = slice(2 * h, 2 * h + 2)
                        ins = nc.vector.tensor_tensor(
                            prod[:, t], qkv[:, s, t, 0:C].rearrange("p t (h d) -> p t h d", h=HEADS),
                            bcast(kk[:, s, t, :], 2, HEADS), ALU.mult)
                    ins.then_inc(prod_done, 1)
                    dve.wait_ge(prod_done, made(q))
                    nc.vector.tensor_reduce(score[:, s], prod[:].rearrange("p t h d -> p (t h) d"), AX.X,
                                            ALU.add).then_inc(score_done, 1)
                    dve.wait_ge(score_done, made(q))
                    nc.vector.tensor_tensor(diff[:, s], score[:, s], score[:, s], ALU.subtract).then_inc(diff_done, 1)

                def weights(i, s):
                    q = quad(i, s)
                    dve.wait_ge(ex_done, made(q))
                    nc.vector.tensor_scalar(den[:, s], ex[:, s], float(HEADS), None, ALU.mult).then_inc(den_done, 1)
                    dve.wait_ge(den_done, made(q))
                    nc.vector.reciprocal(rec[:, s], den[:, s]).then_inc(rec_done, 1)
                    dve.wait_ge(rec_done, made(q))
                    dve.wait_ge(pv_done, freed(q))
                    nc.vector.tensor_tensor(wt[:, s], den[:, s], rec[:, s], ALU.mult).then_inc(wt_done, 1)

                def residual(i, s):
                    q = quad(i, s)
                    dve.wait_ge(pv_done, made(q))
                    at = xs[:, bass.ts(q, QT), :]
                    nc.vector.tensor_tensor(at, at, pv[:, s].rearrange("p t h d -> p t (h d)"),
                                            ALU.add).then_inc(res_done, 1)
                    row_statistics(nc, dve, q, s, xs, stats, mv, res_done, stats_done, mv_done, pow_done, mean_done, dve_turn)

                norm(0, 0)
                norm(0, 1)
                scores(0, 0)
                weights(0, 0)
                with dve.Fori(1, QUADS // RING) as i:
                    for s in range(RING):
                        norm(i, s)
                        scores(i - 1 + s, 1 - s)
                        residual(i - 1, s)
                        weights(i - 1 + s, 1 - s)
                scores(last, 1)
                residual(last, 0)
                weights(last, 1)
                residual(last, 1)


def routing_phase(nc, xs, mean, rstd, eye, gate, tri, iotas, row_tiles, down, wd_hi, wd_lo,
                  idx_map, tile_col, tile_exp):
    E, T = EXPERTS, TILES
    with ExitStack() as stack:
        a = Scope(nc, stack, "route")
        ga, gb = a.sb("ga", [P, E]), a.sb("gb", [CB, E])
        trit = a.sb("trit", [P, P])
        ones = a.sb("ones", [P, P])
        io = a.sb("io", [P, MAPW])
        desc = a.sb("desc", [P, T, E])
        off = a.sb("off", [P, T, E])
        first = a.sb("first", [P, E, T])
        idp = a.sb("idp", [P, 2, T])
        step = a.sb("step", [P, SLOTS])
        pad = a.sb("pad", [P, 5])
        last_col = a.sb("last_col", [P, TILES_MAX])
        xn = a.sb("xn", [P, RING, QT, C])
        xa, xb = a.sb("xa", [P, RING, QT * P]), a.sb("xb", [CB, RING, QT * P])
        stage = a.sb("stage", [P, RING, 3 * C])
        lg, pr, tmp, m1, m2, tmp2 = (a.sb(n, [P, T, E]) for n in ("lg", "pr", "tmp", "m1", "m2", "tmp2"))
        both, gates, base = a.sb("both", [P, T, E]), a.sb("gates", [P, T, E]), a.sb("base", [P, T, E])
        tot, inc = a.sb("tot", [P, E, T]), a.sb("inc", [P, E, T])
        red = a.sb("red", [P, 12, T])
        pos, keyb = a.sb("pos", [P, 2, T]), a.sb("keyb", [P, 2, 2, T])
        posi, keyi = a.sb("posi", [P, 2, T], I32), a.sb("keyi", [P, 2, 2, T], I32)
        ce, cum = a.sb("ce", [P, E]), a.sb("cum", [P, E])
        ge, gc = a.sb("ge", [P, TILES_MAX, E]), a.sb("gc", [P, TILES_MAX, E])
        tt = a.sb("tt", [P, 8, TILES_MAX])
        hot_b = a.sb("hot_b", [P, RING, P], F32R)
        hot_a = a.sb("hot_a", [P, RING, MAPW], F32R)
        cnt = m1[:].rearrange("p t e -> p (t e)").rearrange("p (e k) -> p e k", e=E)
        slot_v, slot_t = base[:].rearrange("p t e -> p (t e)"), both[:].rearrange("p t e -> p (t e)")
        ps_a, ps_b = a.ps("ps_a", [P, RING, 512]), a.ps("ps_b", [P, RING, 512])
        ps_g, ps_p = a.ps("ps_g", [P, 512]), a.ps("ps_p", [P, 512])
        ps_t, ps_m = a.ps("ps_t", [P, 512]), a.ps("ps_m", [P, 512])

        consts_in, gates_out = a.sem("consts_in"), a.sem("gates_out")
        rows_out = [a.sem(f"rows_out{s}") for s in range(RING)]
        stage_in = [a.sem(f"stage_in{s}") for s in range(RING)]
        filled, xn_done, tr_done, ev_done = a.sem("filled"), a.sem("xn_done"), a.sem("tr_done"), a.sem("ev_done")
        gate_done, diff_done, ex_done = a.sem("gate_done"), a.sem("diff_done"), a.sem("ex_done")
        hi_done, lo_done, pool_turn = a.sem("hi_done"), a.sem("lo_done"), a.sem("pool_turn")
        chain = a.sem("chain")
        chosen, counted = a.sem("chosen"), a.sem("counted")
        gates_done = a.sem("gates_done")
        hot_done, map_done = a.sem("hot_done"), a.sem("map_done")
        last = QUADS // RING - 1
        consts = [(ga, gate[0:P, :]), (gb, gate[P:C, :]), (trit, tri)] + [
            (dst, src) for dst, src in zip((io, desc, off, first, idp, step, pad, last_col), iotas)]

        with nc.Block() as block:
            @block.sync
            def _(sp):
                for s in range(RING):
                    sp.sem_inc(rows_out[s], 32)
                for dst, src in consts:
                    sp.dma_start(dst[:], src).then_inc(consts_in, 16)

                def load_weights(i, s):
                    q = quad(i, s)
                    sp.wait_ge(lo_done, freed(q))
                    sp.dma_start(stage[:, s].rearrange("p (k c) -> p k c", k=3),
                                 down[q].rearrange("(k p) c -> p k c", p=P)).then_inc(stage_in[s], 16)

                def store(i, s):
                    q = quad(i, s)
                    sp.wait_ge(xn_done, made(q))
                    sp.dma_start(row_tiles[:, bass.ts(q, QT), 0:C], xn[:, s]).then_inc(rows_out[s], 16)
                    sp.dma_start(row_tiles[:, bass.ts(q, QT), C:GC], xn[:, s, :, P:C]).then_inc(rows_out[s], 16)

                with sp.Fori(0, QUADS // RING) as i:
                    for s in range(RING):
                        load_weights(i, s)
                        store(i, s)
                sp.wait_ge(gates_done, 1)
                sp.dma_start(row_tiles[:, :, GC:ROW], gates[:]).then_inc(gates_out, 16)
                for s in range(RING):
                    sp.wait_ge(rows_out[s], 32 * (QUADS // RING + 1))
                sp.wait_ge(gates_out, 16)

            @block.gpsimd
            def _(pool):
                pool.sem_inc(lo_done, RING)
                nc.gpsimd.memset(ones[:], 1.0).then_inc(filled, 1)

                def split(i, s):
                    q = quad(i, s)
                    pool.wait_ge(hi_done, made(q))
                    pool.sem_inc(pool_turn, 1)
                    nc.gpsimd.tensor_tensor(wd_lo[:, q, :], stage[:, s], wd_hi[:, q, :].bitcast(F32),
                                            ALU.subtract).then_inc(lo_done, 1)

                with pool.Fori(0, QUADS // RING) as i:
                    for s in range(RING):
                        split(i, s)

            @block.scalar
            def _(act):
                act.sem_inc(ev_done, RING)
                act.sem_inc(hi_done, RING)

                with act.Fori(0, QUADS // RING) as i:
                    for s in range(RING):
                        q = quad(i, s)
                        evacuate(nc, act, q, s, ps_a, ps_b, xa, xb, tr_done, gate_done, ev_done)
                        act.wait_ge(stage_in[s], 16 * i + 16)
                        nc.scalar.activation(wd_hi[:, q, :], stage[:, s], ACT.Copy).then_inc(hi_done, 1)
                act.wait_ge(diff_done, 1)
                nc.scalar.activation(pr[:], lg[:], ACT.Exp).then_inc(ex_done, 1)

            @block.tensor
            def _(pe):
                pe.sem_inc(tr_done, RING)
                pe.sem_inc(gate_done, RING)
                pe.wait_ge(consts_in, 16 * len(consts))

                def turn(i, s):
                    transposes(nc, pe, quad(i, s), s, xn, eye, ps_a, ps_b, xn_done, ev_done, tr_done)

                def gate_product(i, s):
                    q = quad(i, s)
                    pe.wait_ge(ev_done, made(q))
                    for t in range(QT):
                        at = ps_g[:, bass.ds((QT * q + t) * E, E)]
                        nc.tensor.matmul(at, xa[:, s, bass.ts(t, P)], ga[:], start=True, stop=False)
                        ins = nc.tensor.matmul(at, xb[:, s, bass.ts(t, P)], gb[:], start=False, stop=True)
                    ins.then_inc(gate_done, 1)

                turn(0, 0)
                with pe.Fori(0, last) as i:
                    turn(i, 1)
                    gate_product(i, 0)
                    turn(i + 1, 0)
                    gate_product(i, 1)
                turn(last, 1)
                gate_product(last, 0)
                gate_product(last, 1)

                pe.wait_ge(chosen, 1)
                pe.wait_ge(filled, 1)
                flat = both[:].rearrange("p t e -> p (t e)")
                nc.tensor.matmul(ps_p[:, 0:T * E], trit[:], flat, start=True, stop=True)
                nc.tensor.matmul(ps_t[:, 0:T * E], ones[:], flat, start=True, stop=True).then_inc(counted, 1)

                def place(n, ring, start, stop):
                    pe.wait_ge(hot_done, n + 1)
                    nc.tensor.matmul(ps_m[:, 0:MAPW], hot_b[:, ring, :], hot_a[:, ring, :], start=start,
                                     stop=stop).then_inc(map_done, 1)

                place(0, 0, True, False)
                place(1, 1, False, False)
                with pe.Fori(1, T - 1) as t:
                    place(2 * t, 0, False, False)
                    place(2 * t + 1, 1, False, False)
                place(2 * T - 2, 0, False, False)
                place(2 * T - 1, 1, False, True)

            @block.vector
            def _(dve):
                dve.sem_inc(xn_done, RING)

                def norm(i, s):
                    dve.wait_ge(rows_out[s], 32 * i + 32)
                    normalise(nc, dve, quad(i, s), s, xs, mean, rstd, xn, tr_done, xn_done)

                with dve.Fori(0, QUADS // RING) as i:
                    for s in range(RING):
                        norm(i, s)

                count = [0]

                def then(ins):
                    ins.then_inc(chain, 1)
                    count[0] += 1
                    dve.wait_ge(chain, count[0])

                tt2, ts = nc.vector.tensor_tensor, nc.vector.tensor_scalar

                def reduce(dst, src, op):
                    then(nc.vector.tensor_reduce(dst, src, AX.X, op))

                def over(ap):
                    return bcast(ap, 2, E)

                mx, sm, rs, p1, f1, p2, f2, dn, rd, g1, g2 = (red[:, k, :] for k in range(11))
                dve.wait_ge(gate_done, QUADS + RING)
                dve.wait_ge(consts_in, 16 * len(consts))
                logits = ps_g[:, 0:T * E].rearrange("p (t e) -> p t e", e=E)
                reduce(mx, logits, ALU.max)
                tt2(lg[:], logits, over(mx), ALU.subtract).then_inc(diff_done, 1)
                dve.wait_ge(ex_done, 1)
                reduce(sm, pr[:], ALU.add)
                then(nc.vector.reciprocal(rs, sm))
                then(tt2(pr[:], pr[:], over(rs), ALU.mult))
                reduce(p1, pr[:], ALU.max)
                then(tt2(tmp[:], pr[:], over(p1), ALU.is_equal))
                then(tt2(tmp2[:], tmp[:], desc[:], ALU.mult))
                reduce(f1, tmp2[:], ALU.max)
                then(tt2(m1[:], desc[:], over(f1), ALU.is_equal))
                then(nc.vector.scalar_tensor_tensor(out=tmp[:], in0=m1[:], scalar=-2.0, in1=pr[:],
                                                    op0=ALU.mult, op1=ALU.add))
                reduce(p2, tmp[:], ALU.max)
                then(tt2(tmp2[:], tmp[:], over(p2), ALU.is_equal))
                then(tt2(tmp[:], tmp2[:], desc[:], ALU.mult))
                reduce(f2, tmp[:], ALU.max)
                then(tt2(m2[:], desc[:], over(f2), ALU.is_equal))
                tt2(both[:], m1[:], m2[:], ALU.add).then_inc(chosen, 1)
                then(tt2(dn, p1, p2, ALU.add))
                then(ts(dn, dn, 1e-8, None, ALU.add))
                then(nc.vector.reciprocal(rd, dn))
                tt2(g1, p1, rd, ALU.mult)
                then(tt2(g2, p2, rd, ALU.mult))
                tt2(tmp[:], m1[:], over(g1), ALU.mult)
                then(tt2(tmp2[:], m2[:], over(g2), ALU.mult))
                tt2(gates[:], tmp[:], tmp2[:], ALU.add).then_inc(gates_done, 1)
                dve.wait_ge(counted, 1)
                then(nc.vector.tensor_copy(tot[:], ps_t[:, 0:T * E].rearrange("p (t e) -> p e t", e=E)))
                flat = "p e t -> p (e t)"
                then(nc.vector.tensor_tensor_scan(inc[:].rearrange(flat), first[:].rearrange(flat),
                                                  tot[:].rearrange(flat), 0.0, ALU.mult, ALU.add))
                then(tt2(tot[:], inc[:], tot[:], ALU.subtract))
                then(tt2(base[:], ps_p[:, 0:T * E].rearrange("p (t e) -> p t e", e=E), off[:], ALU.add))
                then(tt2(base[:], base[:], tot[:].rearrange("p e t -> p t e"), ALU.add))
                tt2(tmp[:], m1[:], base[:], ALU.mult)
                then(tt2(tmp2[:], m2[:], base[:], ALU.mult))
                nc.vector.tensor_reduce(pos[:, 0, :], tmp[:], AX.X, ALU.add)
                reduce(pos[:, 1, :], tmp2[:], ALU.add)
                then(nc.vector.tensor_copy(posi[:], pos[:]))
                ts(keyi[:, 0], posi[:], 7, None, ALU.arith_shift_right)
                then(ts(keyi[:, 1], posi[:], P - 1, None, ALU.bitwise_and))
                then(nc.vector.tensor_copy(keyb[:], keyi[:]))

                def hot(n, t, k, ring):
                    if n is not None:
                        dve.wait_ge(map_done, n - 1)
                    ts(hot_b[:, ring, :], io[:, 0:P], keyb[:, 1, k, bass.ds(t, 1)], None, ALU.is_equal)
                    ts(hot_a[:, ring, :], io[:], keyb[:, 0, k, bass.ds(t, 1)], idp[:, k, bass.ds(t, 1)],
                       ALU.is_equal, ALU.mult).then_inc(hot_done, 1)

                hot(None, 0, 0, 0)
                hot(None, 0, 1, 1)
                with dve.Fori(1, T) as t:
                    hot(2 * t, t, 0, 0)
                    hot(2 * t + 1, t, 1, 1)

                tot_e = inc[:, :, T - 1]
                then(tt2(cnt, bcast(tot_e, 2, SLOTS), bcast(step[:], 1, E), ALU.is_gt))
                reduce(ce[:], cnt, ALU.add)
                then(nc.vector.tensor_tensor_scan(cum[:], ones[:, 0:E], ce[:], 0.0, ALU.mult, ALU.add))
                J = io[:, 0:TILES_MAX]
                then(tt2(ge[:], bcast(J, 2, E), bcast(cum[:], 1, TILES_MAX), ALU.is_ge))
                then(tt2(gc[:], ge[:], bcast(ce[:], 1, TILES_MAX), ALU.mult))
                e_j, start_j, a_j, b_j, c_j, d_j, v_j, w_j = (tt[:, k, :] for k in range(8))
                nc.vector.tensor_reduce(e_j, ge[:], AX.X, ALU.add)
                reduce(start_j, gc[:], ALU.add)
                ts(v_j, e_j, float(E), None, ALU.is_lt)
                then(tt2(a_j, J, start_j, ALU.subtract))
                then(nc.vector.scalar_tensor_tensor(out=b_j, in0=e_j, scalar=float(SLOTS), in1=a_j,
                                                    op0=ALU.mult, op1=ALU.add))
                then(tt2(c_j, b_j, last_col[:], ALU.subtract))
                then(tt2(d_j, c_j, v_j, ALU.mult))
                tt2(tile_col[:], d_j, last_col[:], ALU.add)
                ts(tile_exp[:], e_j, float(E - 1), None, ALU.min)
                flat_t = "p t e -> p (t e)"
                slot_i, slot_e = tmp[:].bitcast(I32).rearrange(flat_t), desc[:].rearrange(flat_t)
                then(nc.vector.tensor_copy(slot_i, io[:]))
                then(ts(slot_i, slot_i, MAPW - SLOTS, 2, ALU.bitwise_and, ALU.arith_shift_left))
                then(nc.vector.tensor_copy(slot_e, slot_i))
                dve.wait_ge(map_done, 2 * T)
                then(nc.vector.tensor_copy(slot_v, ps_m[:, 0:MAPW]))
                ts(slot_t, slot_v, 0.0, pad[:, 0:1], ALU.is_equal, ALU.mult)
                size = tmp2[:].rearrange(flat_t)
                stt = nc.vector.scalar_tensor_tensor
                then(stt(out=size, in0=slot_v, scalar=-1.0, in1=slot_v, op0=ALU.mult, op1=ALU.max))
                then(stt(out=slot_t, in0=size, scalar=-1.0, in1=slot_t, op0=ALU.add, op1=ALU.add))
                then(stt(out=slot_e, in0=slot_v, scalar=0.0, in1=slot_e, op0=ALU.is_equal, op1=ALU.mult))
                then(stt(out=slot_e, in0=slot_t, scalar=0.0, in1=slot_e, op0=ALU.add, op1=ALU.add))
                then(ts(slot_v, slot_v, 0.0, float(TOKENS), ALU.is_le, ALU.mult))
                nc.vector.tensor_copy(idx_map[:, 0:MAPW, 0], slot_t)
                tt2(idx_map[:, 0:MAPW, 1], slot_e, slot_v, ALU.add)
                nc.vector.tensor_copy(idx_map[:, MAPW:MAPW + 2, :], pad[:, 1:5].rearrange("p (a b) -> p a b", a=2))


def expert_phase(nc, xs, eye, rows, chosen_rows, out, wa_hi, wa_lo, wb_hi, wb_lo, wd_hi, wd_lo, idx_map, tile_col, tile_exp):
    with ExitStack() as stack:
        a = Scope(nc, stack, "moe")
        xt = a.sb("xt", [P, XR, ROW])
        idx = a.sb("idx", [P, XR, 2], I32)
        x_hi = a.sb("x_hi", [P, RING, 2 * P], F32R)
        x_lo = a.sb("x_lo", [P, RING, P], F32R)
        sg, hid = a.sb("sg", [P, RING, HID]), a.sb("hid", [P, RING, HID])
        h_hi, h_lo = a.sb("h_hi", [P, RING, HID], F32R), a.sb("h_lo", [P, RING, HID], F32R)
        y = a.sb("y", [P, YR, C])
        pick = a.sb("pick", [P, RING, 2, QT, C])
        ps_x, ps_h = a.ps("ps_x", [P, 512]), a.ps("ps_h", [P, 512])
        ps_g, ps_u, ps_y = (a.ps(n, [P, RING, 512]) for n in ("ps_gt", "ps_u", "ps_y"))

        gathered = [a.sem(f"gathered{s}") for s in range(XR)]
        scattered = [a.sem(f"scattered{s}") for s in range(YR)]
        picked, out_stored = ([a.sem(f"{n}{s}") for s in range(RING)] for n in ("picked", "out_stored"))
        sum_done, total_done = a.sem("sum_done"), a.sem("total_done")
        idx_done, pool_turn = a.sem("idx_done"), a.sem("pool_turn")
        xt_done, gate_done, up_done, ht_done, y_mm = (a.sem(n) for n in ("xt_done", "gate_done", "up_done", "ht_done", "y_mm"))
        x_hi_done, x_lo_done, x_lob_done = a.sem("x_hi_done"), a.sem("x_lo_done"), a.sem("x_lob_done")
        silu_done, hid_done = a.sem("silu_done"), a.sem("hid_done")
        h_hi_done, h_lo_done, y_done = a.sem("h_hi_done"), a.sem("h_lo_done"), a.sem("y_done")
        N = TILES_MAX

        with nc.Block() as block:
            @block.gpsimd
            def _(pool):
                pool.sem_inc(idx_done, RING)

                def gather(i, r):
                    j, n, slot = XR * i + r, i + r // XR, r % XR
                    col = pool.value_load(tile_col[0:1, bass.ds(j, 1)], min_val=0, max_val=MAPW + 1)
                    nc.gpsimd.tensor_copy(idx[:, slot, :], idx_map[:, bass.ds(col, 1), :]).then_inc(idx_done, 1)
                    pool.wait_ge(idx_done, made(j))
                    pool.sem_inc(pool_turn, 1)
                    nc.gpsimd.indirect_dma_start(
                        xt[:, slot, :], None, rows.ap(),
                        bass.IndirectOffsetOnAxis(ap=idx[:, slot, 0:1], axis=0)).then_inc(gathered[slot], 16)

                def scatter(i, r):
                    j, slot = XR * i + r, r % XR
                    pool.wait_ge(y_done, made(j))
                    pool.sem_inc(pool_turn, 1)
                    nc.gpsimd.indirect_dma_start(
                        chosen_rows.ap(), bass.IndirectOffsetOnAxis(ap=idx[:, slot, 1:2], axis=0),
                        y[:, slot % YR, :], None).then_inc(scattered[slot % YR], 16)

                def landed(i, r):
                    pool.wait_ge(scattered[r % YR], 16 * (XR // YR * i + r // YR) + 16)
                    pool.sem_inc(pool_turn, 1)

                for r in range(XR - 1):
                    gather(0, r)
                scatter(0, 0)
                gather(0, XR - 1)
                for r in range(1, XR):
                    scatter(0, r)
                    landed(0, r - 1)
                    gather(0, r + XR - 1)
                with pool.Fori(1, N // XR - 1) as i:
                    for r in range(XR):
                        scatter(i, r)
                        landed(i, r - 1)
                        gather(i, r + XR - 1)
                n = N // XR - 1
                for r in range(XR):
                    scatter(n, r)
                    landed(n, r - 1)
                    if r == 0:
                        gather(n, XR - 1)

            @block.tensor
            def _(pe):
                for c in (xt_done, gate_done, up_done, ht_done, y_mm):
                    pe.sem_inc(c, RING)

                def expert(i, r):
                    return pe.value_load(tile_exp[0:1, bass.ds(XR * i + r, 1)], min_val=0, max_val=EXPERTS - 1)

                def turn_x(i, r):
                    j, n, slot = XR * i + r, i + r // XR, r % XR
                    pe.wait_ge(gathered[slot], 16 * n + 16)
                    pe.wait_ge(x_lob_done, j + RING)
                    nc.tensor.transpose(ps_x[:, 0:P], xt[:, slot, 0:P], eye[:])
                    nc.tensor.transpose(ps_x[:, P:2 * P], xt[:, slot, P:GC], eye[:]).then_inc(xt_done, 1)

                def product(i, r, e, dst, col, read, done):
                    j, s = XR * i + r, r % RING
                    pe.wait_ge(x_lo_done, made(j))
                    pe.wait_ge(x_lob_done, made(j))
                    pe.wait_ge(read, freed(j))
                    at = dst[:, s, 0:HID]
                    w = bass.ds(col, HID)
                    hb = x_hi[:, s, P:2 * P]
                    nc.tensor.matmul(at, x_hi[:, s, 0:P], wa_hi[:, e, w], start=True, stop=False)
                    nc.tensor.matmul(at, x_hi[:, s, 0:P], wa_lo[:, e, w], start=False, stop=False)
                    nc.tensor.matmul(at, x_lo[:, s, :], wa_hi[:, e, w], start=False, stop=False)
                    nc.tensor.matmul(at, hb, wb_hi[:, e, w], start=False, stop=False)
                    nc.tensor.matmul(at, hb[0:CB, :], wb_lo[:, e, w], start=False, stop=True).then_inc(done, 1)

                def turn_h(i, r):
                    j, s = XR * i + r, r % RING
                    pe.wait_ge(hid_done, made(j))
                    pe.wait_ge(h_lo_done, j + RING)
                    for k in range(3):
                        ins = nc.tensor.transpose(ps_h[:, bass.ts(k, P)], hid[:, s, bass.ts(k, P)], eye[:])
                    ins.then_inc(ht_done, 1)

                def down_product(i, r, e):
                    j, s = XR * i + r, r % RING
                    pe.wait_ge(h_lo_done, made(j))
                    pe.wait_ge(y_done, freed(j))
                    at = ps_y[:, s, 0:C]
                    for k in range(3):
                        hi, lo = h_hi[:, s, bass.ts(k, P)], h_lo[:, s, bass.ts(k, P)]
                        w = bass.ts(k, C)
                        nc.tensor.matmul(at, hi, wd_hi[:, e, w], start=(k == 0), stop=False)
                        nc.tensor.matmul(at, hi, wd_lo[:, e, w], start=False, stop=False)
                        ins = nc.tensor.matmul(at, lo, wd_hi[:, e, w], start=False, stop=(k == 2))
                    ins.then_inc(y_mm, 1)

                def gate_product(i, r, e):
                    product(i, r, e, ps_g, 0, silu_done, gate_done)

                def up_product(i, r, e):
                    product(i, r, e, ps_u, HID, hid_done, up_done)

                def step(i, r, more=True):
                    e = expert(i, r)
                    gate_product(i, r, e)
                    turn_h(i, r - 1)
                    if more:
                        turn_x(i, r + 1)
                    up_product(i, r, e)
                    down_product(i, r - 1, expert(i, r - 1))

                turn_x(0, 0)
                e = expert(0, 0)
                gate_product(0, 0, e)
                turn_x(0, 1)
                up_product(0, 0, e)
                with pe.Fori(0, N // XR - 1) as i:
                    for r in range(1, XR + 1):
                        step(i, r)
                n = N // XR - 1
                for r in range(1, XR):
                    step(n, r, r < XR - 1)
                turn_h(n, XR - 1)
                down_product(n, XR - 1, expert(n, XR - 1))

            @block.scalar
            def _(act):
                for c in (x_hi_done, silu_done, h_hi_done, y_done):
                    act.sem_inc(c, RING)

                def x_high(i, r):
                    j, s = XR * i + r, r % RING
                    act.wait_ge(xt_done, made(j))
                    act.wait_ge(up_done, freed(j))
                    nc.scalar.activation(x_hi[:, s, :], ps_x[:, 0:2 * P], ACT.Copy).then_inc(x_hi_done, 1)

                def silu(i, r):
                    j, s = XR * i + r, r % RING
                    act.wait_ge(gate_done, made(j))
                    act.wait_ge(hid_done, freed(j))
                    nc.scalar.activation(sg[:, s, :], ps_g[:, s, 0:HID], ACT.Silu).then_inc(silu_done, 1)

                def h_high(i, r):
                    j, s = XR * i + r, r % RING
                    act.wait_ge(ht_done, made(j))
                    act.wait_ge(y_mm, freed(j))
                    nc.scalar.activation(h_hi[:, s, :], ps_h[:, 0:HID], ACT.Copy).then_inc(h_hi_done, 1)

                def weigh(i, r):
                    j, slot, s = XR * i + r, r % XR, r % RING
                    e = act.value_load(tile_exp[0:1, bass.ds(j, 1)], min_val=0, max_val=EXPERTS - 1)
                    act.wait_ge(y_mm, made(j))
                    nc.scalar.activation(y[:, r % YR, :], ps_y[:, s, 0:C], ACT.Copy,
                                         scale=xt[:, slot, bass.ds(GC + e, 1)]).then_inc(y_done, 1)

                def y_free(i, r):
                    act.wait_ge(scattered[r % YR], 16 * (XR // YR * i + r // YR))

                x_high(0, 0)
                x_high(0, 1)
                silu(0, 0)
                for r in range(1, XR + 1):
                    h_high(0, r - 1)
                    x_high(0, r + 1)
                    silu(0, r)
                    if r > YR:
                        y_free(0, r - 1)
                    weigh(0, r - 1)
                with act.Fori(1, N // XR - 1) as i:
                    for r in range(1, XR + 1):
                        h_high(i, r - 1)
                        x_high(i, r + 1)
                        silu(i, r)
                        y_free(i, r - 1)
                        weigh(i, r - 1)
                n = N // XR - 1
                for r in range(1, XR + 1):
                    h_high(n, r - 1)
                    if r + 1 < XR:
                        x_high(n, r + 1)
                    if r < XR:
                        silu(n, r)
                    y_free(n, r - 1)
                    weigh(n, r - 1)

            @block.vector
            def _(dve):
                for c in (x_lo_done, x_lob_done, hid_done, h_lo_done):
                    dve.sem_inc(c, RING)

                def x_low(i, r):
                    j, s = XR * i + r, r % RING
                    dve.wait_ge(x_hi_done, made(j))
                    dve.wait_ge(up_done, freed(j))
                    nc.vector.tensor_tensor(x_lo[:, s, :], ps_x[:, 0:P], x_hi[:, s, 0:P].bitcast(F32),
                                            ALU.subtract).then_inc(x_lo_done, 1)
                    b = x_hi[CB:P, s, P:2 * P]
                    nc.vector.tensor_tensor(b, ps_x[CB:P, P:2 * P], b.bitcast(F32), ALU.subtract).then_inc(x_lob_done, 1)

                def hidden(i, r):
                    j, s = XR * i + r, r % RING
                    dve.wait_ge(silu_done, made(j))
                    dve.wait_ge(up_done, made(j))
                    dve.wait_ge(ht_done, freed(j))
                    nc.vector.tensor_tensor(hid[:, s, :], ps_u[:, s, 0:HID], sg[:, s, :], ALU.mult).then_inc(hid_done, 1)

                def h_low(i, r):
                    j, s = XR * i + r, r % RING
                    dve.wait_ge(h_hi_done, made(j))
                    dve.wait_ge(y_mm, freed(j))
                    nc.vector.tensor_tensor(h_lo[:, s, :], ps_h[:, 0:HID], h_hi[:, s, :].bitcast(F32),
                                            ALU.subtract).then_inc(h_lo_done, 1)

                x_low(0, 0)
                x_low(0, 1)
                hidden(0, 0)
                with dve.Fori(0, N // XR - 1) as i:
                    for r in range(1, XR + 1):
                        h_low(i, r - 1)
                        x_low(i, r + 1)
                        hidden(i, r)
                n = N // XR - 1
                for r in range(1, XR):
                    h_low(n, r - 1)
                    if r + 1 < XR:
                        x_low(n, r + 1)
                    hidden(n, r)
                h_low(n, XR - 1)

                with dve.Fori(0, QUADS // RING) as i:
                    for s in range(RING):
                        q = quad(i, s)
                        dve.wait_ge(picked[s], 32 * i + 32)
                        nc.vector.tensor_tensor(pick[:, s, 0], pick[:, s, 0], pick[:, s, 1],
                                                ALU.add).then_inc(sum_done, 1)
                        dve.wait_ge(sum_done, q + 1)
                        at = xs[:, bass.ts(q, QT), :]
                        nc.vector.tensor_tensor(at, at, pick[:, s, 0], ALU.add).then_inc(total_done, 1)

            @block.sync
            def _(sp):
                out_tiles = out.rearrange("(t p) c -> p t c", p=P)
                picks = chosen_rows[0:2 * TOKENS, :].rearrange("(k t p) c -> k p t c", k=2, p=P)
                for r in range(YR):
                    sp.wait_ge(scattered[r], 16 * N // YR)

                def load(i, s):
                    q = quad(i, s)
                    for k in range(2):
                        sp.dma_start(pick[:, s, k], picks[k, :, bass.ts(q, QT), :]).then_inc(picked[s], 16)

                def store(i, s):
                    q = quad(i, s)
                    sp.wait_ge(total_done, q + 1)
                    sp.dma_start(out_tiles[:, bass.ts(q, QT), :], xs[:, bass.ts(q, QT), :]).then_inc(out_stored[s], 16)

                load(0, 0)
                load(0, 1)
                with sp.Fori(1, QUADS // RING) as i:
                    for s in range(RING):
                        store(i - 1, s)
                        load(i, s)
                for s in range(RING):
                    store(QUADS // RING - 1, s)
                for s in range(RING):
                    sp.wait_ge(out_stored[s], 16 * QUADS // RING)


def kernel(**inputs):
    import numpy as np
    import concourse.bacc as bacc
    from concourse import mybir as mb
    from concourse.bass_utils import run_bass_kernel_spmd as run

    f = np.float32
    get = {k: np.asarray(v) for k, v in inputs.items()}
    x = get["x"].reshape(TOKENS, C)

    line = int((SIDE * SIDE * 0.25) ** 0.5 // 2)
    mask = np.zeros((SIDE, SIDE))
    mask[SIDE // 2 - line:SIDE // 2 + line, SIDE // 2 - line:SIDE // 2 + line] = 1.0
    unit = np.eye(SEQ).reshape(SEQ, SIDE, SIDE)
    spec = np.fft.fftshift(np.fft.fft2(unit, norm="forward"), axes=(-2, -1)) * mask
    low = np.fft.ifft2(np.fft.ifftshift(spec, axes=(-2, -1)), norm="forward").real.reshape(SEQ, SEQ)
    inv = (1.0 / 10000.0 ** (np.arange(0, HD, 2, dtype=f) / f(HD))).astype(f)
    ang = np.arange(SEQ, dtype=f)[:, None] * inv[None, :]
    cos, sin = np.cos(ang).astype(f), np.sin(ang).astype(f)
    rep = lambda v: np.ascontiguousarray(np.broadcast_to(v.astype(f).reshape(1, -1), (P, v.size)))
    p = np.arange(P)
    token = (p[:, None] + P * np.arange(TILES)[None, :] + 1).astype(f)
    iotas = [
        rep(np.arange(MAPW)),
        rep(np.tile(EXPERTS - np.arange(EXPERTS), TILES)),
        rep(np.tile(TOKENS * np.arange(EXPERTS), TILES)),
        rep(np.tile((np.arange(TILES) > 0), EXPERTS)),
        np.stack([token, -token], 1),
        rep(P * np.arange(SLOTS)),
        np.stack([TOKENS + 1 + p, TOKENS + p, 2 * TOKENS + P * EXPERTS + p,
                  TOKENS + p, 2 * TOKENS + P * (EXPERTS + 1) + p], 1).astype(f),
        rep(MAPW + np.arange(TILES_MAX) % 2),
    ]
    ytab = np.zeros((P, 1), f)
    ytab[[DH, DP + DH]] = 1.0

    rows = lambda *v: np.ascontiguousarray(np.concatenate(v, 0))
    wk, bk = get["L1_attn_Wk"], get["L1_attn_bk"]
    wqkv = rows(np.concatenate([get["L1_attn_Wq"], wk, wk, get["L1_attn_Wv"]], 1),
                np.concatenate([get["L1_attn_bq"], bk, bk, get["L1_attn_bv"]])[None, :])
    arrays = {
        "x": np.ascontiguousarray(x),
        "xT": np.ascontiguousarray(x.T),
        "w1": rows(get["L0_conv_W1"].T, get["L0_conv_b1"][None, :]),
        "w2": rows(get["L0_conv_W2"].T, get["L0_conv_b2"][None, :]),
        "lowpass": low.astype(f),
        "wqkv": wqkv,
        "cos": np.concatenate([cos, cos, cos], 1),
        "sin": np.concatenate([-sin, sin, -sin], 1),
        "gate": np.ascontiguousarray(get["L1_ffn_gate_w"].T),
        "wgu": np.ascontiguousarray(np.concatenate([get["L1_ffn_gate_bank"], get["L1_ffn_up_bank"]], 2).transpose(1, 0, 2)),
        "down": np.ascontiguousarray(get["L1_ffn_down_bank"]),
        "tri": np.triu(np.ones((P, P), f), 1),
        "ident": np.eye(P, dtype=f),
        **{f"iota{k}": v for k, v in enumerate(iotas)},
        "ytab": ytab,
    }
    nc = bacc.Bacc("TRN2", target_bir_lowering=False, num_devices=1)
    ap = {k: nc.dram_tensor(f"in_{k}", v.shape, mb.dt.from_np(v.dtype), kind="ExternalInput").ap()
          for k, v in arrays.items()}
    out = nc.dram_tensor("out_0", (TOKENS, C), mb.dt.float32, kind="ExternalOutput").ap()
    tables = [ap.pop(f"iota{k}") for k in range(len(iotas))]
    program(nc, **ap, iotas=tables, out=out)
    r = run(nc, [{f"in_{k}": v for k, v in arrays.items()}], core_ids=[0])
    return r.results[0]["out_0"].reshape(get["x"].shape)
```

```python
from contextlib import ExitStack

import concourse.bass as bass
from concourse import mybir

F32 = mybir.dt.float32
F32R = mybir.dt.float32r
I32 = mybir.dt.int32
U32 = mybir.dt.uint32
ALU = mybir.AluOpType
ACT = mybir.ActivationFunctionType
AX = mybir.AxisListType

P = 128
IMAGES, SIDE, C = 16, 16, 192
SEQ = SIDE * SIDE
TOKENS = IMAGES * SEQ
DH = 48
DP = 64
CB = C - P
HEADS, HD = 12, 16
QW = C + 3 * HD
KC, VC = C, C + 2 * HD
EXPERTS, HID = 8, 384
TILES = TOKENS // P
QT = 4
QUADS = TILES // QT
RING = 2
XR = 8
AHEAD = XR - 2
YR = 4
PADS = 4
TILES_MAX = -(-(2 * TOKENS // P + EXPERTS - 1) // XR) * XR
GC = C + CB
ROW = GC + 8
EPS = 1e-5
SCALE = HD ** -0.5


def quad(i, s):
    return RING * i + s


def made(n):
    return n + 1 + RING


def freed(n):
    return n + 1


def bcast(ap, axis, n):
    v = ap.unsqueeze(axis)
    shape = list(v.shape)
    shape[axis] = n
    return v.broadcast_to(shape)


def program(nc, x, xT, w1, w2, lowpass, wqkv, cos, sin, gate, wgu, down, tri, ident, iotas, ytab, out):
    chosen_rows = nc.dram_tensor("chosen_rows", [2 * TOKENS + PADS * P, C], F32)
    rows = nc.dram_tensor("rows", [TOKENS + P, ROW], F32)
    x_tiles = x.rearrange("(t p) c -> p t c", p=P)
    row_tiles = rows[0:TOKENS, :].rearrange("(t p) c -> p t c", p=P)

    with ExitStack() as whole:
        def keep(name, shape, dt=F32):
            return whole.enter_context(nc.sbuf_tensor(name, shape, dt))

        wa_hi = keep("wa_hi", [P, EXPERTS, 2 * HID], F32R)
        wa_lo = keep("wa_lo", [P, EXPERTS, 2 * HID], F32R)
        wb_hi = keep("wb_hi", [P, EXPERTS, 2 * HID], F32R)
        wb_lo = keep("wb_lo", [CB, EXPERTS, 2 * HID], F32R)
        wd_hi = keep("wd_hi", [P, EXPERTS, 3 * C], F32R)
        wd_lo = keep("wd_lo", [P, EXPERTS, 3 * C], F32R)
        eye = keep("eye", [P, P])
        idx_map = keep("idx_map", [P, TILES_MAX, 2], I32)
        tile_exp = keep("tile_exp", [P, TILES_MAX], I32)

        xs = keep("xs", [P, TILES, C])
        mean, rstd = keep("mean", [P, TILES]), keep("rstd", [P, TILES])

        conv_phase(nc, xs, mean, rstd, x_tiles, xT, w1, w2, lowpass, wgu, wa_hi, wa_lo, ytab, eye, ident)
        attention_phase(nc, xs, mean, rstd, eye, wqkv, cos, sin, rows, wgu, wb_hi, wb_lo)
        routing_phase(nc, xs, mean, rstd, eye, gate, tri, iotas, row_tiles, down, wd_hi, wd_lo,
                      idx_map, tile_exp)
        expert_phase(nc, xs, eye, rows, chosen_rows, out, wa_hi, wa_lo, wb_hi, wb_lo, wd_hi, wd_lo, idx_map, tile_exp)


class Scope:

    def __init__(self, nc, stack, phase):
        self.nc, self.stack, self.phase = nc, stack, phase

    def sb(self, name, shape, dt=F32):
        return self.stack.enter_context(self.nc.sbuf_tensor(f"{self.phase}_{name}", shape, dt))

    def ps(self, name, shape):
        return self.stack.enter_context(self.nc.psum_tensor(f"{self.phase}_{name}", shape, F32))

    def sem(self, name):
        return self.stack.enter_context(self.nc.semaphore(f"{self.phase}_{name}"))


def conv_phase(nc, xs, mean, rstd, x_tiles, xT, w1, w2, lowpass, wgu, wa_hi, wa_lo, ytab, eye, ident):
    with ExitStack() as stack:
        a = Scope(nc, stack, "conv")
        w1a, w1b = a.sb("w1a", [P, DH]), a.sb("w1b", [CB + 1, DH])
        w2s = a.sb("w2s", [P, C])
        lp = a.sb("lp", [P, 2, SEQ])
        y_bias = a.sb("y_bias", [P, 1])
        xta, xtb = a.sb("xta", [P, RING, QT * P]), a.sb("xtb", [CB + 1, RING, QT * P])
        g = a.sb("g", [P, RING, 2, 2, DP])
        yt = a.sb("yt", [P, RING, SEQ])
        stage = a.sb("stage", [P, RING, 2 * HID])
        stats, mv = a.sb("stats", [P, RING, QT, 6]), a.sb("mv", [P, RING, QT, 2])
        vtmp, half = a.sb("vtmp", [P, RING, QT]), a.sb("half", [P, 1])
        ps_w1, ps_f = a.ps("ps_w1", [P, RING, 512]), a.ps("ps_f", [P, RING, 512])
        ps_c = a.ps("ps_c", [P, RING, 2, 512])

        consts_in = a.sem("consts_in")
        xt_in = [a.sem(f"xt_in{s}") for s in range(RING)]
        x_in = [a.sem(f"x_in{s}") for s in range(4)]
        stage_in = [a.sem(f"stage_in{s}") for s in range(RING)]
        filled = a.sem("filled")
        bias_row = a.sem("bias_row")
        w1_done, fft_done, w2_done = a.sem("w1_done"), a.sem("fft_done"), a.sem("w2_done")
        gelu_done, abs_done, hi_done = a.sem("gelu_done"), a.sem("abs_done"), a.sem("hi_done")
        added, stats_done, mv_done = a.sem("added"), a.sem("stats_done"), a.sem("mv_done")
        lo_done, eps_done, pow_done = a.sem("lo_done"), a.sem("eps_done"), a.sem("pow_done")
        mean_done = a.sem("mean_done")
        pool_turn, dve_turn = a.sem("pool_turn"), a.sem("dve_turn")

        with nc.Block() as block:
            @block.sync
            def _(sp):
                sp.dma_start(w1a[:], w1[0:P, :]).then_inc(consts_in, 16)
                sp.dma_start(w1b[:], w1[P:C + 1, :]).then_inc(consts_in, 16)

                def load(i, s):
                    q = quad(i, s)
                    sp.wait_ge(w1_done, freed(q))
                    sp.dma_start(xta[:, s, :], xT[0:P, bass.ts(q, QT * P)]).then_inc(xt_in[s], 16)
                    sp.dma_start(xtb[0:CB, s, :], xT[P:C, bass.ts(q, QT * P)]).then_inc(xt_in[s], 16)

                def load_weights(i, s):
                    q = quad(i, s)
                    sp.wait_ge(lo_done, freed(q))
                    sp.dma_start(stage[:, s], wgu[0:P, q, :]).then_inc(stage_in[s], 16)

                load(0, 0)
                sp.dma_start(lp[:], lowpass.rearrange("(h p) s -> p h s", p=P)).then_inc(consts_in, 16)
                sp.dma_start(w2s[0:DH + 1, :], w2).then_inc(consts_in, 16)
                sp.dma_start(w2s[DP:DP + DH + 1, :], w2).then_inc(consts_in, 16)
                sp.dma_start(y_bias[:], ytab).then_inc(consts_in, 16)
                sp.dma_start(eye[:], ident).then_inc(consts_in, 16)
                load(0, 1)
                for k, x_part in enumerate(x_in):
                    part = slice(k * TILES // 4, (k + 1) * TILES // 4)
                    sp.dma_start(xs[:, part, :], x_tiles[:, part, :]).then_inc(x_part, 16)
                load_weights(0, 0)
                load_weights(0, 1)
                with sp.Fori(1, QUADS // RING) as i:
                    for s in range(RING):
                        load(i, s)
                        load_weights(i, s)

            @block.tensor
            def _(pe):
                pe.sem_inc(w1_done, RING)
                pe.sem_inc(fft_done, RING)
                pe.sem_inc(w2_done, RING)
                pe.wait_ge(consts_in, 7 * 16)
                pe.wait_ge(filled, 2)
                pe.wait_ge(bias_row, 1)

                def in_product(i, s):
                    q = quad(i, s)
                    pe.wait_ge(xt_in[s], 32 * i + 32)
                    pe.wait_ge(gelu_done, freed(q))
                    for t in range(QT):
                        at = ps_w1[:, s, t * DH:(t + 1) * DH]
                        nc.tensor.matmul(at, xta[:, s, bass.ts(t, P)], w1a[:], start=True, stop=False)
                        last = nc.tensor.matmul(at, xtb[:, s, bass.ts(t, P)], w1b[:], start=False, stop=True)
                    last.then_inc(w1_done, 1)

                def lowpass_product(i, s):
                    q = quad(i, s)
                    pe.wait_ge(gelu_done, made(q))
                    pe.wait_ge(abs_done, freed(q))
                    for h in range(2):
                        last = nc.tensor.matmul(ps_f[:, s, 0:SEQ], g[:, s, h].rearrange("p m d -> p (m d)"),
                                                lp[:, h, :], start=(h == 0), stop=(h == 1))
                    last.then_inc(fft_done, 1)

                def out_product(i, s):
                    q = quad(i, s)
                    pe.wait_ge(abs_done, made(q))
                    pe.wait_ge(added, freed(q))
                    for m in range(2):
                        k = slice(DP * m, DP * m + DH + 1)
                        for h in range(2):
                            last = nc.tensor.matmul(ps_c[:, s, m, h * C:(h + 1) * C], yt[k, s, bass.ts(h, P)],
                                                    w2s[k, :], start=True, stop=True)
                    last.then_inc(w2_done, 1)

                in_product(0, 0)
                in_product(0, 1)
                lowpass_product(0, 0)
                with pe.Fori(1, QUADS // RING) as i:
                    in_product(i, 0)
                    lowpass_product(i - 1, 1)
                    out_product(i - 1, 0)
                    in_product(i, 1)
                    lowpass_product(i, 0)
                    out_product(i - 1, 1)
                last = QUADS // RING - 1
                lowpass_product(last, 1)
                out_product(last, 0)
                out_product(last, 1)

            @block.scalar
            def _(act):
                act.sem_inc(gelu_done, RING)
                act.sem_inc(abs_done, RING)
                act.sem_inc(hi_done, RING)
                act.wait_ge(consts_in, 7 * 16)
                act.wait_ge(filled, 2)

                def gelu(i, s):
                    q = quad(i, s)
                    act.wait_ge(w1_done, made(q))
                    act.wait_ge(fft_done, freed(q))
                    nc.scalar.activation(g[:, s].rearrange("p h m d -> p m h d")[:, :, :, 0:DH],
                                         ps_w1[:, s, 0:QT * DH].rearrange("p (m h d) -> p m h d", m=2, h=2),
                                         ACT.Gelu).then_inc(gelu_done, 1)

                def magnitude(i, s):
                    q = quad(i, s)
                    act.wait_ge(fft_done, made(q))
                    act.wait_ge(w2_done, freed(q))
                    nc.scalar.activation(yt[:, s, :], ps_f[:, s, 0:SEQ], ACT.Abs,
                                         bias=y_bias[:, 0:1]).then_inc(abs_done, 1)

                def split(i, s):
                    act.wait_ge(stage_in[s], 16 * i + 16)
                    nc.scalar.activation(wa_hi[:, quad(i, s), :], stage[:, s], ACT.Copy).then_inc(hi_done, 1)

                gelu(0, 0)
                gelu(0, 1)
                magnitude(0, 0)
                split(0, 0)
                with act.Fori(1, QUADS // RING) as i:
                    gelu(i, 0)
                    magnitude(i - 1, 1)
                    split(i - 1, 1)
                    gelu(i, 1)
                    magnitude(i, 0)
                    split(i, 0)
                last = QUADS // RING - 1
                magnitude(last, 1)
                split(last, 1)

            @block.gpsimd
            def _(pool):
                pool.sem_inc(lo_done, RING)
                pool.sem_inc(pow_done, RING)
                pool.sem_inc(eps_done, RING)
                pool.sem_inc(mean_done, RING)
                nc.gpsimd.memset(g[:], 0.0).then_inc(filled, 1)
                nc.gpsimd.memset(half[:], -0.5).then_inc(filled, 1)
                pool.wait_ge(filled, 2)

                def split(i, s):
                    q = quad(i, s)
                    pool.wait_ge(hi_done, made(q))
                    pool.sem_inc(pool_turn, 1)
                    nc.gpsimd.tensor_tensor(wa_lo[:, q, :], stage[:, s], wa_hi[:, q, :].bitcast(F32),
                                            ALU.subtract).then_inc(lo_done, 1)

                def deviation(i, s):
                    row_deviation(nc, pool, quad(i, s), s, mv, vtmp, half, mean, rstd, mv_done, eps_done,
                                  pow_done, mean_done, pool_turn)

                split(0, 0)
                with pool.Fori(1, QUADS // RING) as i:
                    split(i - 1, 1)
                    deviation(i - 1, 0)
                    split(i, 0)
                    deviation(i - 1, 1)
                last = QUADS // RING - 1
                split(last, 1)
                deviation(last, 0)
                deviation(last, 1)

            @block.vector
            def _(dve):
                nc.vector.memset(xtb[CB:CB + 1, :, :], 1.0).then_inc(bias_row, 1)
                dve.sem_inc(added, RING)
                dve.sem_inc(stats_done, RING)
                dve.sem_inc(mv_done, RING)

                def finish(i, s):
                    q = quad(i, s)
                    dve.wait_ge(w2_done, made(q))
                    for m in range(2):
                        at = xs[:, bass.ts(2 * q + m, 2), :]
                        ins = nc.vector.tensor_tensor(
                            at, ps_c[:, s, m, 0:2 * C].rearrange("p (h c) -> p h c", h=2), at, ALU.add)
                    ins.then_inc(added, 1)
                    row_statistics(nc, dve, q, s, xs, stats, mv, added, stats_done, mv_done, pow_done, mean_done, dve_turn)

                for x_part in x_in:
                    dve.wait_ge(x_part, 16)
                with dve.Fori(0, QUADS // RING) as i:
                    for s in range(RING):
                        finish(i, s)


def row_statistics(nc, dve, q, s, xs, stats, mv, written, stats_done, mv_done, pow_done, mean_done, dve_turn):
    dve.wait_ge(written, made(q))
    dve.sem_inc(dve_turn, 1)
    for t in range(QT):
        ins = nc.vector.bn_stats(stats[:, s, t, :], xs[:, QT * q + t, :])
    ins.then_inc(stats_done, 1)
    dve.wait_ge(stats_done, made(q))
    dve.wait_ge(pow_done, freed(q))
    dve.wait_ge(mean_done, freed(q))
    dve.sem_inc(dve_turn, 1)
    for t in range(QT):
        ins = nc.vector.bn_aggr(mv[:, s, t, :], stats[:, s, t, :])
    ins.then_inc(mv_done, 1)


def row_deviation(nc, pool, q, s, mv, vtmp, half, mean, rstd, mv_done, eps_done, pow_done, mean_done, pool_turn):
    pool.wait_ge(mv_done, made(q))
    pool.sem_inc(pool_turn, 1)
    nc.gpsimd.tensor_scalar(vtmp[:, s, :], mv[:, s, :, 1], EPS, None, ALU.add).then_inc(eps_done, 1)
    nc.gpsimd.tensor_copy(mean[:, bass.ts(q, QT)], mv[:, s, :, 0]).then_inc(mean_done, 1)
    pool.wait_ge(eps_done, made(q))
    pool.sem_inc(pool_turn, 1)
    nc.gpsimd.tensor_tensor(rstd[:, bass.ts(q, QT)], vtmp[:, s, :], half[:, 0:1].broadcast_to([P, QT]),
                            ALU.pow).then_inc(pow_done, 1)


def normalise(nc, dve, q, s, xs, mean, rstd, xn, tr_done, xn_done):
    dve.wait_ge(tr_done, freed(q))
    for t in range(QT):
        at = QT * q + t
        ins = nc.vector.tensor_scalar(xn[:, s, t, :], xs[:, at, :], mean[:, bass.ds(at, 1)],
                                      rstd[:, bass.ds(at, 1)], ALU.subtract, ALU.mult)
    ins.then_inc(xn_done, 1)


def transposes(nc, pe, q, s, xn, eye, ps_a, ps_b, xn_done, ev_done, tr_done):
    pe.wait_ge(xn_done, made(q))
    pe.wait_ge(ev_done, freed(q))
    for t in range(QT):
        nc.tensor.transpose(ps_a[:, s, bass.ts(t, P)], xn[:, s, t, 0:P], eye[:])
        ins = nc.tensor.transpose(ps_b[0:CB, s, bass.ts(t, P)], xn[:, s, t, P:C], eye[:])
    ins.then_inc(tr_done, 1)


def evacuate(nc, act, q, s, ps_a, ps_b, xa, xb, tr_done, used, ev_done):
    act.wait_ge(tr_done, made(q))
    act.wait_ge(used, freed(q))
    nc.scalar.activation(xa[:, s, :], ps_a[:, s, :], ACT.Copy)
    nc.scalar.activation(xb[0:CB, s, :], ps_b[0:CB, s, :], ACT.Copy).then_inc(ev_done, 1)


def attention_phase(nc, xs, mean, rstd, eye, wqkv, cos, sin, rows, wgu, wb_hi, wb_lo):
    with ExitStack() as stack:
        a = Scope(nc, stack, "attn")
        wqa, wqb = a.sb("wqa", [P, QW]), a.sb("wqb", [CB + 1, QW])
        cos_t, sin_t = a.sb("cos_t", [P, QT, 24]), a.sb("sin_t", [P, QT, 24])
        xn = a.sb("xn", [P, RING, QT, C])
        xa, xb = a.sb("xa", [P, RING, QT * P]), a.sb("xb", [CB + 1, RING, QT * P])
        qkv = a.sb("qkv", [P, RING, QT, QW])
        ka, kb, kr = a.sb("ka", [P, QT, 24]), a.sb("kb", [P, QT, 24]), a.sb("kr", [P, QT, 24])
        kc, kd, kk = a.sb("kc", [P, QT, HD]), a.sb("kd", [P, QT, HD]), a.sb("kk", [P, RING, QT, HD])
        prod = a.sb("prod", [P, QT, HEADS, HD])
        pv = a.sb("pv", [P, RING, QT, HEADS, HD])
        score, diff = a.sb("score", [P, RING, QT * HEADS]), a.sb("diff", [P, RING, QT * HEADS])
        ex, den = a.sb("ex", [P, RING, QT * HEADS]), a.sb("den", [P, RING, QT * HEADS])
        rec, wt = a.sb("rec", [P, RING, QT * HEADS]), a.sb("wt", [P, RING, QT * HEADS])
        stage = a.sb("stage", [P, RING, 2 * HID])
        stats, mv = a.sb("stats", [P, RING, QT, 6]), a.sb("mv", [P, RING, QT, 2])
        vtmp, half = a.sb("vtmp", [P, RING, QT]), a.sb("half", [P, 1])
        zero = a.sb("zero", [P, ROW])
        ps_a, ps_b = a.ps("ps_a", [P, RING, 512]), a.ps("ps_b", [P, RING, 512])
        ps_q = a.ps("ps_q", [P, RING, 2, 512])

        consts_in, stored, filled, bias_row = a.sem("consts_in"), a.sem("stored"), a.sem("filled"), a.sem("bias_row")
        stage_in = [a.sem(f"stage_in{s}") for s in range(RING)]
        xn_done, tr_done, ev_done = a.sem("xn_done"), a.sem("tr_done"), a.sem("ev_done")
        qkv_done, cp_done, kk_done = a.sem("qkv_done"), a.sem("cp_done"), a.sem("kk_done")
        rope_step = a.sem("rope_step")
        prod_done, score_done, diff_done = a.sem("prod_done"), a.sem("score_done"), a.sem("diff_done")
        ex_done, den_done, rec_done, wt_done = a.sem("ex_done"), a.sem("den_done"), a.sem("rec_done"), a.sem("wt_done")
        pv_done, res_done = a.sem("pv_done"), a.sem("res_done")
        stats_done, mv_done = a.sem("stats_done"), a.sem("mv_done")
        lo_done, eps_done, pow_done, mean_done = a.sem("lo_done"), a.sem("eps_done"), a.sem("pow_done"), a.sem("mean_done")
        hi_done, pool_turn, dve_turn = a.sem("hi_done"), a.sem("pool_turn"), a.sem("dve_turn")
        last = QUADS // RING - 1

        with nc.Block() as block:
            @block.sync
            def _(sp):
                sp.dma_start(wqa[:], wqkv[0:P, :]).then_inc(consts_in, 16)
                sp.dma_start(wqb[:], wqkv[P:C + 1, :]).then_inc(consts_in, 16)
                for h in range(2):
                    sp.dma_start(cos_t[:, 2 * h:2 * h + 2, :], cos.rearrange("(h p) d -> p h d", p=P)).then_inc(consts_in, 16)
                    sp.dma_start(sin_t[:, 2 * h:2 * h + 2, :], sin.rearrange("(h p) d -> p h d", p=P)).then_inc(consts_in, 16)
                sp.wait_ge(filled, 2)
                sp.dma_start(rows[TOKENS:TOKENS + P, :], zero[:]).then_inc(stored, 16)

                def load_weights(i, s):
                    q = quad(i, s)
                    sp.wait_ge(lo_done, freed(q))
                    sp.dma_start(stage[0:CB, s], wgu[P:C, q, :]).then_inc(stage_in[s], 16)
                    sp.dma_start(stage[CB:P, s], wgu[P:C, q, :]).then_inc(stage_in[s], 16)

                load_weights(0, 0)
                load_weights(0, 1)
                with sp.Fori(1, QUADS // RING) as i:
                    for s in range(RING):
                        load_weights(i, s)
                sp.wait_ge(stored, 16)

            @block.tensor
            def _(pe):
                pe.sem_inc(tr_done, RING)
                pe.sem_inc(qkv_done, RING)
                pe.wait_ge(consts_in, 6 * 16)
                pe.wait_ge(bias_row, 1)

                def turn(i, s):
                    transposes(nc, pe, quad(i, s), s, xn, eye, ps_a, ps_b, xn_done, ev_done, tr_done)

                def project(i, s):
                    q = quad(i, s)
                    pe.wait_ge(ev_done, made(q))
                    pe.wait_ge(cp_done, freed(q))
                    for t in range(QT):
                        at = ps_q[:, s, t // 2, (t % 2) * QW:(t % 2 + 1) * QW]
                        nc.tensor.matmul(at, xa[:, s, bass.ts(t, P)], wqa[:], start=True, stop=False)
                        ins = nc.tensor.matmul(at, xb[:, s, bass.ts(t, P)], wqb[:], start=False, stop=True)
                    ins.then_inc(qkv_done, 1)

                turn(0, 0)
                with pe.Fori(0, last) as i:
                    project(i, 0)
                    turn(i, 1)
                    project(i, 1)
                    turn(i + 1, 0)
                project(last, 0)
                turn(last, 1)
                project(last, 1)

            @block.scalar
            def _(act):
                act.sem_inc(ev_done, RING)
                act.sem_inc(cp_done, RING)
                act.sem_inc(ex_done, RING)
                act.sem_inc(hi_done, RING)

                def out_of_psum(i, s):
                    evacuate(nc, act, quad(i, s), s, ps_a, ps_b, xa, xb, tr_done, qkv_done, ev_done)

                def copy_qkv(i, s):
                    q = quad(i, s)
                    act.wait_ge(qkv_done, made(q))
                    act.wait_ge(prod_done, freed(q))
                    act.wait_ge(pv_done, freed(q))
                    for h in range(2):
                        ins = nc.scalar.activation(qkv[:, s, 2 * h:2 * h + 2, :],
                                                   ps_q[:, s, h, 0:2 * QW].rearrange("p (t c) -> p t c", t=2), ACT.Copy)
                    ins.then_inc(cp_done, 1)

                def exponential(i, s):
                    q = quad(i, s)
                    act.wait_ge(diff_done, made(q))
                    nc.scalar.activation(ex[:, s], diff[:, s], ACT.Exp, scale=SCALE).then_inc(ex_done, 1)

                def split(i, s):
                    act.wait_ge(stage_in[s], 32 * i + 32)
                    nc.scalar.activation(wb_hi[:, quad(i, s), :], stage[:, s], ACT.Copy).then_inc(hi_done, 1)

                def quad_work(i, s, more):
                    copy_qkv(i, s)
                    if more:
                        out_of_psum(i + (s + 1) // RING, (s + 1) % RING)
                    split(i, s)
                    exponential(i, s)

                out_of_psum(0, 0)
                with act.Fori(0, last) as i:
                    quad_work(i, 0, True)
                    quad_work(i, 1, True)
                quad_work(last, 0, True)
                quad_work(last, 1, False)

            @block.gpsimd
            def _(pool):
                for c in (lo_done, pow_done, eps_done, mean_done, kk_done, pv_done):
                    pool.sem_inc(c, RING)
                nc.gpsimd.memset(zero[:], 0.0).then_inc(filled, 1)
                nc.gpsimd.memset(half[:], -0.5).then_inc(filled, 1)
                pool.wait_ge(filled, 2)
                pool.wait_ge(consts_in, 6 * 16)

                def rotate_key(i, s):
                    q = quad(i, s)
                    pool.wait_ge(cp_done, made(q))
                    pool.wait_ge(prod_done, freed(q))
                    pool.sem_inc(pool_turn, 1)
                    nc.gpsimd.tensor_tensor(ka[:], qkv[:, s, :, KC:KC + 24], cos_t[:], ALU.mult)
                    nc.gpsimd.tensor_tensor(kb[:], qkv[:, s, :, KC + 8:KC + 32], sin_t[:], ALU.mult).then_inc(rope_step, 1)
                    pool.wait_ge(rope_step, 3 * q + 1)
                    nc.gpsimd.tensor_tensor(kr[:], ka[:], kb[:], ALU.add).then_inc(rope_step, 1)
                    pool.wait_ge(rope_step, 3 * q + 2)
                    nc.gpsimd.tensor_tensor(kc[:], kr[:, :, 0:HD], cos_t[:, :, 0:HD], ALU.mult)
                    nc.gpsimd.tensor_tensor(kd[:], kr[:, :, 8:8 + HD], sin_t[:, :, 0:HD], ALU.mult).then_inc(rope_step, 1)
                    pool.wait_ge(rope_step, 3 * q + 3)
                    nc.gpsimd.tensor_tensor(kk[:, s], kc[:], kd[:], ALU.subtract).then_inc(kk_done, 1)

                def split(i, s):
                    q = quad(i, s)
                    pool.wait_ge(hi_done, made(q))
                    pool.sem_inc(pool_turn, 1)
                    nc.gpsimd.tensor_tensor(wb_lo[:, q, :], stage[0:CB, s], wb_hi[0:CB, q, :].bitcast(F32),
                                            ALU.subtract).then_inc(lo_done, 1)

                def weigh_value(i, s):
                    q = quad(i, s)
                    pool.wait_ge(wt_done, made(q))
                    pool.wait_ge(res_done, freed(q))
                    pool.sem_inc(pool_turn, 1)
                    w = wt[:, s].rearrange("p (t h) -> p t h", t=QT)
                    for h in range(2):
                        t = slice(2 * h, 2 * h + 2)
                        ins = nc.gpsimd.tensor_tensor(pv[:, s, t], bcast(w[:, t, :], 3, HD),
                                                      bcast(qkv[:, s, t, VC:VC + HD], 2, HEADS), ALU.mult)
                    ins.then_inc(pv_done, 1)

                def deviation(i, s):
                    row_deviation(nc, pool, quad(i, s), s, mv, vtmp, half, mean, rstd, mv_done, eps_done,
                                  pow_done, mean_done, pool_turn)

                rotate_key(0, 0)
                split(0, 0)
                weigh_value(0, 0)
                rotate_key(0, 1)
                split(0, 1)
                deviation(0, 0)
                weigh_value(0, 1)
                with pool.Fori(1, QUADS // RING) as i:
                    for s in range(RING):
                        rotate_key(i, s)
                        split(i, s)
                        deviation(i - 1 + s, 1 - s)
                        weigh_value(i, s)
                deviation(last, 1)

            @block.vector
            def _(dve):
                nc.vector.memset(xb[CB:CB + 1, :, :], 1.0).then_inc(bias_row, 1)
                for c in (xn_done, prod_done, score_done, diff_done, den_done, rec_done, wt_done, res_done,
                          stats_done, mv_done):
                    dve.sem_inc(c, RING)

                def norm(i, s):
                    normalise(nc, dve, quad(i, s), s, xs, mean, rstd, xn, tr_done, xn_done)

                def scores(i, s):
                    q = quad(i, s)
                    dve.wait_ge(kk_done, made(q))
                    for h in range(2):
                        t = slice(2 * h, 2 * h + 2)
                        ins = nc.vector.tensor_tensor(
                            prod[:, t], qkv[:, s, t, 0:C].rearrange("p t (h d) -> p t h d", h=HEADS),
                            bcast(kk[:, s, t, :], 2, HEADS), ALU.mult)
                    ins.then_inc(prod_done, 1)
                    dve.wait_ge(prod_done, made(q))
                    nc.vector.tensor_reduce(score[:, s], prod[:].rearrange("p t h d -> p (t h) d"), AX.X,
                                            ALU.add).then_inc(score_done, 1)
                    dve.wait_ge(score_done, made(q))
                    nc.vector.tensor_tensor(diff[:, s], score[:, s], score[:, s], ALU.subtract).then_inc(diff_done, 1)

                def weights(i, s):
                    q = quad(i, s)
                    dve.wait_ge(ex_done, made(q))
                    nc.vector.tensor_scalar(den[:, s], ex[:, s], float(HEADS), None, ALU.mult).then_inc(den_done, 1)
                    dve.wait_ge(den_done, made(q))
                    nc.vector.reciprocal(rec[:, s], den[:, s]).then_inc(rec_done, 1)
                    dve.wait_ge(rec_done, made(q))
                    dve.wait_ge(pv_done, freed(q))
                    nc.vector.tensor_tensor(wt[:, s], den[:, s], rec[:, s], ALU.mult).then_inc(wt_done, 1)

                def residual(i, s):
                    q = quad(i, s)
                    dve.wait_ge(pv_done, made(q))
                    at = xs[:, bass.ts(q, QT), :]
                    nc.vector.tensor_tensor(at, at, pv[:, s].rearrange("p t h d -> p t (h d)"),
                                            ALU.add).then_inc(res_done, 1)
                    row_statistics(nc, dve, q, s, xs, stats, mv, res_done, stats_done, mv_done, pow_done, mean_done, dve_turn)

                norm(0, 0)
                norm(0, 1)
                scores(0, 0)
                weights(0, 0)
                with dve.Fori(1, QUADS // RING) as i:
                    for s in range(RING):
                        norm(i, s)
                        scores(i - 1 + s, 1 - s)
                        residual(i - 1, s)
                        weights(i - 1 + s, 1 - s)
                scores(last, 1)
                residual(last, 0)
                weights(last, 1)
                residual(last, 1)


def routing_phase(nc, xs, mean, rstd, eye, gate, tri, iotas, row_tiles, down, wd_hi, wd_lo,
                  idx_map, tile_exp):
    E, T = EXPERTS, TILES
    with ExitStack() as stack:
        a = Scope(nc, stack, "route")
        ga, gb = a.sb("ga", [P, E]), a.sb("gb", [CB, E])
        trit = a.sb("trit", [P, P])
        ones = a.sb("ones", [P, P])
        io = a.sb("io", [P, P])
        desc = a.sb("desc", [P, T, E])
        first = a.sb("first", [P, E, T])
        idp = a.sb("idp", [P, 2, T])
        no_row = a.sb("no_row", [P, 1])
        no_place = a.sb("no_place", [P, TILES_MAX])
        xn = a.sb("xn", [P, RING, QT, C])
        xa, xb = a.sb("xa", [P, RING, QT * P]), a.sb("xb", [CB, RING, QT * P])
        stage = a.sb("stage", [P, RING, 3 * C])
        lg, pr, tmp, m1, m2, tmp2 = (a.sb(n, [P, T, E]) for n in ("lg", "pr", "tmp", "m1", "m2", "tmp2"))
        both, gates = a.sb("both", [P, T, E]), a.sb("gates", [P, T, E])
        base = lg
        tot, inc = a.sb("tot", [P, E, T]), a.sb("inc", [P, E, T])
        red = a.sb("red", [P, 12, T])
        pos, keyb = a.sb("pos", [P, 2, T]), a.sb("keyb", [P, 2, 2, T])
        posi, keyi = a.sb("posi", [P, 2, T], I32), a.sb("keyi", [P, 2, 2, T], I32)
        ce, cum, start = a.sb("ce", [P, E]), a.sb("cum", [P, E]), a.sb("start", [P, E])
        cei = a.sb("cei", [P, E], I32)
        ge = xa[:].rearrange("p s c -> p (s c)")[:, 0:TILES_MAX * E].rearrange("p (j e) -> p j e", e=E)
        e_j = a.sb("e_j", [P, TILES_MAX])
        slot_v, slot_t, slot_0, size = (a.sb(n, [P, TILES_MAX]) for n in ("slot_v", "slot_t", "slot_0", "size"))
        hot_b = a.sb("hot_b", [P, RING, 2, QT, P], F32R)
        hot_j = xn[:].rearrange("p a b c -> p (a b c)")[:, 0:RING * 2 * QT * TILES_MAX].rearrange(
            "p (s k t j) -> p s k t j", s=RING, k=2, t=QT)
        hot_a = a.sb("hot_a", [P, RING, 2, QT, TILES_MAX], F32R)
        ps_a, ps_b = a.ps("ps_a", [P, RING, 512]), a.ps("ps_b", [P, RING, 512])
        ps_g, ps_p = a.ps("ps_g", [P, 512]), a.ps("ps_p", [P, 512])
        ps_t, ps_m = a.ps("ps_t", [P, 512]), a.ps("ps_m", [P, 512])

        consts_in, gates_out = a.sem("consts_in"), a.sem("gates_out")
        rows_out = [a.sem(f"rows_out{s}") for s in range(RING)]
        stage_in = [a.sem(f"stage_in{s}") for s in range(RING)]
        filled, xn_done, tr_done, ev_done = a.sem("filled"), a.sem("xn_done"), a.sem("tr_done"), a.sem("ev_done")
        gate_done, diff_done, ex_done = a.sem("gate_done"), a.sem("diff_done"), a.sem("ex_done")
        hi_done, lo_done, pool_turn = a.sem("hi_done"), a.sem("lo_done"), a.sem("pool_turn")
        chain = a.sem("chain")
        chosen, counted = a.sem("chosen"), a.sem("counted")
        gates_done = a.sem("gates_done")
        hot_done, hot_a_done, map_done = a.sem("hot_done"), a.sem("hot_a_done"), a.sem("map_done")
        last = QUADS // RING - 1
        consts = [(ga, gate[0:P, :]), (gb, gate[P:C, :]), (trit, tri)] + [
            (dst, src) for dst, src in zip((io, desc, first, idp, no_row, no_place), iotas)]

        with nc.Block() as block:
            @block.sync
            def _(sp):
                for s in range(RING):
                    sp.sem_inc(rows_out[s], 32)
                for dst, src in consts:
                    sp.dma_start(dst[:], src).then_inc(consts_in, 16)

                def load_weights(i, s):
                    q = quad(i, s)
                    sp.wait_ge(lo_done, freed(q))
                    sp.dma_start(stage[:, s].rearrange("p (k c) -> p k c", k=3),
                                 down[q].rearrange("(k p) c -> p k c", p=P)).then_inc(stage_in[s], 16)

                def store(i, s):
                    q = quad(i, s)
                    sp.wait_ge(xn_done, made(q))
                    sp.dma_start(row_tiles[:, bass.ts(q, QT), 0:C], xn[:, s]).then_inc(rows_out[s], 16)
                    sp.dma_start(row_tiles[:, bass.ts(q, QT), C:GC], xn[:, s, :, P:C]).then_inc(rows_out[s], 16)

                with sp.Fori(0, QUADS // RING) as i:
                    for s in range(RING):
                        load_weights(i, s)
                        store(i, s)
                sp.wait_ge(gates_done, 1)
                sp.dma_start(row_tiles[:, :, GC:ROW], gates[:]).then_inc(gates_out, 16)
                for s in range(RING):
                    sp.wait_ge(rows_out[s], 32 * (QUADS // RING + 1))
                sp.wait_ge(gates_out, 16)

            @block.gpsimd
            def _(pool):
                pool.sem_inc(lo_done, RING)
                nc.gpsimd.memset(ones[:], 1.0).then_inc(filled, 1)

                def split(i, s):
                    q = quad(i, s)
                    pool.wait_ge(hi_done, made(q))
                    pool.sem_inc(pool_turn, 1)
                    nc.gpsimd.tensor_tensor(wd_lo[:, q, :], stage[:, s], wd_hi[:, q, :].bitcast(F32),
                                            ALU.subtract).then_inc(lo_done, 1)

                with pool.Fori(0, QUADS // RING) as i:
                    for s in range(RING):
                        split(i, s)

                def token_at(i, s):
                    q = quad(i, s)
                    pool.wait_ge(hot_done, q + 1)
                    pool.sem_inc(pool_turn, 1)
                    nc.gpsimd.tensor_tensor(hot_a[:, s], hot_j[:, s], bcast(idp[:, :, bass.ts(q, QT)], 3, TILES_MAX),
                                            ALU.mult).then_inc(hot_a_done, 1)

                with pool.Fori(0, QUADS // RING) as i:
                    for s in range(RING):
                        token_at(i, s)

            @block.scalar
            def _(act):
                act.sem_inc(ev_done, RING)
                act.sem_inc(hi_done, RING)

                with act.Fori(0, QUADS // RING) as i:
                    for s in range(RING):
                        q = quad(i, s)
                        evacuate(nc, act, q, s, ps_a, ps_b, xa, xb, tr_done, gate_done, ev_done)
                        act.wait_ge(stage_in[s], 16 * i + 16)
                        nc.scalar.activation(wd_hi[:, q, :], stage[:, s], ACT.Copy).then_inc(hi_done, 1)
                act.wait_ge(diff_done, 1)
                nc.scalar.activation(pr[:], lg[:], ACT.Exp).then_inc(ex_done, 1)

            @block.tensor
            def _(pe):
                pe.sem_inc(tr_done, RING)
                pe.sem_inc(gate_done, RING)
                pe.wait_ge(consts_in, 16 * len(consts))

                def turn(i, s):
                    transposes(nc, pe, quad(i, s), s, xn, eye, ps_a, ps_b, xn_done, ev_done, tr_done)

                def gate_product(i, s):
                    q = quad(i, s)
                    pe.wait_ge(ev_done, made(q))
                    for t in range(QT):
                        at = ps_g[:, bass.ds((QT * q + t) * E, E)]
                        nc.tensor.matmul(at, xa[:, s, bass.ts(t, P)], ga[:], start=True, stop=False)
                        ins = nc.tensor.matmul(at, xb[:, s, bass.ts(t, P)], gb[:], start=False, stop=True)
                    ins.then_inc(gate_done, 1)

                turn(0, 0)
                with pe.Fori(0, last) as i:
                    turn(i, 1)
                    gate_product(i, 0)
                    turn(i + 1, 0)
                    gate_product(i, 1)
                turn(last, 1)
                gate_product(last, 0)
                gate_product(last, 1)

                pe.wait_ge(chosen, 1)
                pe.wait_ge(filled, 1)
                flat = both[:].rearrange("p t e -> p (t e)")
                nc.tensor.matmul(ps_p[:, 0:T * E], trit[:], flat, start=True, stop=True)
                nc.tensor.matmul(ps_t[:, 0:T * E], ones[:], flat, start=True, stop=True).then_inc(counted, 1)

                def place(i, s, start=False, stop=False):
                    pe.wait_ge(hot_a_done, quad(i, s) + 1)
                    for k in range(2):
                        for t in range(QT):
                            ins = nc.tensor.matmul(ps_m[:, 0:TILES_MAX], hot_b[:, s, k, t, :], hot_a[:, s, k, t, :],
                                                   start=start and k + t == 0, stop=stop and k + t == QT)
                    ins.then_inc(map_done, 1)

                place(0, 0, start=True)
                place(0, 1)
                with pe.Fori(1, last) as i:
                    for s in range(RING):
                        place(i, s)
                place(last, 0)
                place(last, 1, stop=True)

            @block.vector
            def _(dve):
                dve.sem_inc(xn_done, RING)

                def norm(i, s):
                    dve.wait_ge(rows_out[s], 32 * i + 32)
                    normalise(nc, dve, quad(i, s), s, xs, mean, rstd, xn, tr_done, xn_done)

                with dve.Fori(0, QUADS // RING) as i:
                    for s in range(RING):
                        norm(i, s)

                count = [0]

                def then(ins):
                    ins.then_inc(chain, 1)
                    count[0] += 1
                    dve.wait_ge(chain, count[0])

                tt2, ts = nc.vector.tensor_tensor, nc.vector.tensor_scalar

                def reduce(dst, src, op):
                    then(nc.vector.tensor_reduce(dst, src, AX.X, op))

                def over(ap):
                    return bcast(ap, 2, E)

                mx, sm, rs, p1, f1, p2, f2, dn, rd, g1, g2 = (red[:, k, :] for k in range(11))
                dve.wait_ge(gate_done, QUADS + RING)
                dve.wait_ge(consts_in, 16 * len(consts))
                logits = ps_g[:, 0:T * E].rearrange("p (t e) -> p t e", e=E)
                reduce(mx, logits, ALU.max)
                tt2(lg[:], logits, over(mx), ALU.subtract).then_inc(diff_done, 1)
                dve.wait_ge(ex_done, 1)
                reduce(sm, pr[:], ALU.add)
                then(nc.vector.reciprocal(rs, sm))
                then(tt2(pr[:], pr[:], over(rs), ALU.mult))
                reduce(p1, pr[:], ALU.max)
                then(tt2(tmp[:], pr[:], over(p1), ALU.is_equal))
                then(tt2(tmp2[:], tmp[:], desc[:], ALU.mult))
                reduce(f1, tmp2[:], ALU.max)
                then(tt2(m1[:], desc[:], over(f1), ALU.is_equal))
                then(nc.vector.scalar_tensor_tensor(out=tmp[:], in0=m1[:], scalar=-2.0, in1=pr[:],
                                                    op0=ALU.mult, op1=ALU.add))
                reduce(p2, tmp[:], ALU.max)
                then(tt2(tmp2[:], tmp[:], over(p2), ALU.is_equal))
                then(tt2(tmp[:], tmp2[:], desc[:], ALU.mult))
                reduce(f2, tmp[:], ALU.max)
                then(tt2(m2[:], desc[:], over(f2), ALU.is_equal))
                tt2(both[:], m1[:], m2[:], ALU.add).then_inc(chosen, 1)
                then(tt2(dn, p1, p2, ALU.add))
                then(ts(dn, dn, 1e-8, None, ALU.add))
                then(nc.vector.reciprocal(rd, dn))
                tt2(g1, p1, rd, ALU.mult)
                then(tt2(g2, p2, rd, ALU.mult))
                tt2(tmp[:], m1[:], over(g1), ALU.mult)
                then(tt2(tmp2[:], m2[:], over(g2), ALU.mult))
                tt2(gates[:], tmp[:], tmp2[:], ALU.add).then_inc(gates_done, 1)
                dve.wait_ge(counted, 1)
                then(nc.vector.tensor_copy(tot[:], ps_t[:, 0:T * E].rearrange("p (t e) -> p e t", e=E)))
                flat = "p e t -> p (e t)"
                then(nc.vector.tensor_tensor_scan(inc[:].rearrange(flat), first[:].rearrange(flat),
                                                  tot[:].rearrange(flat), 0.0, ALU.mult, ALU.add))
                then(ts(ce[:], inc[:, :, T - 1], float(P - 1), None, ALU.add))
                tt2(tot[:], inc[:], tot[:], ALU.subtract)
                then(nc.vector.tensor_copy(cei[:], ce[:]))
                then(ts(cei[:], cei[:], 7, None, ALU.arith_shift_right))
                then(nc.vector.tensor_copy(ce[:], cei[:]))
                then(nc.vector.tensor_tensor_scan(cum[:], ones[:, 0:E], ce[:], 0.0, ALU.mult, ALU.add))
                then(tt2(start[:], cum[:], ce[:], ALU.subtract))
                stt = nc.vector.scalar_tensor_tensor
                then(stt(out=tot[:], in0=bcast(start[:], 2, T), scalar=float(P), in1=tot[:], op0=ALU.mult, op1=ALU.add))
                then(tt2(base[:], ps_p[:, 0:T * E].rearrange("p (t e) -> p t e", e=E),
                         tot[:].rearrange("p e t -> p t e"), ALU.add))
                tt2(tmp[:], m1[:], base[:], ALU.mult)
                then(tt2(tmp2[:], m2[:], base[:], ALU.mult))
                nc.vector.tensor_reduce(pos[:, 0, :], tmp[:], AX.X, ALU.add)
                reduce(pos[:, 1, :], tmp2[:], ALU.add)
                then(nc.vector.tensor_copy(posi[:], pos[:]))
                ts(keyi[:, 0], posi[:], 7, None, ALU.arith_shift_right)
                then(ts(keyi[:, 1], posi[:], P - 1, None, ALU.bitwise_and))
                then(nc.vector.tensor_copy(keyb[:], keyi[:]))

                def hot(i, s, wait=True):
                    q = quad(i, s)
                    if wait:
                        dve.wait_ge(map_done, q - 1)
                    keys = keyb[:, :, :, bass.ts(q, QT)]
                    tt2(hot_b[:, s], bcast(bcast(io[:], 1, QT), 1, 2), bcast(keys[:, 1], 3, P), ALU.is_equal)
                    tt2(hot_j[:, s], bcast(bcast(io[:, 0:TILES_MAX], 1, QT), 1, 2), bcast(keys[:, 0], 3, TILES_MAX),
                        ALU.is_equal).then_inc(hot_done, 1)

                for s in range(RING):
                    dve.wait_ge(rows_out[s], 32 * (QUADS // RING + 1))
                    hot(0, s, wait=False)
                with dve.Fori(1, QUADS // RING) as i:
                    for s in range(RING):
                        hot(i, s)

                then(tt2(ge, bcast(io[:, 0:TILES_MAX], 2, E), bcast(cum[:], 1, TILES_MAX), ALU.is_ge))
                reduce(e_j[:], ge, ALU.add)
                ts(tile_exp[:], e_j[:], float(E - 1), None, ALU.min)
                dve.wait_ge(map_done, QUADS)
                then(nc.vector.tensor_copy(slot_v[:], ps_m[:, 0:TILES_MAX]))
                ts(slot_t[:], slot_v[:], 0.0, no_row[:, 0:1], ALU.is_equal, ALU.mult)
                stt(out=slot_0[:], in0=slot_v[:], scalar=0.0, in1=no_place[:], op0=ALU.is_equal, op1=ALU.mult)
                then(stt(out=size[:], in0=slot_v[:], scalar=-1.0, in1=slot_v[:], op0=ALU.mult, op1=ALU.max))
                then(stt(out=idx_map[:, :, 0], in0=size[:], scalar=-1.0, in1=slot_t[:], op0=ALU.add, op1=ALU.add))
                stt(out=size[:], in0=size[:], scalar=-1.0, in1=slot_0[:], op0=ALU.add, op1=ALU.add)
                then(ts(slot_v[:], slot_v[:], 0.0, float(TOKENS), ALU.is_lt, ALU.mult))
                tt2(idx_map[:, :, 1], size[:], slot_v[:], ALU.add)


def expert_phase(nc, xs, eye, rows, chosen_rows, out, wa_hi, wa_lo, wb_hi, wb_lo, wd_hi, wd_lo, idx_map, tile_exp):
    with ExitStack() as stack:
        a = Scope(nc, stack, "moe")
        xt = a.sb("xt", [P, XR, ROW])
        idx = a.sb("idx", [P, XR, 2], I32)
        x_hi = a.sb("x_hi", [P, RING, 2 * P], F32R)
        x_lo = a.sb("x_lo", [P, RING, P], F32R)
        sg, hid = a.sb("sg", [P, RING, HID]), a.sb("hid", [P, RING, HID])
        h_hi, h_lo = a.sb("h_hi", [P, RING, HID], F32R), a.sb("h_lo", [P, RING, HID], F32R)
        y = a.sb("y", [P, YR, C])
        pick = a.sb("pick", [P, RING, 2, QT, C])
        ps_x, ps_h = a.ps("ps_x", [P, 512]), a.ps("ps_h", [P, 512])
        ps_g, ps_u, ps_y = (a.ps(n, [P, RING, 512]) for n in ("ps_gt", "ps_u", "ps_y"))

        gathered = [a.sem(f"gathered{s}") for s in range(XR)]
        scattered = [a.sem(f"scattered{s}") for s in range(YR)]
        picked, out_stored = ([a.sem(f"{n}{s}") for s in range(RING)] for n in ("picked", "out_stored"))
        sum_done, total_done = a.sem("sum_done"), a.sem("total_done")
        idx_done, pool_turn = a.sem("idx_done"), a.sem("pool_turn")
        xt_done, gate_done, up_done, ht_done, y_mm = (a.sem(n) for n in ("xt_done", "gate_done", "up_done", "ht_done", "y_mm"))
        x_hi_done, x_lo_done, x_lob_done = a.sem("x_hi_done"), a.sem("x_lo_done"), a.sem("x_lob_done")
        silu_done, hid_done = a.sem("silu_done"), a.sem("hid_done")
        h_hi_done, h_lo_done, y_done = a.sem("h_hi_done"), a.sem("h_lo_done"), a.sem("y_done")
        N = TILES_MAX

        with nc.Block() as block:
            @block.gpsimd
            def _(pool):
                pool.sem_inc(idx_done, RING)

                def gather(i, r):
                    j, n, slot = XR * i + r, i + r // XR, r % XR
                    nc.gpsimd.tensor_copy(idx[:, slot, :], idx_map[:, bass.ds(j, 1), :]).then_inc(idx_done, 1)
                    pool.wait_ge(idx_done, made(j))
                    pool.sem_inc(pool_turn, 1)
                    nc.gpsimd.indirect_dma_start(
                        xt[:, slot, :], None, rows.ap(),
                        bass.IndirectOffsetOnAxis(ap=idx[:, slot, 0:1], axis=0)).then_inc(gathered[slot], 16)

                def scatter(i, r):
                    j, slot = XR * i + r, r % XR
                    pool.wait_ge(y_done, made(j))
                    pool.sem_inc(pool_turn, 1)
                    nc.gpsimd.indirect_dma_start(
                        chosen_rows.ap(), bass.IndirectOffsetOnAxis(ap=idx[:, slot, 1:2], axis=0),
                        y[:, slot % YR, :], None).then_inc(scattered[slot % YR], 16)

                def landed(i, r):
                    pool.wait_ge(scattered[r % YR], 16 * (XR // YR * i + r // YR) + 16)
                    pool.sem_inc(pool_turn, 1)

                for r in range(AHEAD):
                    gather(0, r)
                for r in range(XR):
                    scatter(0, r)
                    if r >= 2:
                        landed(0, r - 2)
                    gather(0, r + AHEAD)
                with pool.Fori(1, N // XR - 1) as i:
                    for r in range(XR):
                        scatter(i, r)
                        landed(i, r - 2)
                        gather(i, r + AHEAD)
                n = N // XR - 1
                for r in range(XR):
                    scatter(n, r)
                    landed(n, r - 2)
                    if r < 2:
                        gather(n, r + AHEAD)

            @block.tensor
            def _(pe):
                for c in (xt_done, gate_done, up_done, ht_done, y_mm):
                    pe.sem_inc(c, RING)

                def expert(i, r):
                    return pe.value_load(tile_exp[0:1, bass.ds(XR * i + r, 1)], min_val=0, max_val=EXPERTS - 1)

                def turn_x(i, r):
                    j, n, slot = XR * i + r, i + r // XR, r % XR
                    pe.wait_ge(gathered[slot], 16 * n + 16)
                    nc.tensor.transpose(ps_x[:, 0:P], xt[:, slot, 0:P], eye[:])
                    nc.tensor.transpose(ps_x[:, P:2 * P], xt[:, slot, P:GC], eye[:]).then_inc(xt_done, 1)

                def product(r, e, dst, col, done):
                    s = r % RING
                    at = dst[:, s, 0:HID]
                    w = bass.ds(col, HID)
                    hb = x_hi[:, s, P:2 * P]
                    nc.tensor.matmul(at, x_hi[:, s, 0:P], wa_hi[:, e, w], start=True, stop=False)
                    nc.tensor.matmul(at, x_hi[:, s, 0:P], wa_lo[:, e, w], start=False, stop=False)
                    nc.tensor.matmul(at, x_lo[:, s, :], wa_hi[:, e, w], start=False, stop=False)
                    nc.tensor.matmul(at, hb, wb_hi[:, e, w], start=False, stop=False)
                    nc.tensor.matmul(at, hb[0:CB, :], wb_lo[:, e, w], start=False, stop=True).then_inc(done, 1)

                def turn_h(i, r):
                    j, s = XR * i + r, r % RING
                    pe.wait_ge(hid_done, made(j))
                    pe.wait_ge(h_lo_done, j + RING)
                    for k in range(3):
                        ins = nc.tensor.transpose(ps_h[:, bass.ts(k, P)], hid[:, s, bass.ts(k, P)], eye[:])
                    ins.then_inc(ht_done, 1)

                def down_product(r, e):
                    s = r % RING
                    at = ps_y[:, s, 0:C]
                    for k in range(3):
                        hi, lo = h_hi[:, s, bass.ts(k, P)], h_lo[:, s, bass.ts(k, P)]
                        w = bass.ts(k, C)
                        nc.tensor.matmul(at, hi, wd_hi[:, e, w], start=(k == 0), stop=False)
                        nc.tensor.matmul(at, hi, wd_lo[:, e, w], start=False, stop=False)
                        ins = nc.tensor.matmul(at, lo, wd_hi[:, e, w], start=False, stop=(k == 2))
                    ins.then_inc(y_mm, 1)

                def gate_product(i, r, e):
                    pe.wait_ge(x_lob_done, made(XR * i + r))
                    product(r, e, ps_g, 0, gate_done)

                def up_product(r, e):
                    product(r, e, ps_u, HID, up_done)

                def steps(i, first, last):
                    e = {first: expert(i, first)}
                    for r in range(first, last):
                        gate_product(i, r, e[r])
                        turn_h(i, r - 1)
                        if r + 1 < XR or last > XR:
                            turn_x(i, r + 1)
                        up_product(r, e[r])
                        if r - 2 < first:
                            e[r - 2] = expert(i, r - 2)
                        if r + 1 < last:
                            e[r + 1] = expert(i, r + 1)
                        down_product(r - 2, e[r - 2])
                    return e

                turn_x(0, 0)
                for r in range(2):
                    e = expert(0, r)
                    gate_product(0, r, e)
                    if r:
                        turn_h(0, r - 1)
                    turn_x(0, r + 1)
                    up_product(r, e)
                with pe.Fori(0, N // XR - 1) as i:
                    steps(i, 2, XR + 2)
                n = N // XR - 1
                e = steps(n, 2, XR)
                turn_h(n, XR - 1)
                down_product(XR - 2, e[XR - 2])
                pe.wait_ge(h_lo_done, made(N - 1))
                down_product(XR - 1, e[XR - 1])

            @block.scalar
            def _(act):
                for c in (x_hi_done, silu_done, h_hi_done, y_done):
                    act.sem_inc(c, RING)

                def x_high(i, r):
                    j, s = XR * i + r, r % RING
                    act.wait_ge(xt_done, made(j))
                    nc.scalar.activation(x_hi[:, s, :], ps_x[:, 0:2 * P], ACT.Copy).then_inc(x_hi_done, 1)

                def silu(i, r):
                    j, s = XR * i + r, r % RING
                    act.wait_ge(gate_done, made(j))
                    nc.scalar.activation(sg[:, s, :], ps_g[:, s, 0:HID], ACT.Silu).then_inc(silu_done, 1)

                def h_high(i, r):
                    j, s = XR * i + r, r % RING
                    act.wait_ge(ht_done, made(j))
                    nc.scalar.activation(h_hi[:, s, :], ps_h[:, 0:HID], ACT.Copy).then_inc(h_hi_done, 1)

                def weigh(i, r):
                    j, slot, s = XR * i + r, r % XR, r % RING
                    e = act.value_load(tile_exp[0:1, bass.ds(j, 1)], min_val=0, max_val=EXPERTS - 1)
                    act.wait_ge(y_mm, made(j))
                    nc.scalar.activation(y[:, r % YR, :], ps_y[:, s, 0:C], ACT.Copy,
                                         scale=xt[:, slot, bass.ds(GC + e, 1)]).then_inc(y_done, 1)

                def y_free(i, r):
                    act.wait_ge(scattered[r % YR], 16 * (XR // YR * i + r // YR))

                x_high(0, 0)
                x_high(0, 1)
                silu(0, 0)
                h_high(0, 0)
                x_high(0, 2)
                silu(0, 1)
                for r in range(2, XR + 2):
                    h_high(0, r - 1)
                    x_high(0, r + 1)
                    silu(0, r)
                    if r - 2 >= YR:
                        y_free(0, r - 2)
                    weigh(0, r - 2)
                with act.Fori(1, N // XR - 1) as i:
                    for r in range(2, XR + 2):
                        h_high(i, r - 1)
                        x_high(i, r + 1)
                        silu(i, r)
                        y_free(i, r - 2)
                        weigh(i, r - 2)
                n = N // XR - 1
                for r in range(2, XR + 2):
                    if r - 1 < XR:
                        h_high(n, r - 1)
                    if r + 1 < XR:
                        x_high(n, r + 1)
                    if r < XR:
                        silu(n, r)
                    y_free(n, r - 2)
                    weigh(n, r - 2)

            @block.vector
            def _(dve):
                for c in (x_lo_done, x_lob_done, hid_done, h_lo_done):
                    dve.sem_inc(c, RING)

                def x_low(i, r):
                    j, s = XR * i + r, r % RING
                    dve.wait_ge(x_hi_done, made(j))
                    nc.vector.tensor_tensor(x_lo[:, s, :], ps_x[:, 0:P], x_hi[:, s, 0:P].bitcast(F32),
                                            ALU.subtract).then_inc(x_lo_done, 1)
                    b = x_hi[CB:P, s, P:2 * P]
                    nc.vector.tensor_tensor(b, ps_x[CB:P, P:2 * P], b.bitcast(F32), ALU.subtract).then_inc(x_lob_done, 1)

                def hidden(i, r):
                    j, s = XR * i + r, r % RING
                    dve.wait_ge(silu_done, made(j))
                    dve.wait_ge(up_done, made(j))
                    nc.vector.tensor_tensor(hid[:, s, :], ps_u[:, s, 0:HID], sg[:, s, :], ALU.mult).then_inc(hid_done, 1)

                def h_low(i, r):
                    j, s = XR * i + r, r % RING
                    dve.wait_ge(h_hi_done, made(j))
                    nc.vector.tensor_tensor(h_lo[:, s, :], ps_h[:, 0:HID], h_hi[:, s, :].bitcast(F32),
                                            ALU.subtract).then_inc(h_lo_done, 1)

                x_low(0, 0)
                x_low(0, 1)
                hidden(0, 0)
                with dve.Fori(0, N // XR - 1) as i:
                    for r in range(1, XR + 1):
                        h_low(i, r - 1)
                        x_low(i, r + 1)
                        hidden(i, r)
                n = N // XR - 1
                for r in range(1, XR):
                    h_low(n, r - 1)
                    if r + 1 < XR:
                        x_low(n, r + 1)
                    hidden(n, r)
                h_low(n, XR - 1)

                with dve.Fori(0, QUADS // RING) as i:
                    for s in range(RING):
                        q = quad(i, s)
                        dve.wait_ge(picked[s], 32 * i + 32)
                        nc.vector.tensor_tensor(pick[:, s, 0], pick[:, s, 0], pick[:, s, 1],
                                                ALU.add).then_inc(sum_done, 1)
                        dve.wait_ge(sum_done, q + 1)
                        at = xs[:, bass.ts(q, QT), :]
                        nc.vector.tensor_tensor(at, at, pick[:, s, 0], ALU.add).then_inc(total_done, 1)

            @block.sync
            def _(sp):
                out_tiles = out.rearrange("(t p) c -> p t c", p=P)
                picks = chosen_rows[0:2 * TOKENS, :].rearrange("(k t p) c -> k p t c", k=2, p=P)
                for r in range(YR):
                    sp.wait_ge(scattered[r], 16 * N // YR)

                def load(i, s):
                    q = quad(i, s)
                    for k in range(2):
                        sp.dma_start(pick[:, s, k], picks[k, :, bass.ts(q, QT), :]).then_inc(picked[s], 16)

                def store(i, s):
                    q = quad(i, s)
                    sp.wait_ge(total_done, q + 1)
                    sp.dma_start(out_tiles[:, bass.ts(q, QT), :], xs[:, bass.ts(q, QT), :]).then_inc(out_stored[s], 16)

                load(0, 0)
                load(0, 1)
                with sp.Fori(1, QUADS // RING) as i:
                    for s in range(RING):
                        store(i - 1, s)
                        load(i, s)
                for s in range(RING):
                    store(QUADS // RING - 1, s)
                for s in range(RING):
                    sp.wait_ge(out_stored[s], 16 * QUADS // RING)


def kernel(**inputs):
    import numpy as np
    import concourse.bacc as bacc
    from concourse import mybir as mb
    from concourse.bass_utils import run_bass_kernel_spmd as run

    f = np.float32
    get = {k: np.asarray(v) for k, v in inputs.items()}
    x = get["x"].reshape(TOKENS, C)

    line = int((SIDE * SIDE * 0.25) ** 0.5 // 2)
    mask = np.zeros((SIDE, SIDE))
    mask[SIDE // 2 - line:SIDE // 2 + line, SIDE // 2 - line:SIDE // 2 + line] = 1.0
    unit = np.eye(SEQ).reshape(SEQ, SIDE, SIDE)
    spec = np.fft.fftshift(np.fft.fft2(unit, norm="forward"), axes=(-2, -1)) * mask
    low = np.fft.ifft2(np.fft.ifftshift(spec, axes=(-2, -1)), norm="forward").real.reshape(SEQ, SEQ)
    inv = (1.0 / 10000.0 ** (np.arange(0, HD, 2, dtype=f) / f(HD))).astype(f)
    ang = np.arange(SEQ, dtype=f)[:, None] * inv[None, :]
    cos, sin = np.cos(ang).astype(f), np.sin(ang).astype(f)
    rep = lambda v: np.ascontiguousarray(np.broadcast_to(v.astype(f).reshape(1, -1), (P, v.size)))
    p = np.arange(P)
    token = (p[:, None] + P * np.arange(TILES)[None, :] + 1).astype(f)
    iotas = [
        rep(np.arange(P)),
        rep(np.tile(EXPERTS - np.arange(EXPERTS), TILES)),
        rep(np.tile((np.arange(TILES) > 0), EXPERTS)),
        np.stack([token, -token], 1),
        (TOKENS + 1 + p[:, None]).astype(f),
        (2 * TOKENS + 1 + P * (np.arange(TILES_MAX) % PADS)[None, :] + p[:, None]).astype(f),
    ]
    ytab = np.zeros((P, 1), f)
    ytab[[DH, DP + DH]] = 1.0

    rows = lambda *v: np.ascontiguousarray(np.concatenate(v, 0))
    wk, bk = get["L1_attn_Wk"], get["L1_attn_bk"]
    wqkv = rows(np.concatenate([get["L1_attn_Wq"], wk, wk, get["L1_attn_Wv"]], 1),
                np.concatenate([get["L1_attn_bq"], bk, bk, get["L1_attn_bv"]])[None, :])
    arrays = {
        "x": np.ascontiguousarray(x),
        "xT": np.ascontiguousarray(x.T),
        "w1": rows(get["L0_conv_W1"].T, get["L0_conv_b1"][None, :]),
        "w2": rows(get["L0_conv_W2"].T, get["L0_conv_b2"][None, :]),
        "lowpass": low.astype(f),
        "wqkv": wqkv,
        "cos": np.concatenate([cos, cos, cos], 1),
        "sin": np.concatenate([-sin, sin, -sin], 1),
        "gate": np.ascontiguousarray(get["L1_ffn_gate_w"].T),
        "wgu": np.ascontiguousarray(np.concatenate([get["L1_ffn_gate_bank"], get["L1_ffn_up_bank"]], 2).transpose(1, 0, 2)),
        "down": np.ascontiguousarray(get["L1_ffn_down_bank"]),
        "tri": np.triu(np.ones((P, P), f), 1),
        "ident": np.eye(P, dtype=f),
        **{f"iota{k}": v for k, v in enumerate(iotas)},
        "ytab": ytab,
    }
    nc = bacc.Bacc("TRN2", target_bir_lowering=False, num_devices=1)
    ap = {k: nc.dram_tensor(f"in_{k}", v.shape, mb.dt.from_np(v.dtype), kind="ExternalInput").ap()
          for k, v in arrays.items()}
    out = nc.dram_tensor("out_0", (TOKENS, C), mb.dt.float32, kind="ExternalOutput").ap()
    tables = [ap.pop(f"iota{k}") for k in range(len(iotas))]
    program(nc, **ap, iotas=tables, out=out)
    r = run(nc, [{f"in_{k}": v for k, v in arrays.items()}], core_ids=[0])
    return r.results[0]["out_0"].reshape(get["x"].shape)
```

```python
from contextlib import ExitStack

import concourse.bass as bass
from concourse import mybir

F32 = mybir.dt.float32
F32R = mybir.dt.float32r
I32 = mybir.dt.int32
ALU = mybir.AluOpType
ACT = mybir.ActivationFunctionType
AX = mybir.AxisListType

P = 128
IMAGES, SIDE, C = 16, 16, 192
SEQ = SIDE * SIDE
TOKENS = IMAGES * SEQ
DH = 48
DP = 64
CB = C - P
HEADS, HD = 12, 16
QW = C + 3 * HD
KC, VC = C, C + 2 * HD
EXPERTS, HID = 8, 384
TILES = TOKENS // P
QT = 4
QUADS = TILES // QT
PR = 4
HT, HR = 2, 4
LAG = 3
RING = 2
XR = 8
AHEAD = XR - 2
YR = 4
PADS = 4
TILES_MAX = -(-(2 * TOKENS // P + EXPERTS - 1) // XR) * XR
GC = C + CB
ROW = GC + 8
EPS = 1e-5
SCALE = HD ** -0.5


def quad(i, s):
    return RING * i + s


def turned(i, r):
    return i + r // RING, r % RING


def made(n):
    return n + 1 + RING


def freed(n):
    return n + 1


def bcast(ap, axis, n):
    v = ap.unsqueeze(axis)
    shape = list(v.shape)
    shape[axis] = n
    return v.broadcast_to(shape)


def program(nc, x, xT, w1, w2, lowpass, wqkv, cos, sin, gate, wgu, down, tri, ident, iotas, ytab, out):
    chosen_rows = nc.dram_tensor("chosen_rows", [2 * TOKENS + PADS * P, C], F32)
    rows = nc.dram_tensor("rows", [TOKENS + P, ROW], F32)
    x_tiles = x.rearrange("(t p) c -> p t c", p=P)
    row_tiles = rows[0:TOKENS, :].rearrange("(t p) c -> p t c", p=P)

    with ExitStack() as whole:
        def keep(name, shape, dt=F32):
            return whole.enter_context(nc.sbuf_tensor(name, shape, dt))

        wa_hi = keep("wa_hi", [P, EXPERTS, 2 * HID], F32R)
        wa_lo = keep("wa_lo", [P, EXPERTS, 2 * HID], F32R)
        wb_hi = keep("wb_hi", [P, EXPERTS, 2 * HID], F32R)
        wb_lo = keep("wb_lo", [CB, EXPERTS, 2 * HID], F32R)
        wd = keep("wd", [P, EXPERTS, 3, 2, C], F32R)
        eye = keep("eye", [P, P])
        idx_map = keep("idx_map", [P, TILES_MAX, 2], I32)
        tile_exp = keep("tile_exp", [P, TILES_MAX], I32)

        xs = keep("xs", [P, TILES, C])
        mean, rstd = keep("mean", [P, TILES]), keep("rstd", [P, TILES])

        lg = keep("lg", [P, TILES, EXPERTS])
        wqa, wqb = keep("wqa", [P, QW]), keep("wqb", [CB + 1, QW])
        ga, gb = keep("ga", [P, EXPERTS]), keep("gb", [CB, EXPERTS])
        cos_t, sin_t = keep("cos_t", [P, QT, 24]), keep("sin_t", [P, QT, 24])
        tables = [(dst[:, 2 * h:2 * h + 2, :], src.rearrange("(h p) d -> p h d", p=P))
                  for dst, src in ((cos_t, cos), (sin_t, sin)) for h in range(2)]
        later = [(wqa[:], wqkv[0:P, :]), (wqb[:], wqkv[P:C + 1, :]), (ga[:], gate[0:P, :]),
                 (gb[:], gate[P:C, :])] + tables

        conv_phase(nc, xs, mean, rstd, x_tiles, xT, w1, w2, lowpass, wgu, wa_hi, wa_lo, wb_hi, wb_lo, ytab, eye, ident,
                   later)
        attention_phase(nc, xs, mean, rstd, eye, wqa, wqb, cos_t, sin_t, ga, gb, rows, row_tiles, down, wd, lg)
        routing_phase(nc, lg, tri, iotas, row_tiles, idx_map, tile_exp)
        expert_phase(nc, xs, eye, rows, chosen_rows, out, wa_hi, wa_lo, wb_hi, wb_lo, wd, idx_map, tile_exp)


class Scope:

    def __init__(self, nc, stack, phase):
        self.nc, self.stack, self.phase = nc, stack, phase

    def sb(self, name, shape, dt=F32):
        return self.stack.enter_context(self.nc.sbuf_tensor(f"{self.phase}_{name}", shape, dt))

    def ps(self, name, shape):
        return self.stack.enter_context(self.nc.psum_tensor(f"{self.phase}_{name}", shape, F32))

    def sem(self, name):
        return self.stack.enter_context(self.nc.semaphore(f"{self.phase}_{name}"))


def conv_phase(nc, xs, mean, rstd, x_tiles, xT, w1, w2, lowpass, wgu, wa_hi, wa_lo, wb_hi, wb_lo, ytab, eye, ident,
               later):
    with ExitStack() as stack:
        a = Scope(nc, stack, "conv")
        w1a, w1b = a.sb("w1a", [P, DH]), a.sb("w1b", [CB + 1, DH])
        w2s = a.sb("w2s", [P, C])
        lp = a.sb("lp", [P, 2, SEQ])
        y_bias = a.sb("y_bias", [P, 1])
        xta, xtb = a.sb("xta", [P, RING, QT * P]), a.sb("xtb", [CB + 1, RING, QT * P])
        g = a.sb("g", [P, RING, 2, 2, DP])
        g_hi, g_lo = a.sb("g_hi", [P, RING, 2, 2, DP], F32R), a.sb("g_lo", [P, RING, 2, 2, DP], F32R)
        yt = a.sb("yt", [P, RING, SEQ])
        yt_hi, yt_lo = a.sb("yt_hi", [P, RING, SEQ], F32R), a.sb("yt_lo", [P, RING, SEQ], F32R)
        lp_hi, lp_lo = a.sb("lp_hi", [P, 2, SEQ], F32R), a.sb("lp_lo", [P, 2, SEQ], F32R)
        w2_hi, w2_lo = a.sb("w2_hi", [P, C], F32R), a.sb("w2_lo", [P, C], F32R)
        stage = a.sb("stage", [P, RING, 2, 2 * HID])
        stats, mv = a.sb("stats", [P, RING, QT, 6]), a.sb("mv", [P, RING, QT, 2])
        vtmp, half = a.sb("vtmp", [P, RING, QT]), a.sb("half", [P, 1])
        ps_w1, ps_f = a.ps("ps_w1", [P, RING, 512]), a.ps("ps_f", [P, RING, 512])
        ps_c = a.ps("ps_c", [P, RING, 2, 512])

        consts_in = a.sem("consts_in")
        xt_in = [a.sem(f"xt_in{s}") for s in range(RING)]
        x_in = [a.sem(f"x_in{s}") for s in range(RING)]
        stage_in = [a.sem(f"stage_in{s}") for s in range(RING)]
        filled = a.sem("filled")
        bias_row = a.sem("bias_row")
        w1_done, fft_done, w2_done = a.sem("w1_done"), a.sem("fft_done"), a.sem("w2_done")
        gelu_done, abs_done, hi_done = a.sem("gelu_done"), a.sem("abs_done"), a.sem("hi_done")
        added, stats_done, mv_done = a.sem("added"), a.sem("stats_done"), a.sem("mv_done")
        lo_done, eps_done, pow_done = a.sem("lo_done"), a.sem("eps_done"), a.sem("pow_done")
        mean_done = a.sem("mean_done")
        w1_in, later_in = a.sem("w1_in"), a.sem("later_in")
        const_hi_done, const_lo_done, lob_done = (a.sem(n) for n in ("const_hi_done", "const_lo_done", "lob_done"))
        g_lo_done, yt_lo_done = a.sem("g_lo_done"), a.sem("yt_lo_done")
        g_made = a.sem("g_made")
        pool_turn, dve_turn = a.sem("pool_turn"), a.sem("dve_turn")

        with nc.Block() as block:
            @block.sync
            def _(sp):
                sp.dma_start(w1a[:], w1[0:P, :]).then_inc(w1_in, 16)
                sp.dma_start(w1b[:], w1[P:C + 1, :]).then_inc(w1_in, 16)

                def load(i, s):
                    q = quad(i, s)
                    sp.wait_ge(w1_done, freed(q))
                    sp.dma_start(xta[:, s, :], xT[0:P, bass.ts(q, QT * P)]).then_inc(xt_in[s], 16)
                    sp.dma_start(xtb[0:CB, s, :], xT[P:C, bass.ts(q, QT * P)]).then_inc(xt_in[s], 16)

                def load_rows(i, s):
                    at = bass.ts(quad(i, s), QT)
                    sp.dma_start(xs[:, at, :], x_tiles[:, at, :]).then_inc(x_in[s], 16)

                def load_weights(i, s):
                    q = quad(i, s)
                    sp.wait_ge(lo_done, freed(q))
                    sp.wait_ge(lob_done, freed(q))
                    sp.dma_start(stage[:, s, 0], wgu[0:P, q, :]).then_inc(stage_in[s], 16)
                    for k in range(2):
                        sp.dma_start(stage[k * CB:(k + 1) * CB, s, 1], wgu[P:C, q, :]).then_inc(stage_in[s], 16)

                load(0, 0)
                load(0, 1)
                sp.dma_start(lp[:], lowpass.rearrange("(h p) s -> p h s", p=P)).then_inc(consts_in, 16)
                sp.dma_start(w2s[0:DH + 1, :], w2).then_inc(consts_in, 16)
                sp.dma_start(w2s[DP:DP + DH + 1, :], w2).then_inc(consts_in, 16)
                sp.dma_start(y_bias[:], ytab).then_inc(consts_in, 16)
                sp.dma_start(eye[:], ident).then_inc(consts_in, 16)
                load_rows(0, 0)
                load_rows(0, 1)
                load_weights(0, 0)
                with sp.Fori(1, QUADS // RING) as i:
                    for s in range(RING):
                        load(i, s)
                        load_rows(i, s)
                        load_weights(*turned(i, s - 1))
                load_weights(QUADS // RING - 1, 1)
                for dst, src in later:
                    sp.dma_start(dst, src).then_inc(later_in, 16)
                sp.wait_ge(later_in, 16 * len(later))

            @block.tensor
            def _(pe):
                pe.sem_inc(w1_done, RING)
                pe.sem_inc(fft_done, RING)
                pe.sem_inc(w2_done, RING)
                pe.wait_ge(w1_in, 2 * 16)
                pe.wait_ge(bias_row, 1)

                def in_product(i, s):
                    q = quad(i, s)
                    pe.wait_ge(xt_in[s], 32 * i + 32)
                    pe.wait_ge(gelu_done, freed(q))
                    for t in range(QT):
                        at = ps_w1[:, s, t * DH:(t + 1) * DH]
                        nc.tensor.matmul(at, xta[:, s, bass.ts(t, P)], w1a[:], start=True, stop=False)
                        last = nc.tensor.matmul(at, xtb[:, s, bass.ts(t, P)], w1b[:], start=False, stop=True)
                    last.then_inc(w1_done, 1)

                def lowpass_product(i, s):
                    q = quad(i, s)
                    pe.wait_ge(g_lo_done, made(q))
                    pe.wait_ge(abs_done, freed(q))
                    for h in range(2):
                        hi, lo = (v[:, s, h].rearrange("p m d -> p (m d)") for v in (g_hi, g_lo))
                        nc.tensor.matmul(ps_f[:, s, 0:SEQ], hi, lp_hi[:, h, :], start=(h == 0), stop=False)
                        nc.tensor.matmul(ps_f[:, s, 0:SEQ], hi, lp_lo[:, h, :], start=False, stop=False)
                        last = nc.tensor.matmul(ps_f[:, s, 0:SEQ], lo, lp_hi[:, h, :], start=False, stop=(h == 1))
                    last.then_inc(fft_done, 1)

                def out_product(i, s):
                    q = quad(i, s)
                    pe.wait_ge(yt_lo_done, made(q))
                    pe.wait_ge(added, freed(q))
                    for m in range(2):
                        k = slice(DP * m, DP * m + DH + 1)
                        for h in range(2):
                            at = ps_c[:, s, m, h * C:(h + 1) * C]
                            hi, lo = yt_hi[k, s, bass.ts(h, P)], yt_lo[k, s, bass.ts(h, P)]
                            nc.tensor.matmul(at, hi, w2_hi[k, :], start=True, stop=False)
                            nc.tensor.matmul(at, hi, w2_lo[k, :], start=False, stop=False)
                            last = nc.tensor.matmul(at, lo, w2_hi[k, :], start=False, stop=True)
                    last.then_inc(w2_done, 1)

                in_product(0, 0)
                in_product(0, 1)
                pe.wait_ge(const_lo_done, 1)
                lowpass_product(0, 0)
                with pe.Fori(1, QUADS // RING) as i:
                    in_product(i, 0)
                    lowpass_product(i - 1, 1)
                    out_product(i - 1, 0)
                    in_product(i, 1)
                    lowpass_product(i, 0)
                    out_product(i - 1, 1)
                last = QUADS // RING - 1
                lowpass_product(last, 1)
                out_product(last, 0)
                out_product(last, 1)

            @block.scalar
            def _(act):
                act.sem_inc(gelu_done, RING)
                act.sem_inc(abs_done, RING)
                act.sem_inc(hi_done, RING)
                act.wait_ge(consts_in, 5 * 16)
                act.wait_ge(filled, 2)
                nc.scalar.activation(lp_hi[:], lp[:], ACT.Copy)
                for k in (0, DP):
                    b = slice(k, k + DH + 1)
                    ins = nc.scalar.activation(w2_hi[b, :], w2s[b, :], ACT.Copy)
                ins.then_inc(const_hi_done, 1)

                def gelu(i, s):
                    q = quad(i, s)
                    act.wait_ge(w1_done, made(q))
                    act.wait_ge(fft_done, freed(q))
                    act.wait_ge(g_lo_done, freed(q))
                    nc.scalar.activation(g[:, s].rearrange("p h m d -> p m h d")[:, :, :, 0:DH],
                                         ps_w1[:, s, 0:QT * DH].rearrange("p (m h d) -> p m h d", m=2, h=2),
                                         ACT.Gelu).then_inc(g_made, 1)
                    act.wait_ge(g_made, q + 1)
                    nc.scalar.activation(g_hi[:, s], g[:, s], ACT.Copy).then_inc(gelu_done, 1)

                def magnitude(i, s):
                    q = quad(i, s)
                    act.wait_ge(fft_done, made(q))
                    act.wait_ge(w2_done, freed(q))
                    act.wait_ge(yt_lo_done, freed(q))
                    for dst in (yt, yt_hi):
                        ins = nc.scalar.activation(dst[:, s, :], ps_f[:, s, 0:SEQ], ACT.Abs, bias=y_bias[:, 0:1])
                    ins.then_inc(abs_done, 1)

                def split(i, s):
                    act.wait_ge(stage_in[s], 48 * i + 48)
                    nc.scalar.activation(wa_hi[:, quad(i, s), :], stage[:, s, 0], ACT.Copy)
                    nc.scalar.activation(wb_hi[:, quad(i, s), :], stage[:, s, 1], ACT.Copy).then_inc(hi_done, 1)

                gelu(0, 0)
                gelu(0, 1)
                magnitude(0, 0)
                split(0, 0)
                with act.Fori(1, QUADS // RING) as i:
                    gelu(i, 0)
                    magnitude(i - 1, 1)
                    split(i - 1, 1)
                    gelu(i, 1)
                    magnitude(i, 0)
                    split(i, 0)
                last = QUADS // RING - 1
                magnitude(last, 1)
                split(last, 1)

            @block.gpsimd
            def _(pool):
                pool.sem_inc(lo_done, RING)
                pool.sem_inc(pow_done, RING)
                pool.sem_inc(eps_done, RING)
                pool.sem_inc(mean_done, RING)
                nc.gpsimd.memset(g[:], 0.0).then_inc(filled, 1)
                nc.gpsimd.memset(half[:], -0.5).then_inc(filled, 1)
                pool.wait_ge(filled, 2)

                def split(i, s):
                    q = quad(i, s)
                    pool.wait_ge(hi_done, made(q))
                    pool.sem_inc(pool_turn, 1)
                    nc.gpsimd.tensor_tensor(wa_lo[:, q, :], stage[:, s, 0], wa_hi[:, q, :].bitcast(F32),
                                            ALU.subtract).then_inc(lo_done, 1)

                def deviation(i, s):
                    row_deviation(nc, pool, quad(i, s), s, mv, vtmp, half, mean, rstd, mv_done, eps_done,
                                  pow_done, mean_done, pool_turn)

                split(0, 0)
                with pool.Fori(1, QUADS // RING) as i:
                    split(i - 1, 1)
                    deviation(i - 1, 0)
                    split(i, 0)
                    deviation(i - 1, 1)
                last = QUADS // RING - 1
                split(last, 1)
                deviation(last, 0)
                deviation(last, 1)

            @block.vector
            def _(dve):
                nc.vector.memset(xtb[CB:CB + 1, :, :], 1.0).then_inc(bias_row, 1)
                dve.sem_inc(added, RING)
                dve.sem_inc(g_lo_done, RING)
                dve.sem_inc(yt_lo_done, RING)
                dve.sem_inc(lob_done, RING)
                dve.sem_inc(stats_done, RING)
                dve.sem_inc(mv_done, RING)

                def finish(i, s):
                    q = quad(i, s)
                    dve.wait_ge(x_in[s], 16 * i + 16)
                    dve.wait_ge(w2_done, made(q))
                    for m in range(2):
                        at = xs[:, bass.ts(2 * q + m, 2), :]
                        ins = nc.vector.tensor_tensor(
                            at, ps_c[:, s, m, 0:2 * C].rearrange("p (h c) -> p h c", h=2), at, ALU.add)
                    ins.then_inc(added, 1)
                    row_statistics(nc, dve, q, s, xs, stats, mv, added, stats_done, mv_done, pow_done, mean_done, dve_turn)

                dve.wait_ge(const_hi_done, 1)
                nc.vector.tensor_tensor(lp_lo[:], lp[:], lp_hi[:].bitcast(F32), ALU.subtract)
                for k in (0, DP):
                    b = slice(k, k + DH + 1)
                    ins = nc.vector.tensor_tensor(w2_lo[b, :], w2s[b, :], w2_hi[b, :].bitcast(F32), ALU.subtract)
                ins.then_inc(const_lo_done, 1)

                def g_low(i, s):
                    q = quad(i, s)
                    dve.wait_ge(gelu_done, made(q))
                    dve.wait_ge(fft_done, freed(q))
                    nc.vector.tensor_tensor(g_lo[:, s], g[:, s], g_hi[:, s].bitcast(F32),
                                            ALU.subtract).then_inc(g_lo_done, 1)

                def yt_low(i, s):
                    q = quad(i, s)
                    dve.wait_ge(abs_done, made(q))
                    dve.wait_ge(w2_done, freed(q))
                    nc.vector.tensor_tensor(yt_lo[:, s], yt[:, s], yt_hi[:, s].bitcast(F32),
                                            ALU.subtract).then_inc(yt_lo_done, 1)

                def split(i, s):
                    q = quad(i, s)
                    dve.wait_ge(hi_done, made(q))
                    nc.vector.tensor_tensor(wb_lo[:, q, :], stage[0:CB, s, 1], wb_hi[0:CB, q, :].bitcast(F32),
                                            ALU.subtract).then_inc(lob_done, 1)

                g_low(0, 0)
                g_low(0, 1)
                yt_low(0, 0)
                split(0, 0)
                with dve.Fori(1, QUADS // RING) as i:
                    g_low(i, 0)
                    yt_low(i - 1, 1)
                    finish(i - 1, 0)
                    split(i - 1, 1)
                    g_low(i, 1)
                    yt_low(i, 0)
                    finish(i - 1, 1)
                    split(i, 0)
                last = QUADS // RING - 1
                yt_low(last, 1)
                finish(last, 0)
                split(last, 1)
                finish(last, 1)


def row_statistics(nc, dve, q, s, xs, stats, mv, written, stats_done, mv_done, pow_done, mean_done, dve_turn):
    dve.wait_ge(written, made(q))
    dve.sem_inc(dve_turn, 1)
    for t in range(QT):
        ins = nc.vector.bn_stats(stats[:, s, t, :], xs[:, QT * q + t, :])
    ins.then_inc(stats_done, 1)
    dve.wait_ge(stats_done, made(q))
    dve.wait_ge(pow_done, freed(q))
    dve.wait_ge(mean_done, freed(q))
    dve.sem_inc(dve_turn, 1)
    for t in range(QT):
        ins = nc.vector.bn_aggr(mv[:, s, t, :], stats[:, s, t, :])
    ins.then_inc(mv_done, 1)


def row_deviation(nc, pool, q, s, mv, vtmp, half, mean, rstd, mv_done, eps_done, pow_done, mean_done, pool_turn):
    pool.wait_ge(mv_done, made(q))
    pool.sem_inc(pool_turn, 1)
    nc.gpsimd.tensor_scalar(vtmp[:, s, :], mv[:, s, :, 1], EPS, None, ALU.add).then_inc(eps_done, 1)
    nc.gpsimd.tensor_copy(mean[:, bass.ts(q, QT)], mv[:, s, :, 0]).then_inc(mean_done, 1)
    pool.wait_ge(eps_done, made(q))
    pool.sem_inc(pool_turn, 1)
    nc.gpsimd.tensor_tensor(rstd[:, bass.ts(q, QT)], vtmp[:, s, :], half[:, 0:1].broadcast_to([P, QT]),
                            ALU.pow).then_inc(pow_done, 1)


def normalise(nc, dve, q, xs, mean, rstd, dst):
    for t in range(QT):
        at = QT * q + t
        ins = nc.vector.tensor_scalar(dst[:, t, :], xs[:, at, :], mean[:, bass.ds(at, 1)],
                                      rstd[:, bass.ds(at, 1)], ALU.subtract, ALU.mult)
    return ins


def transposes(nc, src, eye, bank_a, bank_b):
    for t in range(QT):
        nc.tensor.transpose(bank_a[:, bass.ts(t, P)], src[:, t, 0:P], eye[:])
        ins = nc.tensor.transpose(bank_b[0:CB, bass.ts(t, P)], src[:, t, P:C], eye[:])
    return ins


def attention_phase(nc, xs, mean, rstd, eye, wqa, wqb, cos_t, sin_t, ga, gb, rows, row_tiles, down, wd, lg):
    with ExitStack() as stack:
        a = Scope(nc, stack, "attn")
        xn, xr = a.sb("xn", [P, RING, QT, C]), a.sb("xr", [P, RING, QT, C])
        xa, xb = a.sb("xa", [P, RING, QT * P]), a.sb("xb", [CB + 1, RING, QT * P])
        ra, rb = a.sb("ra", [P, QT * P]), a.sb("rb", [CB, QT * P])
        qkv = a.sb("qkv", [P, RING, QT, QW])
        ka, kb, kr = a.sb("ka", [P, QT, 24]), a.sb("kb", [P, QT, 24]), a.sb("kr", [P, QT, 24])
        kc, kd, kk = a.sb("kc", [P, QT, HD]), a.sb("kd", [P, QT, HD]), a.sb("kk", [P, RING, QT, HD])
        prod = a.sb("prod", [P, QT, HEADS, HD])
        score, diff = a.sb("score", [P, RING, QT * HEADS]), a.sb("diff", [P, RING, QT * HEADS])
        ex, den = a.sb("ex", [P, RING, QT * HEADS]), a.sb("den", [P, RING, QT * HEADS])
        rec, wt = a.sb("rec", [P, RING, QT * HEADS]), a.sb("wt", [P, RING, QT * HEADS])
        stage = a.sb("stage", [P, RING, 3 * C])
        stats, mv = a.sb("stats", [P, RING, QT, 6]), a.sb("mv", [P, RING, QT, 2])
        vtmp, half = a.sb("vtmp", [P, RING, QT]), a.sb("half", [P, 1])
        zero = a.sb("zero", [P, ROW])
        ps_a, ps_b = a.ps("ps_a", [P, 512]), a.ps("ps_b", [CB, 512])
        ps_ra, ps_rb = a.ps("ps_ra", [P, 512]), a.ps("ps_rb", [CB, 512])
        ps_q = a.ps("ps_q", [P, RING, 2, 512])
        ps_lg = slice(2 * QW, 2 * QW + QT * EXPERTS)

        stored, filled, bias_row = a.sem("stored"), a.sem("filled"), a.sem("bias_row")
        stage_in = [a.sem(f"stage_in{s}") for s in range(RING)]
        xn_done, tr_done, ev_done = a.sem("xn_done"), a.sem("tr_done"), a.sem("ev_done")
        qkv_done, cp_done, kk_done = a.sem("qkv_done"), a.sem("cp_done"), a.sem("kk_done")
        rope_step = a.sem("rope_step")
        prod_done, score_done, diff_done = a.sem("prod_done"), a.sem("score_done"), a.sem("diff_done")
        ex_done, den_done, rec_done, wt_done = a.sem("ex_done"), a.sem("den_done"), a.sem("rec_done"), a.sem("wt_done")
        pv_done, res_done = a.sem("pv_done"), a.sem("res_done")
        stats_done, mv_done = a.sem("stats_done"), a.sem("mv_done")
        lo_done, eps_done, pow_done, mean_done = (a.sem(n) for n in ("lo_done", "eps_done", "pow_done", "mean_done"))
        hi_done, pool_turn, dve_turn = a.sem("hi_done"), a.sem("pool_turn"), a.sem("dve_turn")
        xr_done, rtr_done, rev_done = a.sem("xr_done"), a.sem("rtr_done"), a.sem("rev_done")
        rows_out = [a.sem(f"rows_out{s}") for s in range(RING)]
        last = QUADS // RING - 1

        with nc.Block() as block:
            @block.sync
            def _(sp):
                for s in range(RING):
                    sp.sem_inc(rows_out[s], 32)
                sp.wait_ge(filled, 2)
                sp.dma_start(rows[TOKENS:TOKENS + P, :], zero[:]).then_inc(stored, 16)

                def load_weights(i, s):
                    q = quad(i, s)
                    sp.wait_ge(lo_done, freed(q))
                    sp.dma_start(stage[:, s].rearrange("p (k c) -> p k c", k=3),
                                 down[q].rearrange("(k p) c -> p k c", p=P)).then_inc(stage_in[s], 16)

                def store(i, s):
                    q = quad(i, s)
                    sp.wait_ge(xr_done, made(q))
                    sp.dma_start(row_tiles[:, bass.ts(q, QT), 0:C], xr[:, s]).then_inc(rows_out[s], 16)
                    sp.dma_start(row_tiles[:, bass.ts(q, QT), C:GC], xr[:, s, :, P:C]).then_inc(rows_out[s], 16)

                load_weights(0, 0)
                load_weights(0, 1)
                with sp.Fori(1, QUADS // RING) as i:
                    for s in range(RING):
                        load_weights(i, s)
                        store(i - 1, s)
                for s in range(RING):
                    store(last, s)
                sp.wait_ge(stored, 16)
                for s in range(RING):
                    sp.wait_ge(rows_out[s], 32 * (QUADS // RING + 1))

            @block.tensor
            def _(pe):
                pe.sem_inc(tr_done, RING)
                pe.sem_inc(rtr_done, RING)
                pe.sem_inc(qkv_done, RING)
                pe.wait_ge(bias_row, 1)

                def turn(i, s):
                    q = quad(i, s)
                    pe.wait_ge(xn_done, made(q))
                    pe.wait_ge(ev_done, q + RING)
                    transposes(nc, xn[:, s], eye, ps_a, ps_b).then_inc(tr_done, 1)

                def turn_route(i, s):
                    q = quad(i, s)
                    pe.wait_ge(xr_done, made(q))
                    pe.wait_ge(rev_done, q + RING)
                    transposes(nc, xr[:, s], eye, ps_ra, ps_rb).then_inc(rtr_done, 1)

                def products(i, s, project=True, route=True):
                    q = quad(i, s)
                    pe.wait_ge(cp_done, freed(q))
                    if project:
                        pe.wait_ge(ev_done, made(q))
                        for t in range(QT):
                            at = ps_q[:, s, t // 2, (t % 2) * QW:(t % 2 + 1) * QW]
                            nc.tensor.matmul(at, xa[:, s, bass.ts(t, P)], wqa[:], start=True, stop=False)
                            ins = nc.tensor.matmul(at, xb[:, s, bass.ts(t, P)], wqb[:], start=False, stop=True)
                    if route:
                        pe.wait_ge(rev_done, made(q - LAG))
                        for t in range(QT):
                            at = ps_q[:, s, 0, ps_lg.start + t * EXPERTS:ps_lg.start + (t + 1) * EXPERTS]
                            nc.tensor.matmul(at, ra[:, bass.ts(t, P)], ga[:], start=True, stop=False)
                            ins = nc.tensor.matmul(at, rb[:, bass.ts(t, P)], gb[:], start=False, stop=True)
                    ins.then_inc(qkv_done, 1)

                turn(0, 0)
                for n in range(LAG):
                    turn(*turned(0, n + 1))
                    products(*turned(0, n), route=False)
                with pe.Fori(LAG // RING, last) as i:
                    for r in range(1, 1 + RING):
                        turn(*turned(i, r + 1))
                        turn_route(*turned(i, r - LAG))
                        products(*turned(i, r))
                for n in range(QUADS - 1, QUADS + LAG):
                    turn_route(*turned(0, n - LAG))
                    products(*turned(0, n), project=n < QUADS)

            @block.scalar
            def _(act):
                act.sem_inc(ev_done, RING)
                act.sem_inc(rev_done, RING)
                act.sem_inc(cp_done, RING)
                act.sem_inc(ex_done, RING)
                act.sem_inc(hi_done, RING)

                def out_of_psum(i, s):
                    q = quad(i, s)
                    act.wait_ge(tr_done, made(q))
                    act.wait_ge(qkv_done, freed(q))
                    nc.scalar.activation(xa[:, s, :], ps_a[:], ACT.Copy)
                    nc.scalar.activation(xb[0:CB, s, :], ps_b[:], ACT.Copy).then_inc(ev_done, 1)

                def route_out_of_psum(i, s):
                    q = quad(i, s)
                    act.wait_ge(rtr_done, made(q))
                    nc.scalar.activation(ra[:], ps_ra[:], ACT.Copy)
                    nc.scalar.activation(rb[:], ps_rb[:], ACT.Copy).then_inc(rev_done, 1)

                def copy_products(i, s, project=True, route=True):
                    q = quad(i, s)
                    act.wait_ge(qkv_done, made(q))
                    if project:
                        act.wait_ge(prod_done, freed(q))
                        act.wait_ge(res_done, freed(q))
                        for h in range(2):
                            ins = nc.scalar.activation(qkv[:, s, 2 * h:2 * h + 2, :],
                                                       ps_q[:, s, h, 0:2 * QW].rearrange("p (t c) -> p t c", t=2), ACT.Copy)
                    if route:
                        ins = nc.scalar.activation(lg[:, bass.ts(q - LAG, QT), :],
                                                   ps_q[:, s, 0, ps_lg].rearrange("p (t e) -> p t e", t=QT), ACT.Copy)
                    ins.then_inc(cp_done, 1)

                def exponential(i, s):
                    q = quad(i, s)
                    act.wait_ge(diff_done, made(q))
                    nc.scalar.activation(ex[:, s], diff[:, s], ACT.Exp, scale=SCALE).then_inc(ex_done, 1)

                def split(i, s):
                    act.wait_ge(stage_in[s], 16 * i + 16)
                    nc.scalar.activation(wd[:, quad(i, s), :, 0, :], stage[:, s].rearrange("p (k c) -> p k c", k=3),
                                         ACT.Copy).then_inc(hi_done, 1)

                def attend(i, s):
                    split(i, s)
                    exponential(i, s)

                out_of_psum(0, 0)
                for n in range(LAG):
                    out_of_psum(*turned(0, n + 1))
                    copy_products(*turned(0, n), route=False)
                    attend(*turned(0, n))
                with act.Fori(LAG // RING, last) as i:
                    for r in range(1, 1 + RING):
                        out_of_psum(*turned(i, r + 1))
                        route_out_of_psum(*turned(i, r - LAG))
                        copy_products(*turned(i, r))
                        attend(*turned(i, r))
                for n in range(QUADS - 1, QUADS + LAG):
                    route_out_of_psum(*turned(0, n - LAG))
                    copy_products(*turned(0, n), project=n < QUADS)
                    if n < QUADS:
                        attend(*turned(0, n))

            @block.gpsimd
            def _(pool):
                for c in (lo_done, pow_done, eps_done, mean_done, kk_done, pv_done):
                    pool.sem_inc(c, RING)
                nc.gpsimd.memset(zero[:], 0.0).then_inc(filled, 1)
                nc.gpsimd.memset(half[:], -0.5).then_inc(filled, 1)
                pool.wait_ge(filled, 2)

                def rotate_key(i, s):
                    q = quad(i, s)
                    pool.wait_ge(cp_done, made(q))
                    pool.wait_ge(prod_done, freed(q))
                    pool.sem_inc(pool_turn, 1)
                    nc.gpsimd.tensor_tensor(ka[:], qkv[:, s, :, KC:KC + 24], cos_t[:], ALU.mult)
                    nc.gpsimd.tensor_tensor(kb[:], qkv[:, s, :, KC + 8:KC + 32], sin_t[:], ALU.mult).then_inc(rope_step, 1)
                    pool.wait_ge(rope_step, 3 * q + 1)
                    nc.gpsimd.tensor_tensor(kr[:], ka[:], kb[:], ALU.add).then_inc(rope_step, 1)
                    pool.wait_ge(rope_step, 3 * q + 2)
                    nc.gpsimd.tensor_tensor(kc[:], kr[:, :, 0:HD], cos_t[:, :, 0:HD], ALU.mult)
                    nc.gpsimd.tensor_tensor(kd[:], kr[:, :, 8:8 + HD], sin_t[:, :, 0:HD], ALU.mult).then_inc(rope_step, 1)
                    pool.wait_ge(rope_step, 3 * q + 3)
                    nc.gpsimd.tensor_tensor(kk[:, s], kc[:], kd[:], ALU.subtract).then_inc(kk_done, 1)

                def split(i, s):
                    q = quad(i, s)
                    pool.wait_ge(hi_done, made(q))
                    pool.sem_inc(pool_turn, 1)
                    nc.gpsimd.tensor_tensor(wd[:, q, :, 1, :], stage[:, s].rearrange("p (k c) -> p k c", k=3),
                                            wd[:, q, :, 0, :].bitcast(F32), ALU.subtract).then_inc(lo_done, 1)

                def weigh_value(i, s):
                    q = quad(i, s)
                    pool.wait_ge(wt_done, made(q))
                    pool.sem_inc(pool_turn, 1)
                    w = wt[:, s].rearrange("p (t h) -> p t h", t=QT)
                    for h in range(2):
                        t = slice(2 * h, 2 * h + 2)
                        ins = nc.gpsimd.tensor_tensor(qkv[:, s, t, 0:C].rearrange("p t (h d) -> p t h d", h=HEADS),
                                                      bcast(w[:, t, :], 3, HD),
                                                      bcast(qkv[:, s, t, VC:VC + HD], 2, HEADS), ALU.mult)
                    ins.then_inc(pv_done, 1)

                def deviation(i, s):
                    row_deviation(nc, pool, quad(i, s), s, mv, vtmp, half, mean, rstd, mv_done, eps_done,
                                  pow_done, mean_done, pool_turn)

                rotate_key(0, 0)
                split(0, 0)
                weigh_value(0, 0)
                rotate_key(0, 1)
                split(0, 1)
                deviation(0, 0)
                weigh_value(0, 1)
                with pool.Fori(1, QUADS // RING) as i:
                    for s in range(RING):
                        rotate_key(i, s)
                        split(i, s)
                        deviation(i - 1 + s, 1 - s)
                        weigh_value(i, s)
                deviation(last, 1)

            @block.vector
            def _(dve):
                nc.vector.memset(xb[CB:CB + 1, :, :], 1.0).then_inc(bias_row, 1)
                for c in (xn_done, xr_done, prod_done, score_done, diff_done, den_done, rec_done, wt_done, res_done,
                          stats_done, mv_done):
                    dve.sem_inc(c, RING)

                def norm(i, s):
                    q = quad(i, s)
                    dve.wait_ge(tr_done, freed(q))
                    normalise(nc, dve, q, xs, mean, rstd, xn[:, s]).then_inc(xn_done, 1)

                def norm_route(i, s):
                    q = quad(i, s)
                    dve.wait_ge(rows_out[s], 32 * i + 32)
                    dve.wait_ge(rtr_done, freed(q))
                    dve.wait_ge(pow_done, made(q))
                    normalise(nc, dve, q, xs, mean, rstd, xr[:, s]).then_inc(xr_done, 1)

                def scores(i, s):
                    q = quad(i, s)
                    dve.wait_ge(kk_done, made(q))
                    for h in range(2):
                        t = slice(2 * h, 2 * h + 2)
                        ins = nc.vector.tensor_tensor(
                            prod[:, t], qkv[:, s, t, 0:C].rearrange("p t (h d) -> p t h d", h=HEADS),
                            bcast(kk[:, s, t, :], 2, HEADS), ALU.mult)
                    ins.then_inc(prod_done, 1)
                    dve.wait_ge(prod_done, made(q))
                    nc.vector.tensor_reduce(score[:, s], prod[:].rearrange("p t h d -> p (t h) d"), AX.X,
                                            ALU.add).then_inc(score_done, 1)
                    dve.wait_ge(score_done, made(q))
                    nc.vector.tensor_tensor(diff[:, s], score[:, s], score[:, s], ALU.subtract).then_inc(diff_done, 1)

                def weights(i, s):
                    q = quad(i, s)
                    dve.wait_ge(ex_done, made(q))
                    nc.vector.tensor_scalar(den[:, s], ex[:, s], float(HEADS), None, ALU.mult).then_inc(den_done, 1)
                    dve.wait_ge(den_done, made(q))
                    nc.vector.reciprocal(rec[:, s], den[:, s]).then_inc(rec_done, 1)
                    dve.wait_ge(rec_done, made(q))
                    dve.wait_ge(pv_done, freed(q))
                    nc.vector.tensor_tensor(wt[:, s], den[:, s], rec[:, s], ALU.mult).then_inc(wt_done, 1)

                def residual(i, s):
                    q = quad(i, s)
                    dve.wait_ge(pv_done, made(q))
                    at = xs[:, bass.ts(q, QT), :]
                    nc.vector.tensor_tensor(at, at, qkv[:, s, :, 0:C], ALU.add).then_inc(res_done, 1)
                    row_statistics(nc, dve, q, s, xs, stats, mv, res_done, stats_done, mv_done, pow_done, mean_done, dve_turn)

                norm(0, 0)
                norm(0, 1)
                for n in range(RING):
                    norm(1, n)
                    scores(0, n)
                    if n:
                        residual(0, n - 1)
                    weights(0, n)
                with dve.Fori(1, last) as i:
                    for s in range(RING):
                        norm(i + 1, s)
                        norm_route(i - 1, s)
                        scores(i, s)
                        residual(i - 1 + s, 1 - s)
                        weights(i, s)
                for s in range(RING):
                    norm_route(last - 1, s)
                    scores(last, s)
                    residual(last - 1 + s, 1 - s)
                    weights(last, s)
                norm_route(last, 0)
                residual(last, 1)
                norm_route(last, 1)


def routing_phase(nc, lg, tri, iotas, row_tiles, idx_map, tile_exp):
    E, T = EXPERTS, TILES
    with ExitStack() as stack:
        a = Scope(nc, stack, "route")
        trit = a.sb("trit", [P, P])
        ones = a.sb("ones", [P, P])
        io = a.sb("io", [P, P])
        desc = a.sb("desc", [P, T, E])
        first = a.sb("first", [P, E, T])
        idp = a.sb("idp", [P, 2, T])
        no_row = a.sb("no_row", [P, 1])
        no_place = a.sb("no_place", [P, TILES_MAX])
        pr, tmp, m1, m2, tmp2 = (a.sb(n, [P, T, E]) for n in ("pr", "tmp", "m1", "m2", "tmp2"))
        both, gates = a.sb("both", [P, T, E]), a.sb("gates", [P, T, E])
        base = lg
        tot, inc = a.sb("tot", [P, E, T]), a.sb("inc", [P, E, T])
        red = a.sb("red", [P, 12, T])
        pos, keyb = a.sb("pos", [P, 2, T]), a.sb("keyb", [P, 2, 2, T])
        posi, keyi = a.sb("posi", [P, 2, T], I32), a.sb("keyi", [P, 2, 2, T], I32)
        ce, cum, start = a.sb("ce", [P, E]), a.sb("cum", [P, E]), a.sb("start", [P, E])
        cei = a.sb("cei", [P, E], I32)
        ge = a.sb("ge", [P, TILES_MAX, E])
        e_j = a.sb("e_j", [P, TILES_MAX])
        slot_v, slot_t, slot_0, size = (a.sb(n, [P, TILES_MAX]) for n in ("slot_v", "slot_t", "slot_0", "size"))
        hot_b = a.sb("hot_b", [P, HR, 2, HT, P], F32R)
        hot_j = a.sb("hot_j", [P, HR, 2, HT, TILES_MAX])
        hot_a = a.sb("hot_a", [P, HR, 2, HT, TILES_MAX], F32R)
        ps_p, ps_t, ps_m = (a.ps(n, [P, 512]) for n in ("ps_p", "ps_t", "ps_m"))

        desc_in = a.sem("desc_in")
        consts_in, gates_out, filled, pool_turn = (a.sem(n) for n in ("consts_in", "gates_out", "filled", "pool_turn"))
        diff_done, ex_done = a.sem("diff_done"), a.sem("ex_done")
        chain = a.sem("chain")
        chosen, counted, gates_done = a.sem("chosen"), a.sem("counted"), a.sem("gates_done")
        hot_done, hot_a_done, map_done = a.sem("hot_done"), a.sem("hot_a_done"), a.sem("map_done")
        consts = [(trit, tri)] + list(zip((io, first, idp, no_row, no_place), iotas[:1] + iotas[2:]))

        with nc.Block() as block:
            @block.sync
            def _(sp):
                sp.dma_start(desc[:], iotas[1]).then_inc(desc_in, 16)
                for dst, src in consts:
                    sp.dma_start(dst[:], src).then_inc(consts_in, 16)
                sp.wait_ge(gates_done, 1)
                sp.dma_start(row_tiles[:, :, GC:ROW], gates[:]).then_inc(gates_out, 16)
                sp.wait_ge(gates_out, 16)

            @block.gpsimd
            def _(pool):
                nc.gpsimd.memset(ones[:], 1.0).then_inc(filled, 1)
                pool.wait_ge(consts_in, 16 * len(consts))

                def token_at(i, s):
                    q = HR * i + s
                    pool.wait_ge(hot_done, q + 1)
                    pool.sem_inc(pool_turn, 1)
                    nc.gpsimd.tensor_tensor(hot_a[:, s], hot_j[:, s], bcast(idp[:, :, bass.ts(q, HT)], 3, TILES_MAX),
                                            ALU.mult).then_inc(hot_a_done, 1)

                with pool.Fori(0, TILES // HT // HR) as i:
                    for s in range(HR):
                        token_at(i, s)

            @block.scalar
            def _(act):
                act.wait_ge(diff_done, 1)
                nc.scalar.activation(pr[:], lg[:], ACT.Exp).then_inc(ex_done, 1)

            @block.tensor
            def _(pe):
                pe.sem_inc(map_done, HR)
                pe.wait_ge(consts_in, 16 * len(consts))

                pe.wait_ge(chosen, 1)
                pe.wait_ge(filled, 1)
                flat = both[:].rearrange("p t e -> p (t e)")
                nc.tensor.matmul(ps_p[:, 0:T * E], trit[:], flat, start=True, stop=True)
                nc.tensor.matmul(ps_t[:, 0:T * E], ones[:], flat, start=True, stop=True).then_inc(counted, 1)

                for q in range(TILES // HT):
                    s = q % HR
                    pe.wait_ge(hot_a_done, q + 1)
                    for k in range(2):
                        for t in range(HT):
                            ins = nc.tensor.matmul(ps_m[:, 0:TILES_MAX], hot_b[:, s, k, t, :], hot_a[:, s, k, t, :],
                                                   start=(q + k + t == 0), stop=(q + k + t == TILES // HT - 1 + HT))
                    ins.then_inc(map_done, 1)

            @block.vector
            def _(dve):
                count = [0]

                def then(ins):
                    ins.then_inc(chain, 1)
                    count[0] += 1
                    dve.wait_ge(chain, count[0])

                tt2, ts = nc.vector.tensor_tensor, nc.vector.tensor_scalar

                def reduce(dst, src, op):
                    then(nc.vector.tensor_reduce(dst, src, AX.X, op))

                def over(ap):
                    return bcast(ap, 2, E)

                mx, sm, rs, p1, f1, p2, f2, dn, rd, g1, g2 = (red[:, k, :] for k in range(11))
                reduce(mx, lg[:], ALU.max)
                tt2(lg[:], lg[:], over(mx), ALU.subtract).then_inc(diff_done, 1)
                dve.wait_ge(ex_done, 1)
                reduce(sm, pr[:], ALU.add)
                then(nc.vector.reciprocal(rs, sm))
                then(tt2(pr[:], pr[:], over(rs), ALU.mult))
                reduce(p1, pr[:], ALU.max)
                then(tt2(tmp[:], pr[:], over(p1), ALU.is_equal))
                dve.wait_ge(desc_in, 16)
                then(tt2(tmp2[:], tmp[:], desc[:], ALU.mult))
                reduce(f1, tmp2[:], ALU.max)
                then(tt2(m1[:], desc[:], over(f1), ALU.is_equal))
                then(nc.vector.scalar_tensor_tensor(out=tmp[:], in0=m1[:], scalar=-2.0, in1=pr[:],
                                                    op0=ALU.mult, op1=ALU.add))
                reduce(p2, tmp[:], ALU.max)
                then(tt2(tmp2[:], tmp[:], over(p2), ALU.is_equal))
                then(tt2(tmp[:], tmp2[:], desc[:], ALU.mult))
                reduce(f2, tmp[:], ALU.max)
                then(tt2(m2[:], desc[:], over(f2), ALU.is_equal))
                tt2(both[:], m1[:], m2[:], ALU.add).then_inc(chosen, 1)
                then(tt2(dn, p1, p2, ALU.add))
                then(ts(dn, dn, 1e-8, None, ALU.add))
                then(nc.vector.reciprocal(rd, dn))
                tt2(g1, p1, rd, ALU.mult)
                then(tt2(g2, p2, rd, ALU.mult))
                tt2(tmp[:], m1[:], over(g1), ALU.mult)
                then(tt2(tmp2[:], m2[:], over(g2), ALU.mult))
                tt2(gates[:], tmp[:], tmp2[:], ALU.add).then_inc(gates_done, 1)
                dve.wait_ge(counted, 1)
                dve.wait_ge(consts_in, 16 * len(consts))
                then(nc.vector.tensor_copy(tot[:], ps_t[:, 0:T * E].rearrange("p (t e) -> p e t", e=E)))
                flat = "p e t -> p (e t)"
                then(nc.vector.tensor_tensor_scan(inc[:].rearrange(flat), first[:].rearrange(flat),
                                                  tot[:].rearrange(flat), 0.0, ALU.mult, ALU.add))
                then(ts(ce[:], inc[:, :, T - 1], float(P - 1), None, ALU.add))
                tt2(tot[:], inc[:], tot[:], ALU.subtract)
                then(nc.vector.tensor_copy(cei[:], ce[:]))
                then(ts(cei[:], cei[:], 7, None, ALU.arith_shift_right))
                then(nc.vector.tensor_copy(ce[:], cei[:]))
                then(nc.vector.tensor_tensor_scan(cum[:], ones[:, 0:E], ce[:], 0.0, ALU.mult, ALU.add))
                then(tt2(start[:], cum[:], ce[:], ALU.subtract))
                stt = nc.vector.scalar_tensor_tensor
                then(stt(out=tot[:], in0=bcast(start[:], 2, T), scalar=float(P), in1=tot[:], op0=ALU.mult, op1=ALU.add))
                then(tt2(base[:], ps_p[:, 0:T * E].rearrange("p (t e) -> p t e", e=E),
                         tot[:].rearrange("p e t -> p t e"), ALU.add))
                tt2(tmp[:], m1[:], base[:], ALU.mult)
                then(tt2(tmp2[:], m2[:], base[:], ALU.mult))
                nc.vector.tensor_reduce(pos[:, 0, :], tmp[:], AX.X, ALU.add)
                reduce(pos[:, 1, :], tmp2[:], ALU.add)
                then(nc.vector.tensor_copy(posi[:], pos[:]))
                ts(keyi[:, 0], posi[:], 7, None, ALU.arith_shift_right)
                then(ts(keyi[:, 1], posi[:], P - 1, None, ALU.bitwise_and))
                then(nc.vector.tensor_copy(keyb[:], keyi[:]))

                def hot(i, s):
                    q = HR * i + s
                    dve.wait_ge(map_done, q + 1)
                    keys = keyb[:, :, :, bass.ts(q, HT)]
                    tt2(hot_b[:, s], bcast(bcast(io[:], 1, HT), 1, 2), bcast(keys[:, 1], 3, P), ALU.is_equal)
                    tt2(hot_j[:, s], bcast(bcast(io[:, 0:TILES_MAX], 1, HT), 1, 2), bcast(keys[:, 0], 3, TILES_MAX),
                        ALU.is_equal).then_inc(hot_done, 1)

                with dve.Fori(0, TILES // HT // HR) as i:
                    for s in range(HR):
                        hot(i, s)

                then(tt2(ge[:], bcast(io[:, 0:TILES_MAX], 2, E), bcast(cum[:], 1, TILES_MAX), ALU.is_ge))
                reduce(e_j[:], ge[:], ALU.add)
                ts(tile_exp[:], e_j[:], float(E - 1), None, ALU.min)
                dve.wait_ge(map_done, TILES // HT + HR)
                then(nc.vector.tensor_copy(slot_v[:], ps_m[:, 0:TILES_MAX]))
                ts(slot_t[:], slot_v[:], 0.0, no_row[:, 0:1], ALU.is_equal, ALU.mult)
                stt(out=slot_0[:], in0=slot_v[:], scalar=0.0, in1=no_place[:], op0=ALU.is_equal, op1=ALU.mult)
                then(stt(out=size[:], in0=slot_v[:], scalar=-1.0, in1=slot_v[:], op0=ALU.mult, op1=ALU.max))
                then(stt(out=idx_map[:, :, 0], in0=size[:], scalar=-1.0, in1=slot_t[:], op0=ALU.add, op1=ALU.add))
                stt(out=size[:], in0=size[:], scalar=-1.0, in1=slot_0[:], op0=ALU.add, op1=ALU.add)
                then(ts(slot_v[:], slot_v[:], 0.0, float(TOKENS), ALU.is_lt, ALU.mult))
                tt2(idx_map[:, :, 1], size[:], slot_v[:], ALU.add)


def expert_phase(nc, xs, eye, rows, chosen_rows, out, wa_hi, wa_lo, wb_hi, wb_lo, wd, idx_map, tile_exp):
    with ExitStack() as stack:
        a = Scope(nc, stack, "moe")
        xt = a.sb("xt", [P, XR, ROW])
        idx = a.sb("idx", [P, XR, 2], I32)
        x_hi = a.sb("x_hi", [P, RING, 2 * P], F32R)
        x_lo = a.sb("x_lo", [P, RING, P], F32R)
        sg, hid = a.sb("sg", [P, RING, HID]), a.sb("hid", [P, RING, HID])
        h_hi, h_lo = a.sb("h_hi", [P, RING, HID], F32R), a.sb("h_lo", [P, RING, HID], F32R)
        yy, y = a.sb("yy", [P, RING, 2, C]), a.sb("y", [P, YR, C])
        pick = wa_hi[:].bitcast(F32).rearrange("p e c -> p (e c)")[:, 0:PR * 2 * QT * C].rearrange(
            "p (s k t c) -> p s k t c", s=PR, k=2, t=QT)
        ps_x, ps_h = a.ps("ps_x", [P, 512]), a.ps("ps_h", [P, 512])
        ps_g, ps_u, ps_y = (a.ps(n, [P, RING, 512]) for n in ("ps_gt", "ps_u", "ps_y"))

        gathered = [a.sem(f"gathered{s}") for s in range(XR)]
        scattered = [a.sem(f"scattered{s}") for s in range(YR)]
        picked, out_stored = ([a.sem(f"{n}{s}") for s in range(PR)] for n in ("picked", "out_stored"))
        sum_done, total_done = a.sem("sum_done"), a.sem("total_done")
        idx_done, pool_turn = a.sem("idx_done"), a.sem("pool_turn")
        xt_done, gate_done, up_done, ht_done, y_mm = (a.sem(n) for n in ("xt_done", "gate_done", "up_done", "ht_done", "y_mm"))
        x_hi_done, x_lo_done, x_lob_done = a.sem("x_hi_done"), a.sem("x_lo_done"), a.sem("x_lob_done")
        silu_done, hid_done, weighed = a.sem("silu_done"), a.sem("hid_done"), a.sem("weighed")
        h_hi_done, h_lo_done, y_done = a.sem("h_hi_done"), a.sem("h_lo_done"), a.sem("y_done")
        N = TILES_MAX

        with nc.Block() as block:
            @block.gpsimd
            def _(pool):
                pool.sem_inc(idx_done, RING)

                def gather(i, r):
                    j, n, slot = XR * i + r, i + r // XR, r % XR
                    nc.gpsimd.tensor_copy(idx[:, slot, :], idx_map[:, bass.ds(j, 1), :]).then_inc(idx_done, 1)
                    pool.wait_ge(idx_done, made(j))
                    pool.sem_inc(pool_turn, 1)
                    nc.gpsimd.indirect_dma_start(
                        xt[:, slot, :], None, rows.ap(),
                        bass.IndirectOffsetOnAxis(ap=idx[:, slot, 0:1], axis=0)).then_inc(gathered[slot], 16)

                def scatter(i, r):
                    j, slot = XR * i + r, r % XR
                    pool.wait_ge(y_done, made(j))
                    pool.sem_inc(pool_turn, 1)
                    nc.gpsimd.indirect_dma_start(
                        chosen_rows.ap(), bass.IndirectOffsetOnAxis(ap=idx[:, slot, 1:2], axis=0),
                        y[:, slot % YR, :], None).then_inc(scattered[slot % YR], 16)

                def landed(i, r):
                    pool.wait_ge(scattered[r % YR], 16 * (XR // YR * i + r // YR) + 16)
                    pool.sem_inc(pool_turn, 1)

                for r in range(AHEAD):
                    gather(0, r)
                for r in range(XR):
                    scatter(0, r)
                    if r >= 2:
                        landed(0, r - 2)
                    gather(0, r + AHEAD)
                with pool.Fori(1, N // XR - 1) as i:
                    for r in range(XR):
                        scatter(i, r)
                        landed(i, r - 2)
                        gather(i, r + AHEAD)
                n = N // XR - 1
                for r in range(XR):
                    scatter(n, r)
                    landed(n, r - 2)
                    if r < 2:
                        gather(n, r + AHEAD)

            @block.tensor
            def _(pe):
                for c in (xt_done, gate_done, up_done, ht_done, y_mm):
                    pe.sem_inc(c, RING)

                def expert(i, r):
                    return pe.value_load(tile_exp[0:1, bass.ds(XR * i + r, 1)]) % EXPERTS

                def turn_x(i, r):
                    j, n, slot = XR * i + r, i + r // XR, r % XR
                    pe.wait_ge(gathered[slot], 16 * n + 16)
                    nc.tensor.transpose(ps_x[:, 0:P], xt[:, slot, 0:P], eye[:])
                    nc.tensor.transpose(ps_x[:, P:2 * P], xt[:, slot, P:GC], eye[:]).then_inc(xt_done, 1)

                def product(r, e, dst, col, done):
                    s = r % RING
                    at = dst[:, s, 0:HID]
                    w = bass.ds(col, HID)
                    hb = x_hi[:, s, P:2 * P]
                    nc.tensor.matmul(at, x_hi[:, s, 0:P], wa_hi[:, e, w], start=True, stop=False)
                    nc.tensor.matmul(at, x_hi[:, s, 0:P], wa_lo[:, e, w], start=False, stop=False)
                    nc.tensor.matmul(at, x_lo[:, s, :], wa_hi[:, e, w], start=False, stop=False)
                    nc.tensor.matmul(at, hb, wb_hi[:, e, w], start=False, stop=False)
                    nc.tensor.matmul(at, hb[0:CB, :], wb_lo[:, e, w], start=False, stop=True).then_inc(done, 1)

                def turn_h(i, r):
                    j, s = XR * i + r, r % RING
                    pe.wait_ge(hid_done, made(j))
                    pe.wait_ge(h_lo_done, j + RING)
                    for k in range(3):
                        ins = nc.tensor.transpose(ps_h[:, bass.ts(k, P)], hid[:, s, bass.ts(k, P)], eye[:])
                    ins.then_inc(ht_done, 1)

                def down_product(r, e):
                    s = r % RING
                    both, first = ps_y[:, s, 0:2 * C], ps_y[:, s, 0:C]
                    for k in range(3):
                        hi, lo = h_hi[:, s, bass.ts(k, P)], h_lo[:, s, bass.ts(k, P)]
                        halves = wd[:, bass.ds(e, 1), k].rearrange("p e h c -> p (e h c)")
                        high = wd[:, bass.ds(e, 1), k, 0].rearrange("p e c -> p (e c)")
                        if k == 2:
                            nc.tensor.matmul(first, lo, high, start=False, stop=False)
                        ins = nc.tensor.matmul(both, hi, halves, start=(k == 0), stop=(k == 2))
                        if k < 2:
                            nc.tensor.matmul(first, lo, high, start=False, stop=False)
                    ins.then_inc(y_mm, 1)

                def gate_product(i, r, e):
                    pe.wait_ge(x_lob_done, made(XR * i + r))
                    product(r, e, ps_g, 0, gate_done)

                def up_product(r, e):
                    product(r, e, ps_u, HID, up_done)

                def steps(i, first, last):
                    e = {first: expert(i, first)}
                    for r in range(first, last):
                        gate_product(i, r, e[r])
                        if r + 1 < XR or last > XR:
                            turn_x(i, r + 1)
                        turn_h(i, r - 1)
                        up_product(r, e[r])
                        if r - 2 < first:
                            e[r - 2] = expert(i, r - 2)
                        if r + 1 < last:
                            e[r + 1] = expert(i, r + 1)
                        down_product(r - 2, e[r - 2])
                    return e

                turn_x(0, 0)
                for r in range(2):
                    e = expert(0, r)
                    gate_product(0, r, e)
                    turn_x(0, r + 1)
                    if r:
                        turn_h(0, r - 1)
                    up_product(r, e)
                with pe.Fori(0, N // XR - 1) as i:
                    steps(i, 2, XR + 2)
                n = N // XR - 1
                e = steps(n, 2, XR)
                turn_h(n, XR - 1)
                down_product(XR - 2, e[XR - 2])
                pe.wait_ge(h_lo_done, made(N - 1))
                down_product(XR - 1, e[XR - 1])

            @block.scalar
            def _(act):
                for c in (x_hi_done, silu_done, h_hi_done, weighed):
                    act.sem_inc(c, RING)

                def x_high(i, r):
                    j, s = XR * i + r, r % RING
                    act.wait_ge(xt_done, made(j))
                    nc.scalar.activation(x_hi[:, s, :], ps_x[:, 0:2 * P], ACT.Copy).then_inc(x_hi_done, 1)

                def silu(i, r):
                    j, s = XR * i + r, r % RING
                    act.wait_ge(gate_done, made(j))
                    nc.scalar.activation(sg[:, s, :], ps_g[:, s, 0:HID], ACT.Silu).then_inc(silu_done, 1)

                def h_high(i, r):
                    j, s = XR * i + r, r % RING
                    act.wait_ge(ht_done, made(j))
                    nc.scalar.activation(h_hi[:, s, :], ps_h[:, 0:HID], ACT.Copy).then_inc(h_hi_done, 1)

                def weigh(i, r):
                    j, slot, s = XR * i + r, r % XR, r % RING
                    e = act.value_load(tile_exp[0:1, bass.ds(j, 1)]) % EXPERTS
                    act.wait_ge(y_mm, made(j))
                    nc.scalar.activation(yy[:, s].rearrange("p h c -> p (h c)"), ps_y[:, s, 0:2 * C], ACT.Copy,
                                         scale=xt[:, slot, bass.ds(GC + e, 1)]).then_inc(weighed, 1)

                x_high(0, 0)
                x_high(0, 1)
                silu(0, 0)
                x_high(0, 2)
                h_high(0, 0)
                silu(0, 1)
                for r in range(2, XR + 2):
                    x_high(0, r + 1)
                    h_high(0, r - 1)
                    silu(0, r)
                    weigh(0, r - 2)
                with act.Fori(1, N // XR - 1) as i:
                    for r in range(2, XR + 2):
                        x_high(i, r + 1)
                        h_high(i, r - 1)
                        silu(i, r)
                        weigh(i, r - 2)
                n = N // XR - 1
                for r in range(2, XR + 2):
                    if r + 1 < XR:
                        x_high(n, r + 1)
                    if r - 1 < XR:
                        h_high(n, r - 1)
                    if r < XR:
                        silu(n, r)
                    weigh(n, r - 2)

            @block.vector
            def _(dve):
                for c in (x_lo_done, x_lob_done, hid_done, h_lo_done, y_done):
                    dve.sem_inc(c, RING)

                def x_low(i, r):
                    j, s = XR * i + r, r % RING
                    dve.wait_ge(x_hi_done, made(j))
                    nc.vector.tensor_tensor(x_lo[:, s, :], ps_x[:, 0:P], x_hi[:, s, 0:P].bitcast(F32),
                                            ALU.subtract).then_inc(x_lo_done, 1)
                    b = x_hi[CB:P, s, P:2 * P]
                    nc.vector.tensor_tensor(b, ps_x[CB:P, P:2 * P], b.bitcast(F32), ALU.subtract).then_inc(x_lob_done, 1)

                def hidden(i, r):
                    j, s = XR * i + r, r % RING
                    dve.wait_ge(silu_done, made(j))
                    dve.wait_ge(up_done, made(j))
                    nc.vector.tensor_tensor(hid[:, s, :], ps_u[:, s, 0:HID], sg[:, s, :], ALU.mult).then_inc(hid_done, 1)

                def h_low(i, r):
                    j, s = XR * i + r, r % RING
                    dve.wait_ge(h_hi_done, made(j))
                    nc.vector.tensor_tensor(h_lo[:, s, :], ps_h[:, 0:HID], h_hi[:, s, :].bitcast(F32),
                                            ALU.subtract).then_inc(h_lo_done, 1)

                def add_parts(i, r, wait=True):
                    j, s = XR * i + r, r % RING
                    if wait:
                        dve.wait_ge(scattered[r % YR], 16 * (XR // YR * i + r // YR))
                    dve.wait_ge(weighed, made(j))
                    nc.vector.tensor_tensor(y[:, r % YR, :], yy[:, s, 0], yy[:, s, 1], ALU.add).then_inc(y_done, 1)

                x_low(0, 0)
                x_low(0, 1)
                hidden(0, 0)
                x_low(0, 2)
                h_low(0, 0)
                hidden(0, 1)
                for r in range(2, XR + 2):
                    x_low(0, r + 1)
                    h_low(0, r - 1)
                    hidden(0, r)
                    add_parts(0, r - 2, wait=r - 2 >= YR)
                with dve.Fori(1, N // XR - 1) as i:
                    for r in range(2, XR + 2):
                        x_low(i, r + 1)
                        h_low(i, r - 1)
                        hidden(i, r)
                        add_parts(i, r - 2)
                n = N // XR - 1
                for r in range(2, XR + 2):
                    if r + 1 < XR:
                        x_low(n, r + 1)
                    if r - 1 < XR:
                        h_low(n, r - 1)
                    if r < XR:
                        hidden(n, r)
                    add_parts(n, r - 2)

                with dve.Fori(0, QUADS // PR) as i:
                    for s in range(PR):
                        q = PR * i + s
                        dve.wait_ge(picked[s], 32 * i + 32)
                        nc.vector.tensor_tensor(pick[:, s, 0], pick[:, s, 0], pick[:, s, 1],
                                                ALU.add).then_inc(sum_done, 1)
                        dve.wait_ge(sum_done, q + 1)
                        at = xs[:, bass.ts(q, QT), :]
                        nc.vector.tensor_tensor(at, at, pick[:, s, 0], ALU.add).then_inc(total_done, 1)

            @block.sync
            def _(sp):
                out_tiles = out.rearrange("(t p) c -> p t c", p=P)
                picks = chosen_rows[0:2 * TOKENS, :].rearrange("(k t p) c -> k p t c", k=2, p=P)
                for r in range(YR):
                    sp.wait_ge(scattered[r], 16 * N // YR)

                def load(i, s):
                    q = PR * i + s
                    for k in range(2):
                        sp.dma_start(pick[:, s, k], picks[k, :, bass.ts(q, QT), :]).then_inc(picked[s], 16)

                def store(i, s):
                    q = PR * i + s
                    sp.wait_ge(total_done, q + 1)
                    sp.dma_start(out_tiles[:, bass.ts(q, QT), :], xs[:, bass.ts(q, QT), :]).then_inc(out_stored[s], 16)

                for s in range(PR):
                    load(0, s)
                with sp.Fori(1, QUADS // PR) as i:
                    for s in range(PR):
                        store(i - 1, s)
                        load(i, s)
                for s in range(PR):
                    store(QUADS // PR - 1, s)
                for s in range(PR):
                    sp.wait_ge(out_stored[s], 16 * QUADS // PR)


def kernel(**inputs):
    import numpy as np
    import concourse.bacc as bacc
    from concourse import mybir as mb
    from concourse.bass_utils import run_bass_kernel_spmd as run

    f = np.float32
    get = {k: np.asarray(v) for k, v in inputs.items()}
    x = get["x"].reshape(TOKENS, C)

    line = int((SIDE * SIDE * 0.25) ** 0.5 // 2)
    mask = np.zeros((SIDE, SIDE))
    mask[SIDE // 2 - line:SIDE // 2 + line, SIDE // 2 - line:SIDE // 2 + line] = 1.0
    unit = np.eye(SEQ).reshape(SEQ, SIDE, SIDE)
    spec = np.fft.fftshift(np.fft.fft2(unit, norm="forward"), axes=(-2, -1)) * mask
    low = np.fft.ifft2(np.fft.ifftshift(spec, axes=(-2, -1)), norm="forward").real.reshape(SEQ, SEQ)
    inv = (1.0 / 10000.0 ** (np.arange(0, HD, 2, dtype=f) / f(HD))).astype(f)
    ang = np.arange(SEQ, dtype=f)[:, None] * inv[None, :]
    cos, sin = np.cos(ang).astype(f), np.sin(ang).astype(f)
    rep = lambda v: np.ascontiguousarray(np.broadcast_to(v.astype(f).reshape(1, -1), (P, v.size)))
    p = np.arange(P)
    token = (p[:, None] + P * np.arange(TILES)[None, :] + 1).astype(f)
    iotas = [
        rep(np.arange(P)),
        rep(np.tile(EXPERTS - np.arange(EXPERTS), TILES)),
        rep(np.tile((np.arange(TILES) > 0), EXPERTS)),
        np.stack([token, -token], 1),
        (TOKENS + 1 + p[:, None]).astype(f),
        (2 * TOKENS + 1 + P * (np.arange(TILES_MAX) % PADS)[None, :] + p[:, None]).astype(f),
    ]
    ytab = np.zeros((P, 1), f)
    ytab[[DH, DP + DH]] = 1.0

    rows = lambda *v: np.ascontiguousarray(np.concatenate(v, 0))
    wk, bk = get["L1_attn_Wk"], get["L1_attn_bk"]
    wqkv = rows(np.concatenate([get["L1_attn_Wq"], wk, wk, get["L1_attn_Wv"]], 1),
                np.concatenate([get["L1_attn_bq"], bk, bk, get["L1_attn_bv"]])[None, :])
    arrays = {
        "x": np.ascontiguousarray(x),
        "xT": np.ascontiguousarray(x.T),
        "w1": rows(get["L0_conv_W1"].T, get["L0_conv_b1"][None, :]),
        "w2": rows(get["L0_conv_W2"].T, get["L0_conv_b2"][None, :]),
        "lowpass": low.astype(f),
        "wqkv": wqkv,
        "cos": np.concatenate([cos, cos, cos], 1),
        "sin": np.concatenate([-sin, sin, -sin], 1),
        "gate": np.ascontiguousarray(get["L1_ffn_gate_w"].T),
        "wgu": np.ascontiguousarray(np.concatenate([get["L1_ffn_gate_bank"], get["L1_ffn_up_bank"]], 2).transpose(1, 0, 2)),
        "down": np.ascontiguousarray(get["L1_ffn_down_bank"]),
        "tri": np.triu(np.ones((P, P), f), 1),
        "ident": np.eye(P, dtype=f),
        **{f"iota{k}": v for k, v in enumerate(iotas)},
        "ytab": ytab,
    }
    nc = bacc.Bacc("TRN2", target_bir_lowering=False, num_devices=1)
    ap = {k: nc.dram_tensor(f"in_{k}", v.shape, mb.dt.from_np(v.dtype), kind="ExternalInput").ap()
          for k, v in arrays.items()}
    out = nc.dram_tensor("out_0", (TOKENS, C), mb.dt.float32, kind="ExternalOutput").ap()
    tables = [ap.pop(f"iota{k}") for k in range(len(iotas))]
    program(nc, **ap, iotas=tables, out=out)
    r = run(nc, [{f"in_{k}": v for k, v in arrays.items()}], core_ids=[0])
    return r.results[0]["out_0"].reshape(get["x"].shape)
```
